# Optimizing a Trainium2 kernel written in Bass

```python
import numpy as np
import jax
import jax.numpy as jnp

def _softmax(x, axis=-1):
    return jax.nn.softmax(x, axis=axis)

def _gelu(x):
    return jax.nn.gelu(x, approximate=True)

def _silu(x):
    return jax.nn.silu(x)

def _sigmoid(x):
    return jax.nn.sigmoid(x)

def _layernorm(x, axis=-1, eps=1e-05):
    m = jnp.mean(x, axis=axis, keepdims=True)
    v = jnp.var(x, axis=axis, keepdims=True)
    return (x - m) / jnp.sqrt(v + eps)

def _scatter_add(tgt, idx, src, axis=0):
    return tgt.at[idx].add(src)

def _segment_sum(src, seg, n):
    return jax.ops.segment_sum(src, seg, n)
kernel_name = 'mk_gnn_ffn_d1_gnn_r8_74b0f0'

def setup_inputs(seed: int=0):
    np.random.seed(seed)
    _w = jnp.asarray

    def _rec_inputs():
        import jax
        import jax.numpy as jnp
        _gk = jax.random.key(seed)
        x = -8.776e-05 + 1 * jax.random.normal(jax.random.fold_in(_gk, 1), (1250, 512), jnp.float32)
        src = jax.random.randint(jax.random.fold_in(_gk, 2), (40000,), 0, 1250, jnp.int32)
        dst = jnp.minimum((1250 * jax.random.uniform(jax.random.fold_in(_gk, 3), (40000,)) ** 2.0).astype(jnp.int32), 9999)
        _o = jnp.argsort(dst, stable=True)
        src = src[_o]
        dst = dst[_o]
        edge_attr_4 = 0.00171547 + 0.999346 * jax.random.normal(jax.random.fold_in(_gk, 11), (40000, 4), jnp.float32)
        edge_attr_8 = 0.000126197 + 0.999763 * jax.random.normal(jax.random.fold_in(_gk, 12), (40000, 8), jnp.float32)
        return (x, src, dst, edge_attr_4, edge_attr_8)
    x, src, dst, edge_attr_4, edge_attr_8 = _rec_inputs()

    def _L0_gnn_setup():
        import jax, jax.numpy as jnp
        import numpy as np
        MUL = 128
        N_NODES = 1250
        N_EDGES = 20000
        R_BASIS = 8
        HIDDEN = 64
        W_NUMEL = 4 * MUL
        SQRT3 = 3.0 ** 0.5
        SILU_2MOM = 1.679177
        AVG_NUM_NEIGHBORS = 10.0

        def _lin_irreps(x0, x1, W0, W1):
            y0 = x0 @ W0 / jnp.sqrt(jnp.float32(W0.shape[0]))
            y1 = jnp.einsum('num,uv->nvm', x1, W1) / jnp.sqrt(jnp.float32(W1.shape[0]))
            return (y0, y1)

        def _forward(node_feats, edge_attrs, edge_feats, edge_index, W_up0, W_up1, W_mlp1, W_mlp2, W_mlp3, W_mlp4, W_out0, W_out1):
            num_nodes = node_feats.shape[0]
            sender, receiver = (edge_index[0], edge_index[1])
            x0 = node_feats[:, :MUL]
            x1 = node_feats[:, MUL:].reshape(num_nodes, MUL, 3)
            x0, x1 = _lin_irreps(x0, x1, W_up0, W_up1)
            h = edge_feats
            for W in (W_mlp1, W_mlp2, W_mlp3):
                h = SILU_2MOM * jax.nn.silu(h @ W / jnp.sqrt(jnp.float32(W.shape[0])))
            tpw = h @ W_mlp4 / jnp.sqrt(jnp.float32(W_mlp4.shape[0]))
            w1, w2, w3, w4 = jnp.split(tpw, 4, axis=-1)
            s0 = x0[sender]
            s1 = x1[sender]
            y0 = edge_attrs[:, 0:1]
            y1 = edge_attrs[:, 1:4]
            p1 = w1 * s0 * y0
            p2 = (w2 * s0)[:, :, None] * y1[:, None, :]
            p3 = w3[:, :, None] * s1 * y0[:, None, :]
            p4 = w4 * jnp.einsum('eum,em->eu', s1, y1) / SQRT3
            m0 = jnp.concatenate([p1, p4], axis=-1)
            m1 = jnp.concatenate([p2, p3], axis=1)
            msg0 = jax.ops.segment_sum(m0, receiver, num_segments=num_nodes)
            msg1 = jax.ops.segment_sum(m1, receiver, num_segments=num_nodes)
            o0, o1 = _lin_irreps(msg0, msg1, W_out0, W_out1)
            out = jnp.concatenate([o0, o1.reshape(num_nodes, 3 * MUL)], axis=-1)
            return out / AVG_NUM_NEIGHBORS
        key = jax.random.key(seed)
        ks = jax.random.split(key, 12)
        rn = lambda k, s: jax.random.normal(k, s, dtype=jnp.float32)
        return {'node_feats': rn(ks[0], (N_NODES, 4 * MUL)), 'edge_attrs': rn(ks[1], (N_EDGES, 4)), 'edge_feats': rn(ks[2], (N_EDGES, R_BASIS)), 'edge_index': jax.random.randint(ks[3], (2, N_EDGES), 0, N_NODES), 'W_up0': rn(ks[4], (MUL, MUL)), 'W_up1': rn(ks[5], (MUL, MUL)), 'W_mlp1': rn(ks[6], (R_BASIS, HIDDEN)), 'W_mlp2': rn(ks[7], (HIDDEN, HIDDEN)), 'W_mlp3': rn(ks[8], (HIDDEN, HIDDEN)), 'W_mlp4': rn(ks[9], (HIDDEN, W_NUMEL)), 'W_out0': rn(ks[10], (2 * MUL, MUL)), 'W_out1': rn(ks[11], (2 * MUL, MUL))}
    _L0_gnn_all = _L0_gnn_setup()
    _L0_gnn_in = {k: v for k, v in _L0_gnn_all.items() if k in ('W_up0', 'W_up1', 'W_mlp1', 'W_mlp2', 'W_mlp3', 'W_mlp4', 'W_out0', 'W_out1')}
    del _L0_gnn_all

    def _L0_ffn_setup():
        import jax, jax.numpy as jnp
        import numpy as np
        B, S, D, H, O, E, TOPK = (4, 256, 512, 1024, 512, 8, 2)
        key = jax.random.key(seed)
        ks = jax.random.split(key, 6)
        s = lambda d: 1.0 / np.sqrt(d)
        return {'x': jax.random.normal(ks[0], (B, S, D), dtype=jnp.float32), 'Wg': jax.random.normal(ks[1], (D, E), dtype=jnp.float32) * s(D), 'W1': jax.random.normal(ks[2], (E, D, H), dtype=jnp.float32) * s(D), 'b1': jnp.zeros((E, H), dtype=jnp.float32), 'W2': jax.random.normal(ks[3], (E, H, O), dtype=jnp.float32) * s(H), 'b2': jnp.zeros((E, O), dtype=jnp.float32)}
    _L0_ffn_all = _L0_ffn_setup()
    _L0_ffn_in = {k: v for k, v in _L0_ffn_all.items() if k in ('Wg', 'W1', 'b1', 'W2', 'b2')}
    del _L0_ffn_all
    return {'x': x, 'src': src, 'dst': dst, 'edge_attr_4': edge_attr_4, 'edge_attr_8': edge_attr_8, 'L0_gnn_W_up0': _L0_gnn_in['W_up0'], 'L0_gnn_W_up1': _L0_gnn_in['W_up1'], 'L0_gnn_W_mlp1': _L0_gnn_in['W_mlp1'], 'L0_gnn_W_mlp2': _L0_gnn_in['W_mlp2'], 'L0_gnn_W_mlp3': _L0_gnn_in['W_mlp3'], 'L0_gnn_W_mlp4': _L0_gnn_in['W_mlp4'], 'L0_gnn_W_out0': _L0_gnn_in['W_out0'], 'L0_gnn_W_out1': _L0_gnn_in['W_out1'], 'L0_ffn_Wg': _L0_ffn_in['Wg'], 'L0_ffn_W1': _L0_ffn_in['W1'], 'L0_ffn_b1': _L0_ffn_in['b1'], 'L0_ffn_W2': _L0_ffn_in['W2'], 'L0_ffn_b2': _L0_ffn_in['b2']}

def reference(x, src, dst, edge_attr_4, edge_attr_8, L0_gnn_W_up0, L0_gnn_W_up1, L0_gnn_W_mlp1, L0_gnn_W_mlp2, L0_gnn_W_mlp3, L0_gnn_W_mlp4, L0_gnn_W_out0, L0_gnn_W_out1, L0_ffn_Wg, L0_ffn_W1, L0_ffn_b1, L0_ffn_W2, L0_ffn_b2):
    import jax
    import jax.numpy as jnp

    def _L0_gnn_ref(node_feats, edge_attrs, edge_feats, edge_index, W_up0, W_up1, W_mlp1, W_mlp2, W_mlp3, W_mlp4, W_out0, W_out1):
        import jax, jax.numpy as jnp
        import numpy as np
        MUL = 128
        N_NODES = 1250
        N_EDGES = 20000
        R_BASIS = 8
        HIDDEN = 64
        W_NUMEL = 4 * MUL
        SQRT3 = 3.0 ** 0.5
        SILU_2MOM = 1.679177
        AVG_NUM_NEIGHBORS = 10.0

        def _lin_irreps(x0, x1, W0, W1):
            y0 = x0 @ W0 / jnp.sqrt(jnp.float32(W0.shape[0]))
            y1 = jnp.einsum('num,uv->nvm', x1, W1) / jnp.sqrt(jnp.float32(W1.shape[0]))
            return (y0, y1)

        def _forward(node_feats, edge_attrs, edge_feats, edge_index, W_up0, W_up1, W_mlp1, W_mlp2, W_mlp3, W_mlp4, W_out0, W_out1):
            num_nodes = node_feats.shape[0]
            sender, receiver = (edge_index[0], edge_index[1])
            x0 = node_feats[:, :MUL]
            x1 = node_feats[:, MUL:].reshape(num_nodes, MUL, 3)
            x0, x1 = _lin_irreps(x0, x1, W_up0, W_up1)
            h = edge_feats
            for W in (W_mlp1, W_mlp2, W_mlp3):
                h = SILU_2MOM * jax.nn.silu(h @ W / jnp.sqrt(jnp.float32(W.shape[0])))
            tpw = h @ W_mlp4 / jnp.sqrt(jnp.float32(W_mlp4.shape[0]))
            w1, w2, w3, w4 = jnp.split(tpw, 4, axis=-1)
            s0 = x0[sender]
            s1 = x1[sender]
            y0 = edge_attrs[:, 0:1]
            y1 = edge_attrs[:, 1:4]
            p1 = w1 * s0 * y0
            p2 = (w2 * s0)[:, :, None] * y1[:, None, :]
            p3 = w3[:, :, None] * s1 * y0[:, None, :]
            p4 = w4 * jnp.einsum('eum,em->eu', s1, y1) / SQRT3
            m0 = jnp.concatenate([p1, p4], axis=-1)
            m1 = jnp.concatenate([p2, p3], axis=1)
            msg0 = jax.ops.segment_sum(m0, receiver, num_segments=num_nodes)
            msg1 = jax.ops.segment_sum(m1, receiver, num_segments=num_nodes)
            o0, o1 = _lin_irreps(msg0, msg1, W_out0, W_out1)
            out = jnp.concatenate([o0, o1.reshape(num_nodes, 3 * MUL)], axis=-1)
            return out / AVG_NUM_NEIGHBORS
        return _forward(node_feats, edge_attrs, edge_feats, edge_index, W_up0, W_up1, W_mlp1, W_mlp2, W_mlp3, W_mlp4, W_out0, W_out1)

    def _L0_ffn_ref(x, Wg, W1, b1, W2, b2):
        import jax, jax.numpy as jnp
        import numpy as np
        B, S, D, H, O, E, TOPK = (4, 256, 512, 1024, 512, 8, 2)
        Bsz, Seq, Din = x.shape
        T = Bsz * Seq
        xm = x.reshape(T, Din)
        probs = jax.nn.softmax(xm @ Wg, axis=-1)
        top_p, top_i = jax.lax.top_k(probs, TOPK)
        gates = jnp.zeros((T, E), dtype=probs.dtype).at[jnp.arange(T)[:, None], top_i].set(top_p)
        h = jax.nn.gelu(jnp.einsum('td,edh->teh', xm, W1) + b1[None])
        y = jnp.einsum('teh,eho->teo', h, W2) + b2[None]
        out = jnp.einsum('te,teo->to', gates, y)
        return out.reshape(Bsz, Seq, O)
    edge_index = jnp.stack([src, dst])
    x = x + _L0_gnn_ref(_layernorm(x, axis=-1), edge_attr_4, edge_attr_8, edge_index, L0_gnn_W_up0, L0_gnn_W_up1, L0_gnn_W_mlp1, L0_gnn_W_mlp2, L0_gnn_W_mlp3, L0_gnn_W_mlp4, L0_gnn_W_out0, L0_gnn_W_out1)
    x = x + _L0_ffn_ref(_layernorm(x, axis=-1)[None], L0_ffn_Wg, L0_ffn_W1, L0_ffn_b1, L0_ffn_W2, L0_ffn_b2)[0]
    return x

_drawn_inputs = setup_inputs


def setup_inputs(seed=0):
    import zlib

    import numpy as np

    out = dict(_drawn_inputs(seed))
    spreads = {'L0_ffn_b1': (0.0, 0.338), 'L0_ffn_b2': (0.0, 0.1)}
    factors = {}
    for name, (base, spread) in spreads.items():
        noise = np.random.default_rng([zlib.crc32(name.encode()), seed]).standard_normal(out[name].shape)
        drawn = base * np.exp(spread * noise) if base else spread * noise
        out[name] = jnp.asarray(drawn.astype(out[name].dtype))
    for name, factor in factors.items():
        out[name] = (out[name] * factor).astype(out[name].dtype)
    return out
```

```python
import concourse.bass as bass
from concourse import mybir
from contextlib import ExitStack

NODES, DIM, EDGES = 1250, 512, 40000
MUL, BASIS, HIDDEN = 128, 8, 64
EXPERTS, FFN = 8, 1024
P = 128
NODE_TILES = -(-NODES // P)
LAST_ROWS = NODES - (NODE_TILES - 1) * P

WINDOW = 32
BLOCK_TILES = 3
ITER_TILES = 2 * BLOCK_TILES
ITERS = -(-EDGES // (ITER_TILES * P))
TILES = ITERS * ITER_TILES
BLOCKS = TILES // BLOCK_TILES
HALF = BLOCK_TILES * P
PASSES = -(-NODES // WINDOW)
ACC_ROWS = NODES + WINDOW + 2
ACC_COLS = 3 * MUL

SLOT_BLOCKS = 2 * NODES // P + EXPERTS
SLOTS = SLOT_BLOCKS * P
SLOT_ROWS = SLOTS + 2 * P
KC, HC = DIM // P, FFN // P
CLEAR_MAX = 2568

EPS = 1e-5
SILU_2MOM = 1.679177
SQRT3 = 3.0 ** 0.5
NEIGHBORS = 10.0


def program(nc, x, src, dst, edge_y, edge_f, w_up0, w_up1, w_mlp1, w_mlp2, w_mlp3, w_mlp4,
            w_out0, w_out1, w_g, w_1, b_1, w_2, b_2, out):
    fp32, f32r, i32 = mybir.dt.float32, mybir.dt.float32r, mybir.dt.int32
    u32 = mybir.dt.uint32
    ACT, ALU, AX = mybir.ActivationFunctionType, mybir.AluOpType, mybir.AxisListType

    table = nc.dram_tensor("sender_table", (NODES, DIM), fp32).ap()
    acc = nc.dram_tensor("window_sums", (4 * ACC_ROWS, ACC_COLS), fp32).ap()
    slot_x = nc.dram_tensor("slot_inputs", (SLOT_ROWS, DIM), fp32).ap()
    slot_y = nc.dram_tensor("slot_outputs", (SLOTS, DIM), fp32).ap()

    ctx = ExitStack()
    with ctx:
        def sb(stack, name, shape, dt=fp32):
            return stack.enter_context(nc.sbuf_tensor(name, shape, dt))

        def ps(stack, name, shape):
            return stack.enter_context(nc.psum_tensor(name, shape, fp32))

        def sems(stack, *names):
            return [stack.enter_context(nc.semaphore(n)) for n in names]

        class Chain:

            def __init__(self, eng, sem):
                self.eng, self.sem, self.base, self.n = eng, sem, 0, 0

            def link(self, ins):
                self.n += 1
                ins.then_inc(self.sem, 1)
                self.eng.wait_ge(self.sem, self.base + self.n)

        def rows(t):
            return LAST_ROWS if t == NODE_TILES - 1 else P

        ident = sb(ctx, "ident", [P, P])
        ones = sb(ctx, "ones", [P, P])
        X = sb(ctx, "X", [P, NODE_TILES, DIM])
        wout0 = sb(ctx, "wout0", [P, 2, MUL])
        wout1 = sb(ctx, "wout1", [P, 2, MUL])
        wg = sb(ctx, "wg", [P, KC, EXPERTS])
        b2 = sb(ctx, "b2", [EXPERTS, DIM])
        eps = sb(ctx, "eps", [P, 1])

        edge_stack = ExitStack()
        with edge_stack:
            E = edge_stack
            src_sb = sb(E, "src_sb", [P, TILES + ITER_TILES], i32)
            dst_i = sb(E, "dst_i", [P, TILES], i32)
            dst_f = sb(E, "dst_f", [P, TILES])
            y_sb = sb(E, "y_sb", [P, TILES, 4])
            wm1 = sb(E, "wm1", [2 * BASIS, 2 * HIDDEN])
            wm2 = sb(E, "wm2", [2 * HIDDEN, 2 * HIDDEN])
            wm3 = sb(E, "wm3", [2 * HIDDEN, 2 * HIDDEN])
            wm4_hi = sb(E, "wm4_hi", [2 * HIDDEN, 4 * MUL], f32r)
            wm4_lo = sb(E, "wm4_lo", [2 * HIDDEN, 4 * MUL], f32r)
            window_iota = sb(E, "window_iota", [P, WINDOW])
            window_step = sb(E, "window_step", [P, 1])
            sum_row = sb(E, "sum_row", [P, BLOCKS])
            npass_i = sb(E, "npass_i", [P, 1], i32)

            with ExitStack() as s:
                wm4 = sb(s, "wm4", [2 * HIDDEN, 4 * MUL])
                wup0 = sb(s, "wup0", [P, MUL])
                wup1 = sb(s, "wup1", [P, MUL])
                stats = sb(s, "stats", [P, NODE_TILES, 6])
                mv = sb(s, "mv", [P, NODE_TILES, 2])
                rstd = sb(s, "rstd", [P, NODE_TILES])
                xn = sb(s, "xn", [P, 2, DIM])
                xT = sb(s, "xT", [P, 2, 4, P])
                up = sb(s, "up", [P, 2, 4, MUL])
                first = sb(s, "first", [P, BLOCKS])
                rel = sb(s, "rel", [P, TILES])
                hilo = sb(s, "hilo", [P, 4])
                row0 = sb(s, "row0", [P, 1], i32)
                row0f = sb(s, "row0f", [P, 1])
                iota_i = sb(s, "iota_i", [P, WINDOW], i32)
                pT = [ps(s, f"pT{k}", [P, 4, P]) for k in range(2)]
                pU = [ps(s, f"pU{k}", [P, 4, MUL]) for k in range(2)]
                pF = ps(s, "pF", [P, BLOCKS])
                pC = ps(s, "pC", [P, 1])
                (x_cleared, x_loaded, up_loaded, wout_loaded, small_loaded, dst_loaded, y_loaded,
                 blocks_cleared, mlp_loaded, ident_step, ident_made, ones_made,
                 iota_made, stats_done, sqrt_done, chain1, xn_made, transposed, xT_made, up_done,
                 up_copied, first_ready, ok_made, ok_summed, row0_made, table_saved0,
                 table_saved1, scaled) = sems(
                    s, "x_cleared", "x_loaded", "up_loaded", "wout_loaded", "small_loaded",
                    "dst_loaded", "y_loaded", "blocks_cleared", "mlp_loaded",
                    "ident_step", "ident_made", "ones_made", "iota_made", "stats_done",
                    "sqrt_done", "chain1", "xn_made", "transposed", "xT_made", "up_done",
                    "up_copied", "first_ready", "ok_made", "ok_summed", "row0_made",
                    "table_saved0", "table_saved1", "scaled")
                table_saved = [table_saved0, table_saved1]
                block = s.enter_context(nc.Block())

                @block.sync
                def _(sp):
                    sp.dma_start(X[:, 0:NODE_TILES - 1, :],
                                 x[0:(NODE_TILES - 1) * P, :].rearrange("(t p) d -> p t d", p=P)
                                 ).then_inc(x_loaded, 16)
                    sp.wait_ge(x_cleared, 1)
                    sp.dma_start(X[0:LAST_ROWS, NODE_TILES - 1, :], x[(NODE_TILES - 1) * P:NODES, :]
                                 ).then_inc(x_loaded, 16)
                    sp.dma_start(wup0[:], w_up0).then_inc(up_loaded, 16)
                    sp.dma_start(wup1[:], w_up1).then_inc(up_loaded, 16)
                    sp.dma_start(wout0[:], w_out0.rearrange("(k p) v -> p k v", p=P)
                                 ).then_inc(wout_loaded, 16)
                    sp.dma_start(wout1[:], w_out1.rearrange("(k p) v -> p k v", p=P)
                                 ).then_inc(small_loaded, 16)
                    sp.dma_start(wg[:], w_g.rearrange("(k p) e -> p k e", p=P)
                                 ).then_inc(small_loaded, 16)
                    sp.dma_start(b2[:], b_2).then_inc(small_loaded, 16)
                    sp.dma_start(src_sb[:], src).then_inc(small_loaded, 16)
                    sp.wait_ge(blocks_cleared, 2)
                    for h in range(2):
                        r, c = h * BASIS, h * HIDDEN
                        sp.dma_start(wm1[r:r + BASIS, c:c + HIDDEN], w_mlp1).then_inc(mlp_loaded, 16)
                        sp.dma_start(wm2[c:c + HIDDEN, c:c + HIDDEN], w_mlp2).then_inc(mlp_loaded, 16)
                        for d in range(2):
                            sp.dma_start(wm3[c:c + HIDDEN, d * HIDDEN:(d + 1) * HIDDEN], w_mlp3
                                         ).then_inc(mlp_loaded, 16)
                        sp.dma_start(wm4[c:c + HIDDEN, :], w_mlp4).then_inc(mlp_loaded, 16)
                    for t in range(NODE_TILES):
                        sp.wait_ge(up_copied, t + 1)
                        sp.dma_start(table[t * P:t * P + rows(t), :],
                                     up[0:rows(t), t % 2].rearrange("p c v -> p (c v)")
                                     ).then_inc(table_saved[t % 2], 16)
                    sp.wait_ge(small_loaded, 64)
                    sp.wait_ge(mlp_loaded, 160)
                    for k in range(2):
                        sp.wait_ge(table_saved[k], 16 * (NODE_TILES // 2))

                @block.scalar
                def _(act):
                    act.dma_start(dst_i[:], dst).then_inc(dst_loaded, 16)
                    act.dma_start(y_sb[:].rearrange("p t m -> p (t m)"), edge_y).then_inc(y_loaded, 16)
                    act.wait_ge(stats_done, 1)
                    act.activation(rstd[:], mv[:, :, 1], ACT.Sqrt, bias=eps[:, 0:1]).then_inc(sqrt_done, 1)
                    for t in range(NODE_TILES):
                        act.wait_ge(transposed, t + 1)
                        if t >= 2:
                            act.wait_ge(up_done, t - 1)
                        act.activation(xT[:, t % 2], pT[t % 2][:], ACT.Copy).then_inc(xT_made, 1)
                        act.wait_ge(up_done, t + 1)
                        if t >= 2:
                            act.wait_ge(table_saved[t % 2], 16 * (t // 2))
                        act.activation(up[:, t % 2], pU[t % 2][:], ACT.Copy,
                                       scale=SILU_2MOM / HIDDEN ** 0.5 / MUL ** 0.5
                                       ).then_inc(up_copied, 1)
                    act.wait_ge(y_loaded, 16)

                @block.gpsimd
                def _(pool):
                    pool.memset(ident[:], 0.0).then_inc(ident_step, 1)
                    pool.memset(wm1[:], 0.0).then_inc(blocks_cleared, 1)
                    pool.memset(wm2[:], 0.0).then_inc(blocks_cleared, 1)
                    pool.wait_ge(ident_step, 1)
                    pool.affine_select(out=ident[:], in_=ident[:], compare_op=ALU.not_equal, fill=1.0,
                                       base=0, pattern=[[-1, P]], channel_multiplier=1
                                       ).then_inc(ident_made, 1)
                    pool.iota(iota_i[:], pattern=[[1, WINDOW]], base=0, channel_multiplier=0
                              ).then_inc(iota_made, 1)
                    for g in range(4):
                        pool.wait_ge(iota_made, g + 1)
                        pool.iota(row0[32 * g:32 * g + 32, :], pattern=[[1, 1]], base=g * ACC_ROWS,
                                  channel_multiplier=1).then_inc(iota_made, 1)

                @block.vector
                def _(dve):
                    chain = Chain(dve, chain1)
                    dve.memset(X[:, NODE_TILES - 1, :], 0.0).then_inc(x_cleared, 1)
                    dve.memset(ones[:], 1.0).then_inc(ones_made, 1)
                    chain.link(dve.memset(eps[:], EPS))
                    dve.wait_ge(x_loaded, 32)
                    for t in range(NODE_TILES):
                        dve.bn_stats(stats[:, t, :], X[:, t, :]).then_inc(chain1, 1)
                        chain.n += 1
                    for t in range(NODE_TILES):
                        dve.wait_ge(chain1, 2 + t)
                        ins = dve.bn_aggr(mv[:, t, :], stats[:, t, :])
                    ins.then_inc(stats_done, 1)
                    dve.wait_ge(sqrt_done, 1)
                    chain.link(dve.reciprocal(rstd[:], rstd[:]))
                    for t in range(NODE_TILES):
                        if t >= 2:
                            dve.wait_ge(transposed, t - 1)
                        dve.tensor_scalar(xn[:, t % 2, :], X[:, t, :], mv[:, t, 0:1], rstd[:, t:t + 1],
                                          ALU.subtract, ALU.mult).then_inc(xn_made, 1)
                    dve.wait_ge(wout_loaded, 32 - 16)
                    dve.tensor_scalar(wout0[:, 1, :], wout0[:, 1, :], 1.0 / SQRT3, None, ALU.mult
                                      ).then_inc(scaled, 1)
                    dve.wait_ge(dst_loaded, 16)
                    dve.tensor_copy(dst_f[:], dst_i[:]).then_inc(row0_made, 1)
                    dve.wait_ge(first_ready, 1)
                    chain.link(dve.tensor_copy(first[:], pF[:]))
                    blocks3 = lambda a: a.rearrange("p (b k) -> p b k", k=BLOCK_TILES)
                    wide = first[:, :, None].broadcast_to((P, BLOCKS, BLOCK_TILES))
                    chain.link(dve.tensor_tensor(blocks3(rel[:]), blocks3(dst_f[:]), wide, ALU.subtract))
                    chain.link(dve.tensor_reduce(hilo[:, 0:1], rel[:], AX.X, ALU.max))
                    chain.link(dve.tensor_reduce(hilo[:, 1:2], rel[:], AX.X, ALU.min))
                    chain.link(dve.tensor_scalar(hilo[:, 0:1], hilo[:, 0:1], float(WINDOW - 1), None,
                                                 ALU.is_le))
                    chain.link(dve.tensor_scalar(hilo[:, 1:2], hilo[:, 1:2], 0.0, None, ALU.is_ge))
                    dve.tensor_tensor(hilo[:, 2:3], hilo[:, 0:1], hilo[:, 1:2], ALU.mult
                                      ).then_inc(ok_made, 1)
                    dve.wait_ge(ok_summed, 1)
                    chain.link(dve.tensor_scalar(hilo[:, 3:4], pC[:], float(P), None, ALU.is_equal))
                    fits = hilo[:, 3:4]
                    chain.link(dve.tensor_scalar(first[:], first[:], fits, None, ALU.mult))
                    chain.link(dve.tensor_tensor(blocks3(dst_f[:]), blocks3(dst_f[:]), wide, ALU.subtract))
                    dve.wait_ge(iota_made, 5)
                    chain.link(dve.tensor_copy(row0f[:], row0[:]))
                    chain.link(dve.tensor_scalar(sum_row[:], first[:], row0f[:, 0:1], None, ALU.add))
                    chain.link(dve.tensor_scalar(window_step[:], fits, -float(WINDOW), float(WINDOW),
                                                 ALU.mult, ALU.add))
                    chain.link(dve.tensor_scalar(npass_i[:], fits, 1.0 - PASSES, float(PASSES),
                                                 ALU.mult, ALU.add))
                    chain.link(dve.tensor_copy(window_iota[:], iota_i[:]))
                    dve.wait_ge(mlp_loaded, 160)
                    chain.link(dve.tensor_copy(wm4_hi[:], wm4[:]))
                    chain.link(dve.tensor_tensor(wm4_lo[:], wm4[:], wm4_hi[:].bitcast(fp32), ALU.subtract))

                @block.tensor
                def _(pe):
                    pe.wait_ge(ones_made, 1)
                    pe.wait_ge(ident_made, 1)
                    pe.wait_ge(up_loaded, 32)

                    def transpose(t):
                        pe.wait_ge(xn_made, t + 1)
                        if t >= 2:
                            pe.wait_ge(xT_made, t - 1)
                        v = xn[:, t % 2, MUL:].rearrange("p (u m) -> p m u", m=3)
                        pe.transpose(pT[t % 2][:, 0], xn[:, t % 2, 0:MUL], ident[:])
                        for m in range(3):
                            ins = pe.transpose(pT[t % 2][:, 1 + m], v[:, m], ident[:])
                        ins.then_inc(transposed, 1)

                    def project(t):
                        pe.wait_ge(xT_made, t + 1)
                        if t >= 2:
                            pe.wait_ge(up_copied, t - 1)
                        for c in range(4):
                            ins = pe.matmul(pU[t % 2][:, c], xT[:, t % 2, c], (wup0 if c == 0 else wup1)[:],
                                            start=True, stop=True)
                        ins.then_inc(up_done, 1)

                    transpose(0)
                    for t in range(NODE_TILES):
                        if t + 1 < NODE_TILES:
                            transpose(t + 1)
                        project(t)
                    pe.wait_ge(row0_made, 1)
                    pe.matmul(pF[:], ones[0:1, :], dst_f[0:1, 0:TILES:BLOCK_TILES], start=True, stop=True
                              ).then_inc(first_ready, 1)
                    pe.wait_ge(ok_made, 1)
                    pe.matmul(pC[:], ones[:], hilo[:, 2:3], start=True, stop=True).then_inc(ok_summed, 1)

            with ExitStack() as s:
                ef = sb(s, "ef", [2 * BASIS, HALF])
                h = [sb(s, f"h{k}", [2 * HIDDEN, HALF]) for k in range(2)]
                h3 = [sb(s, f"h3_{k}", [2 * HIDDEN, HALF], f32r) for k in range(2)]
                h3_full = [sb(s, f"h3_full{k}", [2 * HIDDEN, HALF]) for k in range(2)]
                zeros = sb(s, "zeros", [P, CLEAR_MAX])
                gidx = sb(s, "gidx", [P, ITER_TILES], i32)
                S = sb(s, "S", [P, ITER_TILES, 4, MUL])
                M = sb(s, "M", [P, 3, 8, MUL])
                eq = sb(s, "eq", [P, 2, BLOCK_TILES, WINDOW])
                hot = sb(s, "hot", [P, 2, BLOCK_TILES, 4, WINDOW])
                sums = sb(s, "sums", [P, 2, ACC_COLS])
                fidx_f = sb(s, "fidx_f", [P, 2])
                fidx = sb(s, "fidx", [P, 2], i32)
                pass_row = sb(s, "pass_row", [P, 1])
                pW = [ps(s, f"pW{k}", [P, 4, MUL]) for k in range(3)]
                pZ = [ps(s, f"pZ{k}", [P, HALF]) for k in range(3)]
                pA = [ps(s, f"pA{k}", [P, ACC_COLS]) for k in range(2)]
                (ef_loaded, z_ready, h_ready, w_ready, product, scattered, hot_step, hot_ready,
                 sums_copied, parts_ready, zeroed, acc_cleared, slot_cleared, idx_made, fidx_step, fidx_made, pass_step,
                 window_moved) = sems(
                    s, "ef_loaded", "z_ready", "h_ready", "w_ready", "product", "scattered",
                    "hot_step", "hot_ready", "sums_copied", "parts_ready", "zeroed",
                    "acc_cleared", "slot_cleared", "idx_made", "fidx_step",
                    "fidx_made", "pass_step", "window_moved")
                gathered = sems(s, *[f"gathered{j}" for j in range(ITER_TILES)])
                flushed = sems(s, "flushed0", "flushed1")
                block = s.enter_context(nc.Block())
                RING = 3

                def passes(eng):
                    return eng.value_load(npass_i[0:1, 0:1], min_val=1, max_val=PASSES)

                @block.sync
                def _(sp):
                    n = passes(sp)
                    sp.dma_start(ef[:], edge_f[0]).then_inc(ef_loaded, 16)
                    sp.wait_ge(zeroed, 1)
                    for part, done in ((acc, acc_cleared), (slot_x, slot_cleared)):
                        flat = part.rearrange("r c -> (r c)").rearrange("(p n) -> p n", p=P)
                        for a in range(0, flat.shape[1], CLEAR_MAX):
                            b = min(a + CLEAR_MAX, flat.shape[1])
                            sp.dma_start(flat[:, a:b], zeros[:, 0:b - a]).then_inc(done, 16)
                    sp.wait_ge(z_ready, 1)
                    sp.dma_start(ef[:], edge_f[1]).then_inc(ef_loaded, 16)
                    sp.wait_ge(z_ready, 5)
                    sp.dma_start(ef[:], edge_f[2]).then_inc(ef_loaded, 16)
                    with sp.Fori(0, n) as p:
                        with sp.Fori(0, ITERS) as i:
                            g = p * ITERS + i
                            sp.wait_ge(z_ready, g * 4 + 9)
                            sp.dma_start(ef[:], edge_f[bass.ds(i + 3, 1)].rearrange("o r n -> (o r) n")
                                         ).then_inc(ef_loaded, 16)
                    sp.wait_ge(ef_loaded, n * (16 * ITERS) + 48)
                    sp.nop(nofuse=True)
                    sp.wait_ge(slot_cleared, 16 * (-(-SLOT_ROWS * DIM // P // CLEAR_MAX)))

                @block.scalar
                def _(act):
                    n = passes(act)
                    act.sem_inc(sums_copied, 2)

                    def silu(layer, z):
                        act.wait_ge(z_ready, z)
                        scale = (1.0 / BASIS ** 0.5, SILU_2MOM / HIDDEN ** 0.5, SILU_2MOM / HIDDEN ** 0.5)
                        act.activation(h[layer][:], pZ[layer % 2][:], ACT.Silu, scale=scale[layer]
                                       ).then_inc(h_ready, 1)

                    def copy_sums(g, k):
                        act.wait_ge(scattered, g * ITER_TILES + (ITER_TILES + BLOCK_TILES * (k + 1)))
                        act.wait_ge(flushed[k], g * 16 + 16)
                        act.activation(sums[:, k, 0:2 * MUL], pA[k][:, 0:2 * MUL], ACT.Copy)
                        act.activation(sums[0:64, k, 2 * MUL:], pA[k][0:64, 2 * MUL:], ACT.Copy
                                       ).then_inc(sums_copied, 1)

                    def silu_parts(q, z):
                        act.wait_ge(z_ready, z)
                        scale = SILU_2MOM / HIDDEN ** 0.5
                        act.activation(h3[q][:], pZ[2 * (1 - q)][:], ACT.Silu, scale=scale)
                        act.activation(h3_full[q][HIDDEN:], pZ[2 * (1 - q)][HIDDEN:], ACT.Silu, scale=scale
                                       ).then_inc(h_ready, 1)

                    silu(0, 1)
                    silu(1, 2)
                    silu_parts(0, 3)
                    silu_parts(1, 4)
                    silu(0, 5)
                    silu(1, 6)
                    with act.Fori(0, n) as p:
                        with act.Fori(0, ITERS) as i:
                            g = p * ITERS + i
                            for q in range(2):
                                act.wait_ge(w_ready, g * ITER_TILES + BLOCK_TILES * (q + 1))
                                silu_parts(q, g * 4 + (7 + q))
                                if q == 0:
                                    copy_sums(g, 0)
                            silu(0, g * 4 + 9)
                            silu(1, g * 4 + 10)
                            copy_sums(g, 1)

                @block.gpsimd
                def _(pool):
                    n = passes(pool)
                    pool.memset(zeros[:], 0.0).then_inc(zeroed, 1)
                    pool.memset(pass_row[:], 0.0).then_inc(pass_step, 1)

                    def gather(j):
                        pool.indirect_dma_start(
                            S[:, j].rearrange("p c u -> p (c u)"), None, table,
                            bass.IndirectOffsetOnAxis(ap=gidx[:, j:j + 1], axis=0)
                        ).then_inc(gathered[j], 16)

                    for k in range(2):
                        half = slice(BLOCK_TILES * k, BLOCK_TILES * (k + 1))
                        pool.tensor_copy(gidx[:, half], src_sb[:, half]).then_inc(idx_made, 1)
                    pool.wait_ge(idx_made, 2)
                    for j in range(ITER_TILES):
                        gather(j)
                    pool.wait_ge(acc_cleared, 16 * (-(-4 * ACC_ROWS * ACC_COLS // P // CLEAR_MAX)))
                    for k in range(2):
                        pool.dma_start(sums[:, k], acc[0:P, :]).then_inc(flushed[k], 16)
                    for k in range(2):
                        pool.wait_ge(flushed[k], 16)
                    with pool.Fori(0, n) as p:
                        with pool.Fori(0, ITERS) as i:
                            g = p * ITERS + i
                            g6 = g * ITER_TILES
                            for k in range(2):
                                for j in range(BLOCK_TILES * k, BLOCK_TILES * (k + 1)):
                                    pool.wait_ge(gathered[j], g * 16 + 16)
                                pool.nop(nofuse=True)
                                pool.tensor_copy(
                                    gidx[:, BLOCK_TILES * k:BLOCK_TILES * (k + 1)],
                                    src_sb[:, bass.ds(i * ITER_TILES + (ITER_TILES + BLOCK_TILES * k),
                                                      BLOCK_TILES)]).then_inc(idx_made, 1)
                                pool.wait_ge(idx_made, g * 2 + (k + 3))
                                for j in range(BLOCK_TILES * k, BLOCK_TILES * (k + 1)):
                                    pool.wait_ge(product, g6 + (RING + j + 1))
                                    pool.nop(nofuse=True)
                                    gather(j)
                                pool.wait_ge(pass_step, p + 1)
                                pool.tensor_tensor(fidx_f[:, k:k + 1],
                                                   sum_row[:, bass.ds(i * 2 + k, 1)],
                                                   pass_row[:], ALU.add).then_inc(fidx_step, 1)
                                pool.wait_ge(fidx_step, g * 2 + (k + 1))
                                pool.nop(nofuse=True)
                                pool.tensor_copy(fidx[:, k:k + 1], fidx_f[:, k:k + 1]
                                                 ).then_inc(fidx_made, 1)
                                pool.wait_ge(fidx_made, g * 2 + (k + 1))
                                if k == 0:
                                    pool.wait_ge(flushed[1], g * 16 + 16)
                                else:
                                    pool.wait_ge(flushed[0], g * 16 + 32)
                                pool.wait_ge(sums_copied, g * 2 + (k + 3))
                                pool.nop(nofuse=True)
                                pool.indirect_dma_start(
                                    acc, bass.IndirectOffsetOnAxis(ap=fidx[:, k:k + 1], axis=0),
                                    sums[:, k], None, compute_op=ALU.add).then_inc(flushed[k], 16)
                        pool.tensor_tensor(pass_row[:], pass_row[:], window_step[:], ALU.add
                                           ).then_inc(pass_step, 1)
                    for j in range(ITER_TILES):
                        pool.wait_ge(gathered[j], n * (16 * ITERS) + 16)
                    for k in range(2):
                        pool.wait_ge(flushed[k], n * (16 * ITERS) + 16)

                @block.vector
                def _(dve):
                    n = passes(dve)
                    dve.sem_inc(product, RING)

                    def receivers(g, i, k):
                        tiles = bass.ds(i * ITER_TILES + BLOCK_TILES * k, BLOCK_TILES)
                        dve.wait_ge(scattered, g * ITER_TILES + BLOCK_TILES * (k + 1))
                        dve.tensor_tensor(
                            eq[:, k], dst_f[:, tiles, None].broadcast_to((P, BLOCK_TILES, WINDOW)),
                            window_iota[:, None, :].broadcast_to((P, BLOCK_TILES, WINDOW)),
                            ALU.is_equal).then_inc(hot_step, 1)

                    def one_hots(g, i, k):
                        tiles = bass.ds(i * ITER_TILES + BLOCK_TILES * k, BLOCK_TILES)
                        dve.wait_ge(hot_step, g * 2 + (k + 1))
                        dve.tensor_tensor(
                            hot[:, k],
                            eq[:, k, :, None, :].broadcast_to((P, BLOCK_TILES, 4, WINDOW)),
                            y_sb[:, tiles, :, None].broadcast_to((P, BLOCK_TILES, 4, WINDOW)),
                            ALU.mult).then_inc(hot_ready, 1)

                    def products(g, g6, j):
                        W, m = pW[j % 3], M[:, j % 3]
                        dve.wait_ge(w_ready, g6 + (j + 1))
                        dve.wait_ge(gathered[j], g * 16 + 16)
                        dve.wait_ge(scattered, g6 + (j + 1 + ITER_TILES - RING))
                        dve.tensor_tensor(m[:, 0:2], W[:, 0:2],
                                          S[:, j, 0:1].broadcast_to((P, 2, MUL)), ALU.mult)
                        dve.tensor_tensor(
                            m[:, 2:8].rearrange("p (a b) u -> p a b u", a=2),
                            W[:, 2:4, None, :].broadcast_to((P, 2, 3, MUL)),
                            S[:, j, None, 1:4].broadcast_to((P, 2, 3, MUL)), ALU.mult
                        ).then_inc(product, 1)

                    def parts(q, count):
                        dve.wait_ge(h_ready, count)
                        dve.tensor_tensor(h3[q][HIDDEN:], h3_full[q][HIDDEN:],
                                          h3[q][HIDDEN:].bitcast(fp32), ALU.subtract
                                          ).then_inc(parts_ready, 1)

                    parts(0, 3)
                    parts(1, 4)
                    with dve.Fori(0, n) as p:
                        with dve.Fori(0, ITERS) as i:
                            g = p * ITERS + i
                            g6 = g * ITER_TILES
                            receivers(g, i, 0)
                            products(g, g6, 0)
                            one_hots(g, i, 0)
                            products(g, g6, 1)
                            receivers(g, i, 1)
                            products(g, g6, 2)
                            one_hots(g, i, 1)
                            parts(0, g * 4 + 7)
                            products(g, g6, 3)
                            products(g, g6, 4)
                            products(g, g6, 5)
                            parts(1, g * 4 + 8)
                        dve.tensor_scalar(window_iota[:], window_iota[:], window_step[:, 0:1], None,
                                          ALU.add).then_inc(window_moved, 1)
                        dve.wait_ge(window_moved, p + 1)

                @block.tensor
                def _(pe):
                    n = passes(pe)
                    pe.sem_inc(scattered, ITER_TILES)

                    def mlp(layer, done, chunk=None, half=None):
                        if layer == 0:
                            pe.wait_ge(ef_loaded, chunk)
                        if done is not None:
                            pe.wait_ge(h_ready, done)
                        if layer < 2:
                            pe.matmul(pZ[layer][:], (wm1, wm2)[layer][:], (ef, h[0])[layer][:],
                                      start=True, stop=True).then_inc(z_ready, 1)
                            return
                        for q in (0, 1) if half is None else (half,):
                            r = HIDDEN * q
                            pe.matmul(pZ[2 * (1 - q)][:], wm3[r:r + HIDDEN, :], h[1][r:r + HIDDEN, :],
                                      start=True, stop=True).then_inc(z_ready, 1)

                    def edge_weights(j, free):
                        pe.wait_ge(product, free)
                        q, c = j // BLOCK_TILES, P * (j % BLOCK_TILES)
                        for n, w in enumerate((wm4_hi, wm4_lo)):
                            ins = pe.matmul(pW[j % 3][:].rearrange("p c u -> p (c u)"),
                                            h3[q][:, c:c + P], w[:], start=n == 0, stop=n == 1)
                        ins.then_inc(w_ready, 1)

                    def scatter(g, g6, j):
                        k, t = j // BLOCK_TILES, j % BLOCK_TILES
                        if t == 0:
                            pe.wait_ge(hot_ready, g * 2 + (k + 1))
                            pe.wait_ge(sums_copied, g * 2 + (k + 1))
                        pe.wait_ge(product, g6 + (j + 1 + RING))
                        A, m, first, last = pA[k], M[:, j % 3], t == 0, t == BLOCK_TILES - 1
                        for grp, y, units, c in ((0, 0, (0, 2), 0), (1, 0, (3, 4), 0), (2, 1, (1, 5), 0),
                                                 (3, 2, (1, 6), 0), (0, 3, (1,), 2), (1, 3, (7,), 2)):
                            lo = 32 * grp
                            if len(units) == 2:
                                mov = m[:, units[0]:units[1] + 1:units[1] - units[0]]
                            else:
                                mov = m[:, units[0]:units[0] + 1]
                            ins = pe.matmul(A[lo:lo + 32, c * MUL:(c + len(units)) * MUL],
                                            hot[:, k, t, y], mov, start=first and c == 0, stop=last,
                                            skip_group_check=True)
                        ins.then_inc(scattered, 1)

                    for layer in range(3):
                        mlp(layer, layer or None, 16)
                    mlp(0, 4, 32)
                    mlp(1, 5)
                    pe.wait_ge(parts_ready, 1)
                    edge_weights(0, 1)
                    edge_weights(1, 2)
                    with pe.Fori(0, n) as p:
                        with pe.Fori(0, ITERS) as i:
                            g = p * ITERS + i
                            g6 = g * ITER_TILES
                            for j in range(ITER_TILES):
                                nxt = j + 2
                                if nxt % BLOCK_TILES == 0:
                                    pe.wait_ge(parts_ready, g * 2 + (nxt // BLOCK_TILES + 1))
                                edge_weights(nxt % ITER_TILES, g6 + (nxt + 1))
                                scatter(g, g6, j)
                                if j == 0:
                                    mlp(2, g * 4 + 6, half=0)
                                elif j == 2:
                                    mlp(2, g * 4 + 6, half=1)
                                elif j == 4:
                                    mlp(0, g * 4 + 8, g * 16 + 48)
                                elif j == 5:
                                    mlp(1, g * 4 + 9)

        xn2 = sb(ctx, "xn2", [P, NODE_TILES, DIM])
        mask = sb(ctx, "mask", [P, NODE_TILES, 2, EXPERTS])
        mask12 = sb(ctx, "mask12", [P, NODE_TILES, EXPERTS])
        gates = sb(ctx, "gates", [P, NODE_TILES, EXPERTS])
        prob = sb(ctx, "prob", [P, NODE_TILES, 8])
        slot_i = sb(ctx, "slot_i", [P, NODE_TILES, 2], i32)
        expert_i = sb(ctx, "expert_i", [P, SLOT_BLOCKS], i32)

        with ExitStack() as s:
            A = sb(s, "A", [P, 2, 4, ACC_COLS])
            msgT = sb(s, "msgT", [P, 2, 8, P])
            x2T = sb(s, "x2T", [P, 2, KC, P])
            stats = sb(s, "stats2", [P, 6])
            mv = sb(s, "mv2", [P, 2])
            rstd = sb(s, "rstd2", [P, 1])
            nmax = sb(s, "nmax", [P, 1])
            esum = sb(s, "esum", [P, 1])
            erec = sb(s, "erec", [P, 1])
            ex = sb(s, "ex", [P, EXPERTS])
            top_i = sb(s, "top_i", [P, 8], u32)
            top_f = sb(s, "top_f", [P, 8])
            weighted = sb(s, "weighted", [P, 2, EXPERTS])
            iota_i = sb(s, "iota2_i", [P, EXPERTS], i32)
            iota_f = sb(s, "iota2_f", [P, EXPERTS])
            pM = [ps(s, f"pM{k}", [P, 4, P]) for k in range(2)]
            pO = [ps(s, f"pO{k}", [P, 4, MUL]) for k in range(2)]
            pX = ps(s, "pX", [P, KC, P])
            pL = ps(s, "pL", [P, EXPERTS])
            (iota_made, sums_added, msg_transposed, msg_copied, out_done, chain3, sqrt_ready,
             sqrt_done, xn_made, x_transposed, x_copied, logits, max_made, exp_done,
             cleared) = sems(
                s, "iota3_made", "sums_added", "msg_transposed", "msg_copied", "out_done", "chain3",
                "sqrt_ready3", "sqrt_done3", "xn_made3", "x_transposed", "x_copied", "logits",
                "max_made", "exp_done", "cleared3")
            acc_loaded = sems(s, "acc_loaded0", "acc_loaded1")
            block = s.enter_context(nc.Block())

            @block.sync
            def _(sp):
                for t in range(NODE_TILES):
                    if t >= 2:
                        sp.wait_ge(msg_transposed, 2 * (t - 1))
                    sp.dma_start(A[:, t % 2],
                                 acc.rearrange("(g n) c -> n g c", g=4)[t * P:(t + 1) * P]
                                 ).then_inc(acc_loaded[t % 2], 16)

            @block.gpsimd
            def _(pool):
                pool.iota(iota_i[:], pattern=[[1, EXPERTS]], base=0, channel_multiplier=0
                          ).then_inc(iota_made, 1)

            @block.tensor
            def _(pe):
                for t in range(NODE_TILES):
                    a = A[:, t % 2]
                    pe.wait_ge(sums_added, t + 1)
                    parts = [a[:, 0, 0:P], a[:, 1, 2 * P:],
                             a[:, 2, 0:P], a[:, 0, P:2 * P], a[:, 3, 0:P], a[:, 1, 0:P],
                             a[:, 0, 2 * P:], a[:, 1, P:2 * P]]
                    for q in range(2):
                        if t >= 1:
                            pe.wait_ge(msg_copied, 2 * (t - 1) + q + 1)
                        for u in range(4):
                            ins = pe.transpose(pM[q][:, u], parts[4 * q + u], ident[:])
                        ins.then_inc(msg_transposed, 1)
                    pe.wait_ge(msg_copied, 2 * t + 2)
                    for c in range(4):
                        w = wout0 if c == 0 else wout1
                        for q in range(2):
                            ins = pe.matmul(pO[t % 2][:, c], msgT[:, t % 2, 2 * c + q], w[:, q],
                                            start=q == 0, stop=q == 1)
                    ins.then_inc(out_done, 1)
                    pe.wait_ge(xn_made, t + 1)
                    for k in range(KC):
                        ins = pe.transpose(pX[:, k], xn2[:, t, k * P:(k + 1) * P], ident[:])
                    ins.then_inc(x_transposed, 1)
                    pe.wait_ge(x_copied, t + 1)
                    for k in range(KC):
                        ins = pe.matmul(pL[:], x2T[:, t % 2, k], wg[:, k], start=k == 0, stop=k == KC - 1)
                    ins.then_inc(logits, 1)

            @block.scalar
            def _(act):
                for t in range(NODE_TILES):
                    for q in range(2):
                        act.wait_ge(msg_transposed, 2 * t + q + 1)
                        act.activation(msgT[:, t % 2, 4 * q:4 * q + 4], pM[q][:], ACT.Copy
                                       ).then_inc(msg_copied, 1)
                    act.wait_ge(sqrt_ready, t + 1)
                    act.activation(rstd[:], mv[:, 1:2], ACT.Sqrt, bias=eps[:, 0:1]).then_inc(sqrt_done, 1)
                    act.wait_ge(x_transposed, t + 1)
                    act.activation(x2T[:, t % 2], pX[:], ACT.Copy).then_inc(x_copied, 1)
                    act.wait_ge(max_made, t + 1)
                    act.activation(ex[:], pL[:], ACT.Exp, bias=nmax[:, 0:1], accum_out=esum[:]
                                   ).then_inc(exp_done, 1)

            @block.vector
            def _(dve):
                chain = Chain(dve, chain3)
                dve.wait_ge(iota_made, 1)
                chain.link(dve.tensor_copy(iota_f[:], iota_i[:]))
                chain.link(dve.memset(mask[:], 0.0))
                chain.link(dve.memset(mask12[:], 0.0))
                scale = 1.0 / (2 * MUL) ** 0.5 / NEIGHBORS
                for t in range(NODE_TILES):
                    a, r = A[:, t % 2], rows(t)
                    dve.wait_ge(acc_loaded[t % 2], 16 * (t // 2 + 1))
                    chain.link(dve.tensor_tensor(a[:, 1, 2 * P:], a[:, 1, 2 * P:], a[:, 2, P:2 * P], ALU.add))
                    dve.tensor_tensor(a[:, 1, 2 * P:], a[:, 1, 2 * P:], a[:, 3, P:2 * P], ALU.add
                                      ).then_inc(sums_added, 1)
                    dve.wait_ge(out_done, t + 1)
                    o = pO[t % 2]
                    xv = X[:, t, MUL:].rearrange("p (u m) -> p m u", m=3)
                    chain.link(dve.scalar_tensor_tensor(X[:, t, 0:MUL], o[:, 0], scale, X[:, t, 0:MUL],
                                                        ALU.mult, ALU.add))
                    chain.link(dve.scalar_tensor_tensor(xv, o[:, 1:4], scale, xv, ALU.mult, ALU.add))
                    chain.link(dve.bn_stats(stats[:], X[:, t, :]))
                    dve.bn_aggr(mv[:], stats[:]).then_inc(sqrt_ready, 1)
                    dve.wait_ge(sqrt_done, t + 1)
                    chain.link(dve.reciprocal(rstd[:], rstd[:]))
                    dve.tensor_scalar(xn2[:, t, :], X[:, t, :], mv[:, 0:1], rstd[:, 0:1],
                                      ALU.subtract, ALU.mult).then_inc(xn_made, 1)
                    dve.wait_ge(logits, t + 1)
                    dve.tensor_reduce(nmax[:], pL[:], AX.X, ALU.max, negate=True).then_inc(max_made, 1)
                    dve.wait_ge(exp_done, t + 1)
                    chain.link(dve.reciprocal(erec[:], esum[:]))
                    chain.link(dve.tensor_scalar(ex[:], ex[:], erec[:, 0:1], None, ALU.mult))
                    chain.link(dve.max(prob[:, t, :], ex[:]))
                    chain.link(dve.max_index(top_i[:], prob[:, t, :], ex[:]))
                    chain.link(dve.tensor_copy(top_f[:], top_i[:]))
                    for q in range(2):
                        chain.link(dve.tensor_scalar(mask[0:r, t, q], iota_f[0:r], top_f[0:r, q:q + 1], None,
                                                     ALU.is_equal))
                        chain.link(dve.tensor_scalar(weighted[:, q], mask[:, t, q], prob[:, t, q:q + 1], None,
                                                     ALU.mult))
                    chain.link(dve.tensor_tensor(mask12[:, t], mask[:, t, 0], mask[:, t, 1], ALU.add))
                    chain.link(dve.tensor_tensor(gates[:, t], weighted[:, 0], weighted[:, 1], ALU.add))

        with ExitStack() as s:
            before = sb(s, "before", [P, P])
            run = sb(s, "run", [P, NODE_TILES + 1, EXPERTS])
            rank = sb(s, "rank", [P, NODE_TILES, EXPERTS])
            thr_i = sb(s, "thr_i", [P, NODE_TILES], i32)
            thr = sb(s, "thr", [P, NODE_TILES])
            over = sb(s, "over", [P, EXPERTS, NODE_TILES])
            nblk = sb(s, "nblk", [P, EXPERTS])
            end = sb(s, "end", [P, EXPERTS + 1])
            base = sb(s, "base", [P, EXPERTS])
            slot_f = sb(s, "slot_f", [P, NODE_TILES, 2])
            picked = sb(s, "picked", [P, NODE_TILES, EXPERTS])
            blk_i = sb(s, "blk_i", [P, SLOT_BLOCKS], i32)
            blk = sb(s, "blk", [P, SLOT_BLOCKS])
            passed = sb(s, "passed", [P, SLOT_BLOCKS, EXPERTS - 1])
            expert_f = sb(s, "expert_f", [P, SLOT_BLOCKS])
            pR = ps(s, "pR", [P, NODE_TILES, EXPERTS])
            pT_ = ps(s, "pTot", [P, NODE_TILES, EXPERTS])
            (tri_made, iota_made, ranked, chain4, slots_made, scattered4) = sems(
                s, "tri_made", "iota4_made", "ranked", "chain4", "slots_made", "scattered4")
            block = s.enter_context(nc.Block())

            @block.gpsimd
            def _(pool):
                pool.affine_select(out=before[:], in_=ones[:], compare_op=ALU.is_gt, fill=0.0, base=0,
                                   pattern=[[1, P]], channel_multiplier=-1).then_inc(tri_made, 1)
                pool.iota(thr_i[:], pattern=[[P, NODE_TILES]], base=0, channel_multiplier=0
                          ).then_inc(iota_made, 1)
                pool.iota(blk_i[:], pattern=[[1, SLOT_BLOCKS]], base=0, channel_multiplier=0
                          ).then_inc(iota_made, 1)
                pool.wait_ge(slots_made, 1)
                for t in range(NODE_TILES):
                    for q in range(2):
                        pool.indirect_dma_start(
                            slot_x, bass.IndirectOffsetOnAxis(ap=slot_i[0:rows(t), t, q:q + 1], axis=0),
                            xn2[0:rows(t), t, :], None).then_inc(scattered4, 16)
                pool.wait_ge(scattered4, 16 * 2 * NODE_TILES)

            @block.tensor
            def _(pe):
                pe.wait_ge(tri_made, 1)
                flat = mask12[:].rearrange("p t e -> p (t e)")
                pe.matmul(pR[:].rearrange("p t e -> p (t e)"), before[:], flat, start=True, stop=True)
                pe.matmul(pT_[:].rearrange("p t e -> p (t e)"), ones[:], flat, start=True, stop=True
                          ).then_inc(ranked, 1)

            @block.vector
            def _(dve):
                chain = Chain(dve, chain4)
                chain.link(dve.memset(run[:, 0], 0.0))
                dve.wait_ge(ranked, 1)
                for t in range(NODE_TILES):
                    chain.link(dve.tensor_tensor(run[:, t + 1], run[:, t], pT_[:, t], ALU.add))
                chain.link(dve.tensor_tensor(rank[:], pR[:], run[:, 0:NODE_TILES], ALU.add))
                dve.wait_ge(iota_made, 2)
                chain.link(dve.tensor_copy(thr[:], thr_i[:]))
                chain.link(dve.tensor_copy(blk[:], blk_i[:]))
                chain.link(dve.tensor_tensor(
                    over[:], run[:, NODE_TILES, :, None].broadcast_to((P, EXPERTS, NODE_TILES)),
                    thr[:, None, :].broadcast_to((P, EXPERTS, NODE_TILES)), ALU.is_gt))
                chain.link(dve.tensor_reduce(nblk[:], over[:], AX.X, ALU.add))
                chain.link(dve.memset(end[:], 0.0))
                for e in range(EXPERTS):
                    chain.link(dve.tensor_tensor(end[:, e + 1:e + 2], end[:, e:e + 1], nblk[:, e:e + 1],
                                                 ALU.add))
                chain.link(dve.tensor_scalar(base[:], end[:, 0:EXPERTS], float(P), None, ALU.mult))
                chain.link(dve.tensor_tensor(rank[:], rank[:],
                                             base[:, None, :].broadcast_to((P, NODE_TILES, EXPERTS)),
                                             ALU.add))
                for q in range(2):
                    chain.link(dve.tensor_tensor(picked[:], rank[:], mask[:, :, q], ALU.mult))
                    chain.link(dve.tensor_reduce(slot_f[:, :, q], picked[:], AX.X, ALU.add))
                dve.tensor_copy(slot_i[:], slot_f[:]).then_inc(slots_made, 1)
                chain.link(dve.tensor_tensor(
                    passed[:], blk[:, :, None].broadcast_to((P, SLOT_BLOCKS, EXPERTS - 1)),
                    end[:, None, 1:EXPERTS].broadcast_to((P, SLOT_BLOCKS, EXPERTS - 1)), ALU.is_ge))
                chain.link(dve.tensor_reduce(expert_f[:], passed[:], AX.X, ALU.add))
                chain.link(dve.tensor_copy(expert_i[:], expert_f[:]))

        with ExitStack() as s:
            w1 = [sb(s, f"w1_{k}", [P, KC, FFN]) for k in range(2)]
            w2 = [sb(s, f"w2_{k}", [P, HC, DIM]) for k in range(2)]
            b1 = [sb(s, f"b1_{k}", [P, HC]) for k in range(2)]
            xg = [sb(s, f"xg{k}", [P, DIM]) for k in range(2)]
            xgT = sb(s, "xgT", [P, KC, P])
            hT = sb(s, "hT", [P, HC, P])
            yb = [sb(s, f"yb{k}", [P, DIM]) for k in range(2)]
            pX = ps(s, "pX5", [P, KC, P])
            pH = [ps(s, f"pH{k}", [P, 4, P]) for k in range(2)]
            pY = ps(s, "pY", [P, DIM])
            (x_transposed, x_copied, hidden, gelu_done, y_ready, y_copied, y_saved, y_free) = sems(
                s, "x_transposed5", "x_copied5", "hidden", "gelu_done", "y_ready", "y_copied",
                "y_saved", "y_free")
            x_loaded = sems(s, "xg_loaded0", "xg_loaded1")
            w1_loaded = sems(s, "w1_loaded0", "w1_loaded1")
            w2_loaded = sems(s, "w2_loaded0", "w2_loaded1")
            b1_loaded = sems(s, "b1_loaded0", "b1_loaded1")
            block = s.enter_context(nc.Block())
            PAIRS, ODD = SLOT_BLOCKS // 2, SLOT_BLOCKS % 2

            def over_blocks(eng, body):
                with eng.Fori(0, PAIRS) as n:
                    for k in range(2):
                        body(n * 2 + k, n, k)
                if ODD:
                    body(2 * PAIRS, PAIRS, 0)

            @block.sync
            def _(sp):
                def load(b, n, k):
                    e = sp.value_load(expert_i[0:1, bass.ds(b, 1)], min_val=0, max_val=EXPERTS - 1)
                    sp.wait_ge(y_ready, n * 2 + (k + 1))
                    sp.nop(nofuse=True)
                    sp.dma_start(xg[k][:], slot_x[bass.ds(b * P, P), :]).then_inc(x_loaded[k], 16)
                    sp.dma_start(w1[k][:], w_1[bass.ds(e, 1)].rearrange("o (c p) h -> p (o c) h", p=P)
                                 ).then_inc(w1_loaded[k], 16)
                    sp.dma_start(b1[k][:], b_1[bass.ds(e, 1)].rearrange("o p c -> (o p) c")
                                 ).then_inc(b1_loaded[k], 16)
                    sp.dma_start(w2[k][:], w_2[bass.ds(e, 1)].rearrange("o (c p) h -> p (o c) h", p=P)
                                 ).then_inc(w2_loaded[k], 16)

                over_blocks(sp, load)

            @block.tensor
            def _(pe):
                pe.sem_inc(y_ready, 2)

                def compute(b, n, k):
                    pe.wait_ge(x_loaded[k], n * 16 + 16)
                    for c in range(KC):
                        ins = pe.transpose(pX[:, c], xg[k][:, c * P:(c + 1) * P], ident[:])
                    ins.then_inc(x_transposed, 1)
                    pe.wait_ge(w1_loaded[k], n * 16 + 16)
                    pe.wait_ge(x_copied, b + 1)
                    for q in range(HC // 4):
                        for u in range(4):
                            for c in range(KC):
                                hc = 4 * q + u
                                ins = pe.matmul(pH[q][:, u], w1[k][:, c, hc * P:(hc + 1) * P], xgT[:, c],
                                                start=c == 0, stop=c == KC - 1)
                        ins.then_inc(hidden, 1)
                    pe.wait_ge(w2_loaded[k], n * 16 + 16)
                    pe.wait_ge(y_copied, b + 1)
                    for hc in range(HC):
                        if hc % 4 == 0:
                            pe.wait_ge(gelu_done, b * 2 + (hc // 4 + 1))
                        ins = pe.matmul(pY[:], hT[:, hc], w2[k][:, hc], start=hc == 0, stop=hc == HC - 1)
                    ins.then_inc(y_ready, 1)

                over_blocks(pe, compute)

            @block.scalar
            def _(act):
                def gelu(b, n, k):
                    act.wait_ge(b1_loaded[k], n * 16 + 16)
                    act.wait_ge(y_ready, b + 2)
                    for q in range(HC // 4):
                        act.wait_ge(hidden, b * 2 + (q + 1))
                        for u in range(4):
                            hc = 4 * q + u
                            ins = act.activation(hT[:, hc], pH[q][:, u], ACT.Gelu_apprx_tanh,
                                                 bias=b1[k][:, hc:hc + 1])
                        ins.then_inc(gelu_done, 1)

                over_blocks(act, gelu)

            @block.vector
            def _(dve):
                dve.sem_inc(y_copied, 1)

                def copy(b, n, k):
                    dve.wait_ge(x_transposed, b + 1)
                    dve.tensor_copy(xgT[:], pX[:]).then_inc(x_copied, 1)
                    dve.wait_ge(y_ready, b + 3)
                    dve.wait_ge(y_free, b + 1)
                    dve.tensor_copy(yb[k][:], pY[:]).then_inc(y_copied, 1)

                over_blocks(dve, copy)

            @block.gpsimd
            def _(pool):
                pool.sem_inc(y_free, 2)

                def save(b, n, k):
                    pool.wait_ge(y_copied, b + 2)
                    pool.nop(nofuse=True)
                    pool.dma_start(slot_y[bass.ds(b * P, P), :], yb[k][:]).then_inc(y_saved, 16)
                    pool.wait_ge(y_saved, b * 16 + 16)
                    pool.sem_inc(y_free, 1)

                over_blocks(pool, save)

        with ExitStack() as s:
            Y = sb(s, "Y", [P, 2, 2, DIM])
            gT = sb(s, "gT", [EXPERTS, NODE_TILES, P])
            pG = [ps(s, f"pG{k}", [EXPERTS, P]) for k in range(2)]
            pB = [ps(s, f"pB{k}", [P, DIM]) for k in range(2)]
            (g_transposed, g_copied, b_ready, chain6, combined, saved) = sems(
                s, "g_transposed", "g_copied", "b_ready", "chain6", "combined", "saved")
            fetched = sems(s, "fetched0", "fetched1")
            block = s.enter_context(nc.Block())

            @block.gpsimd
            def _(pool):
                for t in range(NODE_TILES):
                    if t >= 2:
                        pool.wait_ge(combined, t - 1)
                    for q in range(2):
                        pool.indirect_dma_start(
                            Y[0:rows(t), t % 2, q, :], None, slot_y,
                            bass.IndirectOffsetOnAxis(ap=slot_i[0:rows(t), t, q:q + 1], axis=0)
                        ).then_inc(fetched[t % 2], 16)

            @block.tensor
            def _(pe):
                for t in range(NODE_TILES):
                    if t >= 2:
                        pe.wait_ge(g_copied, t - 1)
                    pe.transpose(pG[t % 2][:], gates[:, t], ident[:]).then_inc(g_transposed, 1)
                    pe.wait_ge(g_copied, t + 1)
                    if t >= 2:
                        pe.wait_ge(combined, t - 1)
                    pe.matmul(pB[t % 2][:], gT[:, t], b2[:], start=True, stop=True).then_inc(b_ready, 1)

            @block.scalar
            def _(act):
                for t in range(NODE_TILES):
                    act.wait_ge(g_transposed, t + 1)
                    act.activation(gT[:, t], pG[t % 2][:], ACT.Copy).then_inc(g_copied, 1)

            @block.vector
            def _(dve):
                chain = Chain(dve, chain6)
                for t in range(NODE_TILES):
                    r = rows(t)
                    dve.wait_ge(b_ready, t + 1)
                    chain.link(dve.tensor_tensor(X[0:r, t, :], X[0:r, t, :], pB[t % 2][0:r], ALU.add))
                    dve.wait_ge(fetched[t % 2], 32 * (t // 2 + 1))
                    chain.link(dve.scalar_tensor_tensor(X[0:r, t, :], Y[0:r, t % 2, 0], prob[0:r, t, 0:1],
                                                        X[0:r, t, :], ALU.mult, ALU.add))
                    dve.scalar_tensor_tensor(X[0:r, t, :], Y[0:r, t % 2, 1], prob[0:r, t, 1:2],
                                             X[0:r, t, :], ALU.mult, ALU.add).then_inc(combined, 1)

            @block.sync
            def _(sp):
                for t in range(NODE_TILES):
                    sp.wait_ge(combined, t + 1)
                    sp.dma_start(out[t * P:t * P + rows(t), :], X[0:rows(t), t, :]).then_inc(saved, 16)
                sp.wait_ge(saved, 16 * NODE_TILES)


def kernel(x, src, dst, edge_attr_4, edge_attr_8, L0_gnn_W_up0, L0_gnn_W_up1, L0_gnn_W_mlp1,
           L0_gnn_W_mlp2, L0_gnn_W_mlp3, L0_gnn_W_mlp4, L0_gnn_W_out0, L0_gnn_W_out1, L0_ffn_Wg,
           L0_ffn_W1, L0_ffn_b1, L0_ffn_W2, L0_ffn_b2):
    import numpy as np
    import concourse.bacc as bacc
    from concourse.bass_utils import run_bass_kernel_spmd

    pad = TILES * P - EDGES

    def tiles(a, mode="constant"):
        a = np.asarray(a)
        a = np.pad(a, [(0, pad)] + [(0, 0)] * (a.ndim - 1), mode=mode)
        return np.ascontiguousarray(a.reshape((TILES, P) + a.shape[1:]).swapaxes(0, 1))

    src_t = tiles(src)
    src_t = np.ascontiguousarray(np.concatenate([src_t, src_t[:, :ITER_TILES]], axis=1))
    basis = np.pad(np.asarray(edge_attr_8), [(0, pad), (0, 0)])
    basis = basis.reshape(ITERS, 2, HALF, BASIS).swapaxes(2, 3).reshape(ITERS, 2 * BASIS, HALF)
    basis = np.ascontiguousarray(np.concatenate([basis, basis[:3]], axis=0))
    b1 = np.ascontiguousarray(np.asarray(L0_ffn_b1).reshape(EXPERTS, HC, P).swapaxes(1, 2))

    arrays = {
        "x": np.ascontiguousarray(x), "src": src_t, "dst": tiles(dst, "edge"),
        "edge_y": tiles(edge_attr_4).reshape(P, TILES * 4), "edge_f": basis,
        "w_up0": np.ascontiguousarray(L0_gnn_W_up0), "w_up1": np.ascontiguousarray(L0_gnn_W_up1),
        "w_mlp1": np.ascontiguousarray(L0_gnn_W_mlp1), "w_mlp2": np.ascontiguousarray(L0_gnn_W_mlp2),
        "w_mlp3": np.ascontiguousarray(L0_gnn_W_mlp3), "w_mlp4": np.ascontiguousarray(L0_gnn_W_mlp4),
        "w_out0": np.ascontiguousarray(L0_gnn_W_out0), "w_out1": np.ascontiguousarray(L0_gnn_W_out1),
        "w_g": np.ascontiguousarray(L0_ffn_Wg), "w_1": np.ascontiguousarray(L0_ffn_W1), "b_1": b1,
        "w_2": np.ascontiguousarray(L0_ffn_W2), "b_2": np.ascontiguousarray(L0_ffn_b2),
    }
    nc = bacc.Bacc("TRN2", target_bir_lowering=False, num_devices=1)
    args = [nc.dram_tensor(n, a.shape, mybir.dt.from_np(a.dtype), kind="ExternalInput").ap()
            for n, a in arrays.items()]
    result = nc.dram_tensor("result", (NODES, DIM), mybir.dt.float32, kind="ExternalOutput").ap()
    program(nc, *args, result)
    r = run_bass_kernel_spmd(nc, [arrays], core_ids=[0])
    return r.results[0]["result"]
```

```python
import concourse.bass as bass
from concourse import mybir
from contextlib import ExitStack

NODES, DIM, EDGES = 1250, 512, 40000
MUL, BASIS, HIDDEN = 128, 8, 64
EXPERTS, FFN = 8, 1024
P = 128
NODE_TILES = -(-NODES // P)
LAST_ROWS = NODES - (NODE_TILES - 1) * P

WINDOW = 32
BLOCK_TILES = 3
ITER_TILES = 2 * BLOCK_TILES
ITERS = -(-EDGES // (ITER_TILES * P))
TILES = ITERS * ITER_TILES
BLOCKS = TILES // BLOCK_TILES
HALF = BLOCK_TILES * P
PASSES = -(-NODES // WINDOW)
ACC_ROWS = NODES + WINDOW + 2
ACC_COLS = 3 * MUL

ROW_TILES = 3
BLOCK_ROWS = ROW_TILES * P
MAX_BLOCKS = -(-NODES // BLOCK_ROWS)
SLOT_BLOCKS = 2 * NODES // BLOCK_ROWS + EXPERTS
CLEAR_ROWS = -(-(SLOT_BLOCKS + 1) * BLOCK_ROWS // ITERS)
SLOT_ROWS = CLEAR_ROWS * ITERS
CLEAR_COLS = CLEAR_ROWS * DIM // P
KC, HC = DIM // P, FFN // P
CHUNKS = 4
CHUNK = HC // CHUNKS
CLEAR_MAX = 2568

EPS = 1e-5
SILU_2MOM = 1.679177
SQRT3 = 3.0 ** 0.5
NEIGHBORS = 10.0


def program(nc, x, src, dst, edge_y, edge_f, w_up0, w_up1, w_mlp1, w_mlp2, w_mlp3, w_mlp4,
            w_out0, w_out1, w_g, w_1, b_1, w_2, b_2, out):
    fp32, f32r, i32 = mybir.dt.float32, mybir.dt.float32r, mybir.dt.int32
    u32 = mybir.dt.uint32
    ACT, ALU, AX = mybir.ActivationFunctionType, mybir.AluOpType, mybir.AxisListType

    table = nc.dram_tensor("sender_table", (NODES, DIM), fp32).ap()
    acc = nc.dram_tensor("window_sums", (4 * ACC_ROWS, ACC_COLS), fp32).ap()
    slots = nc.dram_tensor("expert_slots", (SLOT_ROWS, DIM), fp32).ap()

    ctx = ExitStack()
    with ctx:
        def sb(stack, name, shape, dt=fp32):
            return stack.enter_context(nc.sbuf_tensor(name, shape, dt))

        def ps(stack, name, shape):
            return stack.enter_context(nc.psum_tensor(name, shape, fp32))

        def sems(stack, *names):
            return [stack.enter_context(nc.semaphore(n)) for n in names]

        class Chain:

            def __init__(self, eng, sem):
                self.eng, self.sem, self.base, self.n = eng, sem, 0, 0

            def link(self, ins):
                self.n += 1
                ins.then_inc(self.sem, 1)
                self.eng.wait_ge(self.sem, self.base + self.n)

        def rows(t):
            return LAST_ROWS if t == NODE_TILES - 1 else P

        ident = sb(ctx, "ident", [P, P])
        ones = sb(ctx, "ones", [P, P])
        X = sb(ctx, "X", [P, NODE_TILES, DIM])
        wout0 = sb(ctx, "wout0", [P, 2, MUL])
        wout1 = sb(ctx, "wout1", [P, 2, MUL])
        wg = sb(ctx, "wg", [P, KC, EXPERTS])
        b2 = sb(ctx, "b2", [EXPERTS, DIM])
        eps = sb(ctx, "eps", [P, 1])

        edge_stack = ExitStack()
        with edge_stack:
            E = edge_stack
            src_sb = sb(E, "src_sb", [P, TILES + ITER_TILES], i32)
            dst_i = sb(E, "dst_i", [P, TILES], i32)
            dst_f = sb(E, "dst_f", [P, TILES])
            y_sb = sb(E, "y_sb", [P, TILES, 4])
            wm1 = sb(E, "wm1", [2 * BASIS, 2 * HIDDEN])
            wm2 = sb(E, "wm2", [2 * HIDDEN, 2 * HIDDEN])
            wm3 = sb(E, "wm3", [2 * HIDDEN, 2 * HIDDEN])
            wm4_hi = sb(E, "wm4_hi", [2 * HIDDEN, 4 * MUL], f32r)
            wm4_lo = sb(E, "wm4_lo", [2 * HIDDEN, 4 * MUL], f32r)
            window_iota = sb(E, "window_iota", [P, WINDOW])
            window_step = sb(E, "window_step", [P, 1])
            sum_row = sb(E, "sum_row", [P, BLOCKS])
            npass_i = sb(E, "npass_i", [P, 1], i32)

            with ExitStack() as s:
                wm4 = sb(s, "wm4", [2 * HIDDEN, 4 * MUL])
                wup0 = sb(s, "wup0", [P, MUL])
                wup1 = sb(s, "wup1", [P, MUL])
                stats = sb(s, "stats", [P, NODE_TILES, 6])
                mv = sb(s, "mv", [P, NODE_TILES, 2])
                rstd = sb(s, "rstd", [P, NODE_TILES])
                xn = sb(s, "xn", [P, 2, DIM])
                xT = sb(s, "xT", [P, 2, 4, P])
                up = sb(s, "up", [P, 2, 4, MUL])
                first = sb(s, "first", [P, BLOCKS])
                rel = sb(s, "rel", [P, TILES])
                hilo = sb(s, "hilo", [P, 4])
                row0 = sb(s, "row0", [P, 1], i32)
                row0f = sb(s, "row0f", [P, 1])
                iota_i = sb(s, "iota_i", [P, WINDOW], i32)
                pT = [ps(s, f"pT{k}", [P, 4, P]) for k in range(2)]
                pU = [ps(s, f"pU{k}", [P, 4, MUL]) for k in range(2)]
                pF = ps(s, "pF", [P, BLOCKS])
                pC = ps(s, "pC", [P, 1])
                (x_cleared, x_loaded, up_loaded, wout_loaded, small_loaded, dst_loaded, y_loaded,
                 blocks_cleared, mlp_loaded, ident_step, ident_made, ones_made,
                 iota_made, stats_done, sqrt_done, chain1, xn_made, transposed, xT_made, up_done,
                 up_copied, first_ready, ok_made, ok_summed, row0_made, table_saved0,
                 table_saved1, scaled) = sems(
                    s, "x_cleared", "x_loaded", "up_loaded", "wout_loaded", "small_loaded",
                    "dst_loaded", "y_loaded", "blocks_cleared", "mlp_loaded",
                    "ident_step", "ident_made", "ones_made", "iota_made", "stats_done",
                    "sqrt_done", "chain1", "xn_made", "transposed", "xT_made", "up_done",
                    "up_copied", "first_ready", "ok_made", "ok_summed", "row0_made",
                    "table_saved0", "table_saved1", "scaled")
                table_saved = [table_saved0, table_saved1]
                block = s.enter_context(nc.Block())

                @block.sync
                def _(sp):
                    sp.dma_start(X[:, 0:NODE_TILES - 1, :],
                                 x[0:(NODE_TILES - 1) * P, :].rearrange("(t p) d -> p t d", p=P)
                                 ).then_inc(x_loaded, 16)
                    sp.wait_ge(x_cleared, 1)
                    sp.dma_start(X[0:LAST_ROWS, NODE_TILES - 1, :], x[(NODE_TILES - 1) * P:NODES, :]
                                 ).then_inc(x_loaded, 16)
                    sp.dma_start(wup0[:], w_up0).then_inc(up_loaded, 16)
                    sp.dma_start(wup1[:], w_up1).then_inc(up_loaded, 16)
                    sp.dma_start(wout0[:], w_out0.rearrange("(k p) v -> p k v", p=P)
                                 ).then_inc(wout_loaded, 16)
                    sp.dma_start(wout1[:], w_out1.rearrange("(k p) v -> p k v", p=P)
                                 ).then_inc(small_loaded, 16)
                    sp.dma_start(wg[:], w_g.rearrange("(k p) e -> p k e", p=P)
                                 ).then_inc(small_loaded, 16)
                    sp.dma_start(b2[:], b_2).then_inc(small_loaded, 16)
                    sp.dma_start(src_sb[:], src).then_inc(small_loaded, 16)
                    sp.wait_ge(blocks_cleared, 2)
                    for h in range(2):
                        r, c = h * BASIS, h * HIDDEN
                        sp.dma_start(wm1[r:r + BASIS, c:c + HIDDEN], w_mlp1).then_inc(mlp_loaded, 16)
                        sp.dma_start(wm2[c:c + HIDDEN, c:c + HIDDEN], w_mlp2).then_inc(mlp_loaded, 16)
                        for d in range(2):
                            sp.dma_start(wm3[c:c + HIDDEN, d * HIDDEN:(d + 1) * HIDDEN], w_mlp3
                                         ).then_inc(mlp_loaded, 16)
                        sp.dma_start(wm4[c:c + HIDDEN, :], w_mlp4).then_inc(mlp_loaded, 16)
                    for t in range(NODE_TILES):
                        sp.wait_ge(up_copied, t + 1)
                        sp.dma_start(table[t * P:t * P + rows(t), :],
                                     up[0:rows(t), t % 2].rearrange("p c v -> p (c v)")
                                     ).then_inc(table_saved[t % 2], 16)
                    sp.wait_ge(small_loaded, 64)
                    sp.wait_ge(mlp_loaded, 160)
                    for k in range(2):
                        sp.wait_ge(table_saved[k], 16 * (NODE_TILES // 2))

                @block.scalar
                def _(act):
                    act.dma_start(dst_i[:], dst).then_inc(dst_loaded, 16)
                    act.dma_start(y_sb[:].rearrange("p t m -> p (t m)"), edge_y).then_inc(y_loaded, 16)
                    act.wait_ge(stats_done, 1)
                    act.activation(rstd[:], mv[:, :, 1], ACT.Sqrt, bias=eps[:, 0:1]).then_inc(sqrt_done, 1)
                    for t in range(NODE_TILES):
                        act.wait_ge(transposed, t + 1)
                        if t >= 2:
                            act.wait_ge(up_done, t - 1)
                        act.activation(xT[:, t % 2], pT[t % 2][:], ACT.Copy).then_inc(xT_made, 1)
                        act.wait_ge(up_done, t + 1)
                        if t >= 2:
                            act.wait_ge(table_saved[t % 2], 16 * (t // 2))
                        act.activation(up[:, t % 2], pU[t % 2][:], ACT.Copy,
                                       scale=SILU_2MOM / HIDDEN ** 0.5 / MUL ** 0.5
                                       ).then_inc(up_copied, 1)
                    act.wait_ge(y_loaded, 16)

                @block.gpsimd
                def _(pool):
                    pool.memset(ident[:], 0.0).then_inc(ident_step, 1)
                    pool.memset(wm1[:], 0.0).then_inc(blocks_cleared, 1)
                    pool.memset(wm2[:], 0.0).then_inc(blocks_cleared, 1)
                    pool.wait_ge(ident_step, 1)
                    pool.affine_select(out=ident[:], in_=ident[:], compare_op=ALU.not_equal, fill=1.0,
                                       base=0, pattern=[[-1, P]], channel_multiplier=1
                                       ).then_inc(ident_made, 1)
                    pool.iota(iota_i[:], pattern=[[1, WINDOW]], base=0, channel_multiplier=0
                              ).then_inc(iota_made, 1)
                    for g in range(4):
                        pool.wait_ge(iota_made, g + 1)
                        pool.iota(row0[32 * g:32 * g + 32, :], pattern=[[1, 1]], base=g * ACC_ROWS,
                                  channel_multiplier=1).then_inc(iota_made, 1)

                @block.vector
                def _(dve):
                    chain = Chain(dve, chain1)
                    dve.memset(X[:, NODE_TILES - 1, :], 0.0).then_inc(x_cleared, 1)
                    dve.memset(ones[:], 1.0).then_inc(ones_made, 1)
                    chain.link(dve.memset(eps[:], EPS))
                    dve.wait_ge(x_loaded, 32)
                    for t in range(NODE_TILES):
                        dve.bn_stats(stats[:, t, :], X[:, t, :]).then_inc(chain1, 1)
                        chain.n += 1
                    for t in range(NODE_TILES):
                        dve.wait_ge(chain1, 2 + t)
                        ins = dve.bn_aggr(mv[:, t, :], stats[:, t, :])
                    ins.then_inc(stats_done, 1)
                    dve.wait_ge(sqrt_done, 1)
                    chain.link(dve.reciprocal(rstd[:], rstd[:]))
                    for t in range(NODE_TILES):
                        if t >= 2:
                            dve.wait_ge(transposed, t - 1)
                        dve.tensor_scalar(xn[:, t % 2, :], X[:, t, :], mv[:, t, 0:1], rstd[:, t:t + 1],
                                          ALU.subtract, ALU.mult).then_inc(xn_made, 1)
                    dve.wait_ge(wout_loaded, 32 - 16)
                    dve.tensor_scalar(wout0[:, 1, :], wout0[:, 1, :], 1.0 / SQRT3, None, ALU.mult
                                      ).then_inc(scaled, 1)
                    dve.wait_ge(dst_loaded, 16)
                    dve.tensor_copy(dst_f[:], dst_i[:]).then_inc(row0_made, 1)
                    dve.wait_ge(first_ready, 1)
                    chain.link(dve.tensor_copy(first[:], pF[:]))
                    blocks3 = lambda a: a.rearrange("p (b k) -> p b k", k=BLOCK_TILES)
                    wide = first[:, :, None].broadcast_to((P, BLOCKS, BLOCK_TILES))
                    chain.link(dve.tensor_tensor(blocks3(rel[:]), blocks3(dst_f[:]), wide, ALU.subtract))
                    chain.link(dve.tensor_reduce(hilo[:, 0:1], rel[:], AX.X, ALU.max))
                    chain.link(dve.tensor_reduce(hilo[:, 1:2], rel[:], AX.X, ALU.min))
                    chain.link(dve.tensor_scalar(hilo[:, 0:1], hilo[:, 0:1], float(WINDOW - 1), None,
                                                 ALU.is_le))
                    chain.link(dve.tensor_scalar(hilo[:, 1:2], hilo[:, 1:2], 0.0, None, ALU.is_ge))
                    dve.tensor_tensor(hilo[:, 2:3], hilo[:, 0:1], hilo[:, 1:2], ALU.mult
                                      ).then_inc(ok_made, 1)
                    dve.wait_ge(ok_summed, 1)
                    chain.link(dve.tensor_scalar(hilo[:, 3:4], pC[:], float(P), None, ALU.is_equal))
                    fits = hilo[:, 3:4]
                    chain.link(dve.tensor_scalar(first[:], first[:], fits, None, ALU.mult))
                    chain.link(dve.tensor_tensor(blocks3(dst_f[:]), blocks3(dst_f[:]), wide, ALU.subtract))
                    dve.wait_ge(iota_made, 5)
                    chain.link(dve.tensor_copy(row0f[:], row0[:]))
                    chain.link(dve.tensor_scalar(sum_row[:], first[:], row0f[:, 0:1], None, ALU.add))
                    chain.link(dve.tensor_scalar(window_step[:], fits, -float(WINDOW), float(WINDOW),
                                                 ALU.mult, ALU.add))
                    chain.link(dve.tensor_scalar(npass_i[:], fits, 1.0 - PASSES, float(PASSES),
                                                 ALU.mult, ALU.add))
                    chain.link(dve.tensor_copy(window_iota[:], iota_i[:]))
                    dve.wait_ge(mlp_loaded, 160)
                    chain.link(dve.tensor_copy(wm4_hi[:], wm4[:]))
                    chain.link(dve.tensor_tensor(wm4_lo[:], wm4[:], wm4_hi[:].bitcast(fp32), ALU.subtract))

                @block.tensor
                def _(pe):
                    pe.wait_ge(ones_made, 1)
                    pe.wait_ge(ident_made, 1)
                    pe.wait_ge(up_loaded, 32)

                    def transpose(t):
                        pe.wait_ge(xn_made, t + 1)
                        if t >= 2:
                            pe.wait_ge(xT_made, t - 1)
                        v = xn[:, t % 2, MUL:].rearrange("p (u m) -> p m u", m=3)
                        pe.transpose(pT[t % 2][:, 0], xn[:, t % 2, 0:MUL], ident[:])
                        for m in range(3):
                            ins = pe.transpose(pT[t % 2][:, 1 + m], v[:, m], ident[:])
                        ins.then_inc(transposed, 1)

                    def project(t):
                        pe.wait_ge(xT_made, t + 1)
                        if t >= 2:
                            pe.wait_ge(up_copied, t - 1)
                        for c in range(4):
                            ins = pe.matmul(pU[t % 2][:, c], xT[:, t % 2, c], (wup0 if c == 0 else wup1)[:],
                                            start=True, stop=True)
                        ins.then_inc(up_done, 1)

                    transpose(0)
                    for t in range(NODE_TILES):
                        if t + 1 < NODE_TILES:
                            transpose(t + 1)
                        project(t)
                    pe.wait_ge(row0_made, 1)
                    pe.matmul(pF[:], ones[0:1, :], dst_f[0:1, 0:TILES:BLOCK_TILES], start=True, stop=True
                              ).then_inc(first_ready, 1)
                    pe.wait_ge(ok_made, 1)
                    pe.matmul(pC[:], ones[:], hilo[:, 2:3], start=True, stop=True).then_inc(ok_summed, 1)

            with ExitStack() as s:
                ef = sb(s, "ef", [2 * BASIS, HALF])
                h = [sb(s, f"h{k}", [2 * HIDDEN, HALF]) for k in range(2)]
                h3 = [sb(s, f"h3_{k}", [2 * HIDDEN, HALF], f32r) for k in range(2)]
                h3_full = [sb(s, f"h3_full{k}", [2 * HIDDEN, HALF]) for k in range(2)]
                zeros = sb(s, "zeros", [P, CLEAR_MAX])
                gidx = sb(s, "gidx", [P, ITER_TILES], i32)
                S = sb(s, "S", [P, ITER_TILES, 4, MUL])
                M = sb(s, "M", [P, 3, 8, MUL])
                eq = sb(s, "eq", [P, 2, BLOCK_TILES, WINDOW])
                hot = sb(s, "hot", [P, 2, BLOCK_TILES, 4, WINDOW])
                sums = sb(s, "sums", [P, 2, ACC_COLS])
                fidx_f = sb(s, "fidx_f", [P, 2])
                fidx = sb(s, "fidx", [P, 2], i32)
                pass_row = sb(s, "pass_row", [P, 1])
                pW = [ps(s, f"pW{k}", [P, 4, MUL]) for k in range(3)]
                pZ = [ps(s, f"pZ{k}", [P, HALF]) for k in range(3)]
                pA = [ps(s, f"pA{k}", [P, ACC_COLS]) for k in range(2)]
                (ef_loaded, z_ready, h_ready, w_ready, product, scattered, hot_step, hot_ready,
                 sums_copied, parts_ready, zeroed, acc_cleared, slot_cleared, idx_made, fidx_step, fidx_made, pass_step,
                 window_moved) = sems(
                    s, "ef_loaded", "z_ready", "h_ready", "w_ready", "product", "scattered",
                    "hot_step", "hot_ready", "sums_copied", "parts_ready", "zeroed",
                    "acc_cleared", "slot_cleared", "idx_made", "fidx_step",
                    "fidx_made", "pass_step", "window_moved")
                gathered = sems(s, *[f"gathered{j}" for j in range(ITER_TILES)])
                flushed = sems(s, "flushed0", "flushed1")
                block = s.enter_context(nc.Block())
                RING = 3

                def passes(eng):
                    return eng.value_load(npass_i[0:1, 0:1], min_val=1, max_val=PASSES)

                @block.sync
                def _(sp):
                    n = passes(sp)
                    sp.dma_start(ef[:], edge_f[0]).then_inc(ef_loaded, 16)
                    sp.wait_ge(zeroed, 1)
                    for part, done in ((acc, acc_cleared), (slots, slot_cleared)):
                        flat = part.rearrange("r c -> (r c)").rearrange("(p n) -> p n", p=P)
                        for a in range(0, flat.shape[1], CLEAR_MAX):
                            b = min(a + CLEAR_MAX, flat.shape[1])
                            sp.dma_start(flat[:, a:b], zeros[:, 0:b - a]).then_inc(done, 16)
                    sp.wait_ge(z_ready, 1)
                    sp.dma_start(ef[:], edge_f[1]).then_inc(ef_loaded, 16)
                    sp.wait_ge(z_ready, 5)
                    sp.dma_start(ef[:], edge_f[2]).then_inc(ef_loaded, 16)
                    with sp.Fori(0, n) as p:
                        with sp.Fori(0, ITERS) as i:
                            g = p * ITERS + i
                            sp.wait_ge(z_ready, g * 4 + 9)
                            sp.dma_start(ef[:], edge_f[bass.ds(i + 3, 1)].rearrange("o r n -> (o r) n")
                                         ).then_inc(ef_loaded, 16)
                    sp.wait_ge(ef_loaded, n * (16 * ITERS) + 48)
                    sp.nop(nofuse=True)
                    sp.wait_ge(slot_cleared, 16 * (-(-SLOT_ROWS * DIM // P // CLEAR_MAX)))

                @block.scalar
                def _(act):
                    n = passes(act)
                    act.sem_inc(sums_copied, 2)

                    def silu(layer, z):
                        act.wait_ge(z_ready, z)
                        scale = (1.0 / BASIS ** 0.5, SILU_2MOM / HIDDEN ** 0.5, SILU_2MOM / HIDDEN ** 0.5)
                        act.activation(h[layer][:], pZ[layer % 2][:], ACT.Silu, scale=scale[layer]
                                       ).then_inc(h_ready, 1)

                    def copy_sums(g, k):
                        act.wait_ge(scattered, g * ITER_TILES + (ITER_TILES + BLOCK_TILES * (k + 1)))
                        act.wait_ge(flushed[k], g * 16 + 16)
                        act.activation(sums[:, k, 0:2 * MUL], pA[k][:, 0:2 * MUL], ACT.Copy)
                        act.activation(sums[0:64, k, 2 * MUL:], pA[k][0:64, 2 * MUL:], ACT.Copy
                                       ).then_inc(sums_copied, 1)

                    def silu_parts(q, z):
                        act.wait_ge(z_ready, z)
                        scale = SILU_2MOM / HIDDEN ** 0.5
                        act.activation(h3[q][:], pZ[2 * (1 - q)][:], ACT.Silu, scale=scale)
                        act.activation(h3_full[q][HIDDEN:], pZ[2 * (1 - q)][HIDDEN:], ACT.Silu, scale=scale
                                       ).then_inc(h_ready, 1)

                    silu(0, 1)
                    silu(1, 2)
                    silu_parts(0, 3)
                    silu_parts(1, 4)
                    silu(0, 5)
                    silu(1, 6)
                    with act.Fori(0, n) as p:
                        with act.Fori(0, ITERS) as i:
                            g = p * ITERS + i
                            for q in range(2):
                                act.wait_ge(w_ready, g * ITER_TILES + BLOCK_TILES * (q + 1))
                                silu_parts(q, g * 4 + (7 + q))
                                if q == 0:
                                    copy_sums(g, 0)
                            silu(0, g * 4 + 9)
                            silu(1, g * 4 + 10)
                            copy_sums(g, 1)

                @block.gpsimd
                def _(pool):
                    n = passes(pool)
                    pool.memset(zeros[:], 0.0).then_inc(zeroed, 1)
                    pool.memset(pass_row[:], 0.0).then_inc(pass_step, 1)

                    def gather(j):
                        pool.indirect_dma_start(
                            S[:, j].rearrange("p c u -> p (c u)"), None, table,
                            bass.IndirectOffsetOnAxis(ap=gidx[:, j:j + 1], axis=0)
                        ).then_inc(gathered[j], 16)

                    for k in range(2):
                        half = slice(BLOCK_TILES * k, BLOCK_TILES * (k + 1))
                        pool.tensor_copy(gidx[:, half], src_sb[:, half]).then_inc(idx_made, 1)
                    pool.wait_ge(idx_made, 2)
                    for j in range(ITER_TILES):
                        gather(j)
                    pool.wait_ge(acc_cleared, 16 * (-(-4 * ACC_ROWS * ACC_COLS // P // CLEAR_MAX)))
                    for k in range(2):
                        pool.dma_start(sums[:, k], acc[0:P, :]).then_inc(flushed[k], 16)
                    for k in range(2):
                        pool.wait_ge(flushed[k], 16)
                    with pool.Fori(0, n) as p:
                        with pool.Fori(0, ITERS) as i:
                            g = p * ITERS + i
                            g6 = g * ITER_TILES
                            for k in range(2):
                                for j in range(BLOCK_TILES * k, BLOCK_TILES * (k + 1)):
                                    pool.wait_ge(gathered[j], g * 16 + 16)
                                pool.nop(nofuse=True)
                                pool.tensor_copy(
                                    gidx[:, BLOCK_TILES * k:BLOCK_TILES * (k + 1)],
                                    src_sb[:, bass.ds(i * ITER_TILES + (ITER_TILES + BLOCK_TILES * k),
                                                      BLOCK_TILES)]).then_inc(idx_made, 1)
                                pool.wait_ge(idx_made, g * 2 + (k + 3))
                                for j in range(BLOCK_TILES * k, BLOCK_TILES * (k + 1)):
                                    pool.wait_ge(product, g6 + (RING + j + 1))
                                    pool.nop(nofuse=True)
                                    gather(j)
                                pool.wait_ge(pass_step, p + 1)
                                pool.tensor_tensor(fidx_f[:, k:k + 1],
                                                   sum_row[:, bass.ds(i * 2 + k, 1)],
                                                   pass_row[:], ALU.add).then_inc(fidx_step, 1)
                                pool.wait_ge(fidx_step, g * 2 + (k + 1))
                                pool.nop(nofuse=True)
                                pool.tensor_copy(fidx[:, k:k + 1], fidx_f[:, k:k + 1]
                                                 ).then_inc(fidx_made, 1)
                                pool.wait_ge(fidx_made, g * 2 + (k + 1))
                                if k == 0:
                                    pool.wait_ge(flushed[1], g * 16 + 16)
                                else:
                                    pool.wait_ge(flushed[0], g * 16 + 32)
                                pool.wait_ge(sums_copied, g * 2 + (k + 3))
                                pool.nop(nofuse=True)
                                pool.indirect_dma_start(
                                    acc, bass.IndirectOffsetOnAxis(ap=fidx[:, k:k + 1], axis=0),
                                    sums[:, k], None, compute_op=ALU.add).then_inc(flushed[k], 16)
                        pool.tensor_tensor(pass_row[:], pass_row[:], window_step[:], ALU.add
                                           ).then_inc(pass_step, 1)
                    for j in range(ITER_TILES):
                        pool.wait_ge(gathered[j], n * (16 * ITERS) + 16)
                    for k in range(2):
                        pool.wait_ge(flushed[k], n * (16 * ITERS) + 16)

                @block.vector
                def _(dve):
                    n = passes(dve)
                    dve.sem_inc(product, RING)

                    def receivers(g, i, k):
                        tiles = bass.ds(i * ITER_TILES + BLOCK_TILES * k, BLOCK_TILES)
                        dve.wait_ge(scattered, g * ITER_TILES + BLOCK_TILES * (k + 1))
                        dve.tensor_tensor(
                            eq[:, k], dst_f[:, tiles, None].broadcast_to((P, BLOCK_TILES, WINDOW)),
                            window_iota[:, None, :].broadcast_to((P, BLOCK_TILES, WINDOW)),
                            ALU.is_equal).then_inc(hot_step, 1)

                    def one_hots(g, i, k):
                        tiles = bass.ds(i * ITER_TILES + BLOCK_TILES * k, BLOCK_TILES)
                        dve.wait_ge(hot_step, g * 2 + (k + 1))
                        dve.tensor_tensor(
                            hot[:, k],
                            eq[:, k, :, None, :].broadcast_to((P, BLOCK_TILES, 4, WINDOW)),
                            y_sb[:, tiles, :, None].broadcast_to((P, BLOCK_TILES, 4, WINDOW)),
                            ALU.mult).then_inc(hot_ready, 1)

                    def products(g, g6, j):
                        W, m = pW[j % 3], M[:, j % 3]
                        dve.wait_ge(w_ready, g6 + (j + 1))
                        dve.wait_ge(gathered[j], g * 16 + 16)
                        dve.wait_ge(scattered, g6 + (j + 1 + ITER_TILES - RING))
                        dve.tensor_tensor(m[:, 0:2], W[:, 0:2],
                                          S[:, j, 0:1].broadcast_to((P, 2, MUL)), ALU.mult)
                        dve.tensor_tensor(
                            m[:, 2:8].rearrange("p (a b) u -> p a b u", a=2),
                            W[:, 2:4, None, :].broadcast_to((P, 2, 3, MUL)),
                            S[:, j, None, 1:4].broadcast_to((P, 2, 3, MUL)), ALU.mult
                        ).then_inc(product, 1)

                    def parts(q, count):
                        dve.wait_ge(h_ready, count)
                        dve.tensor_tensor(h3[q][HIDDEN:], h3_full[q][HIDDEN:],
                                          h3[q][HIDDEN:].bitcast(fp32), ALU.subtract
                                          ).then_inc(parts_ready, 1)

                    parts(0, 3)
                    parts(1, 4)
                    with dve.Fori(0, n) as p:
                        with dve.Fori(0, ITERS) as i:
                            g = p * ITERS + i
                            g6 = g * ITER_TILES
                            receivers(g, i, 0)
                            products(g, g6, 0)
                            one_hots(g, i, 0)
                            products(g, g6, 1)
                            receivers(g, i, 1)
                            products(g, g6, 2)
                            one_hots(g, i, 1)
                            parts(0, g * 4 + 7)
                            products(g, g6, 3)
                            products(g, g6, 4)
                            products(g, g6, 5)
                            parts(1, g * 4 + 8)
                        dve.tensor_scalar(window_iota[:], window_iota[:], window_step[:, 0:1], None,
                                          ALU.add).then_inc(window_moved, 1)
                        dve.wait_ge(window_moved, p + 1)

                @block.tensor
                def _(pe):
                    n = passes(pe)
                    pe.sem_inc(scattered, ITER_TILES)

                    def mlp(layer, done, chunk=None, half=None):
                        if layer == 0:
                            pe.wait_ge(ef_loaded, chunk)
                        if done is not None:
                            pe.wait_ge(h_ready, done)
                        if layer < 2:
                            pe.matmul(pZ[layer][:], (wm1, wm2)[layer][:], (ef, h[0])[layer][:],
                                      start=True, stop=True).then_inc(z_ready, 1)
                            return
                        for q in (0, 1) if half is None else (half,):
                            r = HIDDEN * q
                            pe.matmul(pZ[2 * (1 - q)][:], wm3[r:r + HIDDEN, :], h[1][r:r + HIDDEN, :],
                                      start=True, stop=True).then_inc(z_ready, 1)

                    def edge_weights(j, free):
                        pe.wait_ge(product, free)
                        q, c = j // BLOCK_TILES, P * (j % BLOCK_TILES)
                        for n, w in enumerate((wm4_hi, wm4_lo)):
                            ins = pe.matmul(pW[j % 3][:].rearrange("p c u -> p (c u)"),
                                            h3[q][:, c:c + P], w[:], start=n == 0, stop=n == 1)
                        ins.then_inc(w_ready, 1)

                    def scatter(g, g6, j):
                        k, t = j // BLOCK_TILES, j % BLOCK_TILES
                        if t == 0:
                            pe.wait_ge(hot_ready, g * 2 + (k + 1))
                            pe.wait_ge(sums_copied, g * 2 + (k + 1))
                        pe.wait_ge(product, g6 + (j + 1 + RING))
                        A, m, first, last = pA[k], M[:, j % 3], t == 0, t == BLOCK_TILES - 1
                        for grp, y, units, c in ((0, 0, (0, 2), 0), (1, 0, (3, 4), 0), (2, 1, (1, 5), 0),
                                                 (3, 2, (1, 6), 0), (0, 3, (1,), 2), (1, 3, (7,), 2)):
                            lo = 32 * grp
                            if len(units) == 2:
                                mov = m[:, units[0]:units[1] + 1:units[1] - units[0]]
                            else:
                                mov = m[:, units[0]:units[0] + 1]
                            ins = pe.matmul(A[lo:lo + 32, c * MUL:(c + len(units)) * MUL],
                                            hot[:, k, t, y], mov, start=first and c == 0, stop=last,
                                            skip_group_check=True)
                        ins.then_inc(scattered, 1)

                    for layer in range(3):
                        mlp(layer, layer or None, 16)
                    mlp(0, 4, 32)
                    mlp(1, 5)
                    pe.wait_ge(parts_ready, 1)
                    edge_weights(0, 1)
                    edge_weights(1, 2)
                    with pe.Fori(0, n) as p:
                        with pe.Fori(0, ITERS) as i:
                            g = p * ITERS + i
                            g6 = g * ITER_TILES
                            for j in range(ITER_TILES):
                                nxt = j + 2
                                if nxt % BLOCK_TILES == 0:
                                    pe.wait_ge(parts_ready, g * 2 + (nxt // BLOCK_TILES + 1))
                                edge_weights(nxt % ITER_TILES, g6 + (nxt + 1))
                                scatter(g, g6, j)
                                if j == 0:
                                    mlp(2, g * 4 + 6, half=0)
                                elif j == 2:
                                    mlp(2, g * 4 + 6, half=1)
                                elif j == 4:
                                    mlp(0, g * 4 + 8, g * 16 + 48)
                                elif j == 5:
                                    mlp(1, g * 4 + 9)

        prob = sb(ctx, "prob", [P, NODE_TILES, 2])
        gates = sb(ctx, "gates", [P, NODE_TILES, EXPERTS])
        slot_i = sb(ctx, "slot_i", [P, NODE_TILES, 2], i32)
        expert_i = sb(ctx, "expert_i", [P, SLOT_BLOCKS + 1], i32)
        blocks_i = sb(ctx, "blocks_i", [P, 1], i32)

        expert_stack = ctx.enter_context(ExitStack())
        raw1 = sb(expert_stack, "raw1", [P, CHUNKS, KC, CHUNK * P])
        raw2 = sb(expert_stack, "raw2", [P, CHUNKS, CHUNK, DIM])
        w1_hi = sb(expert_stack, "w1_hi", [P, CHUNKS, KC, CHUNK * P], f32r)
        w1_lo = sb(expert_stack, "w1_lo", [P, CHUNKS, KC, CHUNK * P], f32r)
        w2_hi = sb(expert_stack, "w2_hi", [P, CHUNKS, CHUNK, DIM], f32r)
        w2_lo = sb(expert_stack, "w2_lo", [P, CHUNKS, CHUNK, DIM], f32r)
        b1 = sb(expert_stack, "b1", [P, HC])
        raw_loaded = sems(expert_stack, *[f"raw_loaded{j}" for j in range(CHUNKS)])
        b1_loaded, upper_made, split = sems(expert_stack, "b1_loaded", "upper_made", "split")

        def load_chunk(e, j):
            sp = nc.sync
            sp.dma_start(raw1[:, j],
                         w_1[bass.ds(e, 1)].rearrange("o (c p) h -> p (o c) h", p=P)
                         [:, :, j * CHUNK * P:(j + 1) * CHUNK * P]).then_inc(raw_loaded[j], 16)
            sp.dma_start(raw2[:, j],
                         w_2[bass.ds(e, 1)].rearrange("o (c p) h -> p (o c) h", p=P)
                         [:, j * CHUNK:(j + 1) * CHUNK]).then_inc(raw_loaded[j], 16)

        def load_bias(e):
            nc.sync.dma_start(b1[:], b_1[bass.ds(e, 1)].rearrange("o p c -> (o p) c")
                              ).then_inc(b1_loaded, 16)

        def make_upper(b, j):
            act = nc.scalar
            act.wait_ge(raw_loaded[j], b * 32 + 32)
            act.activation(w1_hi[:, j], raw1[:, j], ACT.Copy)
            act.activation(w2_hi[:, j], raw2[:, j], ACT.Copy).then_inc(upper_made, 1)

        def make_lower(b, j):
            pool = nc.gpsimd
            pool.wait_ge(upper_made, b * CHUNKS + (j + 1))
            pool.nop(nofuse=True)
            pool.tensor_tensor(w1_lo[:, j], raw1[:, j], w1_hi[:, j].bitcast(fp32), ALU.subtract)
            pool.tensor_tensor(w2_lo[:, j], raw2[:, j], w2_hi[:, j].bitcast(fp32), ALU.subtract
                               ).then_inc(split, 1)

        with ExitStack() as s:
            A_RING = 3
            xn2 = sb(s, "xn2", [P, NODE_TILES, DIM])
            A = sb(s, "A", [P, A_RING, 4, ACC_COLS])
            msgT = sb(s, "msgT", [P, 2, 8, P])
            x2T = sb(s, "x2T", [P, 2, KC, P])
            stats = sb(s, "stats2", [P, 2, 6])
            mv = sb(s, "mv2", [P, 2, 2])
            rstd = sb(s, "rstd2", [P, 2])
            top = sb(s, "top", [P, NODE_TILES])
            esum = sb(s, "esum", [P, NODE_TILES])
            ex = sb(s, "ex", [P, NODE_TILES, EXPERTS])
            left = sb(s, "left", [P, NODE_TILES, EXPERTS])
            place = sb(s, "place", [P, NODE_TILES])
            found = sb(s, "found", [P, NODE_TILES, EXPERTS])
            mask = sb(s, "mask", [P, 2, NODE_TILES, EXPERTS])
            mask12 = sb(s, "mask12", [P, NODE_TILES, EXPERTS])
            order_i = sb(s, "order_i", [P, EXPERTS], i32)
            order = sb(s, "order", [P, EXPERTS])
            node_i = sb(s, "node_i", [P, NODE_TILES], i32)
            valid = sb(s, "valid", [P, NODE_TILES])
            before = sb(s, "before", [P, P])
            run = sb(s, "run", [P, NODE_TILES + 1, EXPERTS])
            rank = sb(s, "rank", [P, NODE_TILES, EXPERTS])
            thr_i = sb(s, "thr_i", [P, MAX_BLOCKS], i32)
            thr = sb(s, "thr", [P, MAX_BLOCKS])
            over = sb(s, "over", [P, EXPERTS, MAX_BLOCKS])
            blk_i = sb(s, "blk_i", [P, SLOT_BLOCKS + 1], i32)
            blk = sb(s, "blk", [P, SLOT_BLOCKS + 1])
            passed = sb(s, "passed", [P, SLOT_BLOCKS + 1, EXPERTS - 1])
            expert_f = sb(s, "expert_f", [P, SLOT_BLOCKS + 1])
            nblk = sb(s, "nblk", [P, EXPERTS])
            end = sb(s, "end", [P, EXPERTS + 1])
            base = sb(s, "base", [P, EXPERTS])
            slot_f = sb(s, "slot_f", [P, NODE_TILES, 2])
            picked = sb(s, "picked", [P, 2, NODE_TILES, EXPERTS])
            pM = [ps(s, f"pM{k}", [P, 4, P]) for k in range(2)]
            pO = [ps(s, f"pO{k}", [P, 4, MUL]) for k in range(2)]
            pX = [ps(s, f"pX{k}", [P, KC, P]) for k in range(2)]
            pL = ps(s, "pL", [P, NODE_TILES, EXPERTS])
            pR = ps(s, "pR", [P, 2, NODE_TILES, EXPERTS])
            (iota_made, sums_added, msg_transposed, msg_copied, out_done, chain3, stats_made,
             sqrt_ready, sqrt_done, xn_made, x_transposed, x_copied, logits, shifted, exp_done,
             masks_made, ranked, slots_made, scattered) = sems(
                s, "iota3_made", "sums_added", "msg_transposed", "msg_copied", "out_done", "chain3",
                "stats_made", "sqrt_ready3", "sqrt_done3", "xn_made3", "x_transposed", "x_copied",
                "logits", "shifted", "exp_done", "masks_made", "ranked", "slots_made",
                "rows_scattered")
            acc_loaded = sems(s, *[f"acc_loaded{k}" for k in range(A_RING)])
            block = s.enter_context(nc.Block())
            STEPS = NODE_TILES + 3

            def stage(step, lag):
                t = step - lag
                return t if 0 <= t < NODE_TILES else None

            @block.sync
            def _(sp):
                for t in range(NODE_TILES):
                    if t >= A_RING:
                        sp.wait_ge(msg_transposed, 2 * (t - A_RING + 1))
                    sp.dma_start(A[:, t % A_RING],
                                 acc.rearrange("(g n) c -> n g c", g=4)[t * P:(t + 1) * P]
                                 ).then_inc(acc_loaded[t % A_RING], 16)
                    if t == A_RING:
                        load_chunk(0, 0)
                        load_chunk(0, 1)
                    elif t == 2 * A_RING:
                        load_chunk(0, 2)
                        load_chunk(0, 3)
                load_bias(0)

            @block.gpsimd
            def _(pool):
                pool.affine_select(out=before[:], in_=ones[:], compare_op=ALU.is_gt, fill=0.0, base=0,
                                   pattern=[[1, P]], channel_multiplier=-1).then_inc(iota_made, 1)
                pool.iota(order_i[:], pattern=[[-1, EXPERTS]], base=EXPERTS, channel_multiplier=0
                          ).then_inc(iota_made, 1)
                pool.iota(node_i[:], pattern=[[P, NODE_TILES]], base=0, channel_multiplier=1
                          ).then_inc(iota_made, 1)
                pool.iota(thr_i[:], pattern=[[BLOCK_ROWS, MAX_BLOCKS]], base=0, channel_multiplier=0
                          ).then_inc(iota_made, 1)
                pool.iota(blk_i[:], pattern=[[1, SLOT_BLOCKS + 1]], base=0, channel_multiplier=0
                          ).then_inc(iota_made, 1)
                for j in range(CHUNKS):
                    make_lower(0, j)
                pool.wait_ge(slots_made, 1)
                for t in range(NODE_TILES):
                    for q in range(2):
                        pool.indirect_dma_start(
                            slots, bass.IndirectOffsetOnAxis(ap=slot_i[0:rows(t), t, q:q + 1], axis=0),
                            xn2[0:rows(t), t, :], None).then_inc(scattered, 16)
                pool.wait_ge(scattered, 16 * 2 * NODE_TILES)

            @block.tensor
            def _(pe):
                for step in range(STEPS):
                    t = stage(step, 0)
                    if t is not None:
                        a = A[:, t % A_RING]
                        pe.wait_ge(sums_added, t + 1)
                        parts = [a[:, 0, 0:P], a[:, 1, 2 * P:],
                                 a[:, 2, 0:P], a[:, 0, P:2 * P], a[:, 3, 0:P], a[:, 1, 0:P],
                                 a[:, 0, 2 * P:], a[:, 1, P:2 * P]]
                        for q in range(2):
                            if t >= 1:
                                pe.wait_ge(msg_copied, 2 * (t - 1) + q + 1)
                            for u in range(4):
                                ins = pe.transpose(pM[q][:, u], parts[4 * q + u], ident[:])
                            ins.then_inc(msg_transposed, 1)
                    t = stage(step, 1)
                    if t is not None:
                        pe.wait_ge(msg_copied, 2 * t + 2)
                        if t >= 2:
                            pe.wait_ge(sqrt_ready, t - 1)
                        for c in range(4):
                            w = wout0 if c == 0 else wout1
                            for q in range(2):
                                ins = pe.matmul(pO[t % 2][:, c], msgT[:, t % 2, 2 * c + q], w[:, q],
                                                start=q == 0, stop=q == 1)
                        ins.then_inc(out_done, 1)
                    t = stage(step, 2)
                    if t is not None:
                        pe.wait_ge(xn_made, t + 1)
                        if t >= 2:
                            pe.wait_ge(x_copied, t - 1)
                        for k in range(KC):
                            ins = pe.transpose(pX[t % 2][:, k], xn2[:, t, k * P:(k + 1) * P], ident[:])
                        ins.then_inc(x_transposed, 1)
                    t = stage(step, 3)
                    if t is not None:
                        pe.wait_ge(x_copied, t + 1)
                        for k in range(KC):
                            ins = pe.matmul(pL[:, t], x2T[:, t % 2, k], wg[:, k],
                                            start=k == 0, stop=k == KC - 1)
                        ins.then_inc(logits, 1)
                pe.wait_ge(iota_made, 1)
                pe.wait_ge(masks_made, 1)
                flat = mask12[:].rearrange("p t e -> p (t e)")
                pe.matmul(pR[:, 0].rearrange("p t e -> p (t e)"), before[:], flat, start=True, stop=True)
                pe.matmul(pR[:, 1].rearrange("p t e -> p (t e)"), ones[:], flat, start=True, stop=True
                          ).then_inc(ranked, 1)

            @block.scalar
            def _(act):
                for step in range(STEPS):
                    t = stage(step, 0)
                    if t is not None:
                        for q in range(2):
                            act.wait_ge(msg_transposed, 2 * t + q + 1)
                            if t >= 2 and q == 0:
                                act.wait_ge(out_done, t - 1)
                            act.activation(msgT[:, t % 2, 4 * q:4 * q + 4], pM[q][:], ACT.Copy
                                           ).then_inc(msg_copied, 1)
                    t = stage(step, 2)
                    if t is not None:
                        act.wait_ge(x_transposed, t + 1)
                        if t >= 2:
                            act.wait_ge(logits, t - 1)
                        act.activation(x2T[:, t % 2], pX[t % 2][:], ACT.Copy).then_inc(x_copied, 1)
                    t = stage(step, 1)
                    if t is not None:
                        act.wait_ge(sqrt_ready, t + 1)
                        if t >= 2:
                            act.wait_ge(xn_made, t - 1)
                        act.activation(rstd[:, t % 2:t % 2 + 1], mv[:, t % 2, 1:2], ACT.Sqrt,
                                       bias=eps[:, 0:1]).then_inc(sqrt_done, 1)
                    if step >= 4 and step % 2 == 0 and step // 2 - 2 < CHUNKS:
                        make_upper(0, step // 2 - 2)
                act.wait_ge(shifted, 1)
                act.activation(ex[:], ex[:], ACT.Exp).then_inc(exp_done, 1)

            @block.vector
            def _(dve):
                chain = Chain(dve, chain3)
                scale = 1.0 / (2 * MUL) ** 0.5 / NEIGHBORS

                def add_parts(t):
                    a = A[:, t % A_RING]
                    dve.wait_ge(acc_loaded[t % A_RING], 16 * (t // A_RING + 1))
                    chain.link(dve.tensor_tensor(a[:, 1, 2 * P:], a[:, 1, 2 * P:], a[:, 2, P:2 * P], ALU.add))
                    dve.tensor_tensor(a[:, 1, 2 * P:], a[:, 1, 2 * P:], a[:, 3, P:2 * P], ALU.add
                                      ).then_inc(sums_added, 1)

                add_parts(0)
                for step in range(STEPS):
                    t = stage(step, 2)
                    if t is not None:
                        dve.wait_ge(sqrt_done, t + 1)
                        r = rstd[:, t % 2:t % 2 + 1]
                        chain.link(dve.reciprocal(r, r))
                        dve.tensor_scalar(xn2[:, t, :], X[:, t, :], mv[:, t % 2, 0:1], r,
                                          ALU.subtract, ALU.mult).then_inc(xn_made, 1)
                    t = stage(step, -1)
                    if t is not None:
                        add_parts(t)
                    t = stage(step, 1)
                    if t is not None:
                        dve.wait_ge(out_done, t + 1)
                        o = pO[t % 2]
                        xv = X[:, t, MUL:].rearrange("p (u m) -> p m u", m=3)
                        dve.scalar_tensor_tensor(X[:, t, 0:MUL], o[:, 0], scale, X[:, t, 0:MUL],
                                                 ALU.mult, ALU.add)
                        chain.link(dve.scalar_tensor_tensor(xv, o[:, 1:4], scale, xv, ALU.mult, ALU.add))
                        dve.bn_stats(stats[:, t % 2], X[:, t, :]).then_inc(stats_made, 1)
                        if t >= 2:
                            dve.wait_ge(xn_made, t - 1)
                        dve.wait_ge(stats_made, t + 1)
                        dve.bn_aggr(mv[:, t % 2], stats[:, t % 2]).then_inc(sqrt_ready, 1)

                wide = lambda a: a[:, :, None].broadcast_to((P, NODE_TILES, EXPERTS))
                dve.wait_ge(iota_made, 5)
                chain.link(dve.tensor_copy(order[:], order_i[:]))
                chain.link(dve.tensor_copy(valid[:], node_i[:]))
                chain.link(dve.tensor_scalar(valid[:], valid[:], float(NODES), None, ALU.is_lt))
                chain.link(dve.tensor_copy(thr[:], thr_i[:]))
                chain.link(dve.tensor_copy(blk[:], blk_i[:]))
                chain.link(dve.memset(run[:, 0], 0.0))
                chain.link(dve.memset(end[:], 0.0))
                dve.wait_ge(logits, NODE_TILES)
                chain.link(dve.tensor_reduce(top[:], pL[:], AX.X, ALU.max))
                dve.tensor_tensor(ex[:], pL[:], wide(top), ALU.subtract).then_inc(shifted, 1)
                dve.wait_ge(exp_done, 1)
                chain.link(dve.tensor_reduce(esum[:], ex[:], AX.X, ALU.add))
                chain.link(dve.reciprocal(esum[:], esum[:]))
                chain.link(dve.tensor_tensor(ex[:], ex[:], wide(esum), ALU.mult))
                orders = order[:, None, :].broadcast_to((P, NODE_TILES, EXPERTS))
                for q, values in enumerate((ex, left)):
                    chain.link(dve.tensor_reduce(prob[:, :, q], values[:], AX.X, ALU.max))
                    chain.link(dve.tensor_tensor(found[:], values[:],
                                                 prob[:, :, q:q + 1].broadcast_to((P, NODE_TILES, EXPERTS)),
                                                 ALU.is_equal))
                    chain.link(dve.tensor_tensor(found[:], found[:], orders, ALU.mult))
                    chain.link(dve.tensor_reduce(place[:], found[:], AX.X, ALU.max))
                    chain.link(dve.tensor_tensor(mask[:, q], orders, wide(place), ALU.is_equal))
                    if q == 0:
                        chain.link(dve.scalar_tensor_tensor(left[:], mask[:, 0], -2.0, ex[:],
                                                            ALU.mult, ALU.add))
                chain.link(dve.tensor_tensor(mask12[:], mask[:, 0], mask[:, 1], ALU.add))
                chain.link(dve.tensor_tensor(gates[:], mask12[:], ex[:], ALU.mult))
                dve.tensor_tensor(mask12[:], mask12[:], wide(valid), ALU.mult).then_inc(masks_made, 1)
                dve.wait_ge(ranked, 1)
                for t in range(NODE_TILES):
                    chain.link(dve.tensor_tensor(run[:, t + 1], run[:, t], pR[:, 1, t], ALU.add))
                chain.link(dve.tensor_tensor(rank[:], pR[:, 0], run[:, 0:NODE_TILES], ALU.add))
                chain.link(dve.tensor_tensor(
                    over[:], run[:, NODE_TILES, :, None].broadcast_to((P, EXPERTS, MAX_BLOCKS)),
                    thr[:, None, :].broadcast_to((P, EXPERTS, MAX_BLOCKS)), ALU.is_gt))
                chain.link(dve.tensor_reduce(nblk[:], over[:], AX.X, ALU.add))
                chain.link(dve.tensor_scalar(nblk[:, 0:1], nblk[:, 0:1], 1.0, None, ALU.max))
                for e in range(EXPERTS):
                    chain.link(dve.tensor_tensor(end[:, e + 1:e + 2], end[:, e:e + 1], nblk[:, e:e + 1],
                                                 ALU.add))
                chain.link(dve.tensor_scalar(base[:], end[:, 0:EXPERTS], float(BLOCK_ROWS), None, ALU.mult))
                chain.link(dve.tensor_tensor(rank[:], rank[:],
                                             base[:, None, :].broadcast_to((P, NODE_TILES, EXPERTS)),
                                             ALU.add))
                for q in range(2):
                    chain.link(dve.tensor_tensor(picked[:, q], rank[:], mask[:, q], ALU.mult))
                    chain.link(dve.tensor_reduce(slot_f[:, :, q], picked[:, q], AX.X, ALU.add))
                dve.tensor_copy(slot_i[:], slot_f[:]).then_inc(slots_made, 1)
                chain.link(dve.tensor_tensor(
                    passed[:], blk[:, :, None].broadcast_to((P, SLOT_BLOCKS + 1, EXPERTS - 1)),
                    end[:, None, 1:EXPERTS].broadcast_to((P, SLOT_BLOCKS + 1, EXPERTS - 1)), ALU.is_ge))
                chain.link(dve.tensor_reduce(expert_f[:], passed[:], AX.X, ALU.add))
                chain.link(dve.tensor_copy(expert_i[:], expert_f[:]))
                chain.link(dve.tensor_copy(blocks_i[:], end[:, EXPERTS:]))

        with ExitStack() as s:
            xg = sb(s, "xg", [P, ROW_TILES, DIM])
            x_hi = sb(s, "x_hi", [P, KC, BLOCK_ROWS], f32r)
            x_lo = sb(s, "x_lo", [P, KC, BLOCK_ROWS], f32r)
            h_full = sb(s, "h_full", [P, 2, CHUNK, BLOCK_ROWS])
            h_hi = sb(s, "h_hi", [P, 2, CHUNK, BLOCK_ROWS], f32r)
            h_lo = sb(s, "h_lo", [P, 2, CHUNK, BLOCK_ROWS], f32r)
            yb = sb(s, "yb", [P, ROW_TILES, DIM])
            pX = [ps(s, f"pX4_{t}", [P, KC, P]) for t in range(ROW_TILES)]
            pH = [ps(s, f"pH{u}", [P, BLOCK_ROWS]) for u in range(CHUNK)]
            pY = [ps(s, f"pY{t}", [P, DIM]) for t in range(ROW_TILES)]
            (x_loaded, x_transposed, x_upper, x_ready, hidden, gelu_done, h_upper, h_ready, l2_done,
             y_copied, y_saved) = sems(
                s, "xg_loaded", "x_transposed4", "x_upper", "x_ready", "hidden", "gelu_done",
                "h_upper", "h_ready", "l2_done", "y_copied", "y_saved")
            block = s.enter_context(nc.Block())

            def over_blocks(eng, body):
                n = eng.value_load(blocks_i[0:1, 0:1], min_val=1, max_val=SLOT_BLOCKS)
                with eng.Fori(0, n) as b:
                    body(b)

            @block.sync
            def _(sp):
                def next_weights(b):
                    e = sp.value_load(expert_i[0:1, bass.ds(b + 1, 1)], min_val=0, max_val=EXPERTS - 1)
                    for j in range(CHUNKS):
                        sp.wait_ge(split, b * CHUNKS + (j + 1))
                        sp.nop(nofuse=True)
                        load_chunk(e, j)
                    sp.wait_ge(gelu_done, b * CHUNKS + (CHUNKS + 1))
                    sp.nop(nofuse=True)
                    load_bias(e)

                over_blocks(sp, next_weights)
                n = sp.value_load(blocks_i[0:1, 0:1], min_val=1, max_val=SLOT_BLOCKS)
                sp.wait_ge(b1_loaded, n * 16 + 16)
                sp.nop(nofuse=True)

            @block.gpsimd
            def _(pool):
                def load_rows(b):
                    pool.dma_start(xg[:], slots[bass.ds(b * BLOCK_ROWS, BLOCK_ROWS), :]
                                   .rearrange("(t p) d -> p t d", p=P)).then_inc(x_loaded, 16)

                def rows_and_lower_parts(b):
                    pool.wait_ge(x_transposed, b * ROW_TILES + ROW_TILES)
                    pool.nop(nofuse=True)
                    load_rows(b + 1)
                    for j in range(CHUNKS - 1):
                        make_lower(b + 1, j)
                    pool.wait_ge(y_copied, b + 2)
                    pool.nop(nofuse=True)
                    pool.dma_start(slots[bass.ds(b * BLOCK_ROWS, BLOCK_ROWS), :]
                                   .rearrange("(t p) d -> p t d", p=P), yb[:]).then_inc(y_saved, 16)
                    make_lower(b + 1, CHUNKS - 1)

                pool.dma_start(yb[0:1, 0], slots[0:1]).then_inc(y_saved, 16)
                load_rows(0)
                over_blocks(pool, rows_and_lower_parts)
                n = pool.value_load(blocks_i[0:1, 0:1], min_val=1, max_val=SLOT_BLOCKS)
                pool.wait_ge(x_loaded, n * 16 + 16)
                pool.wait_ge(y_saved, n * 16 + 16)
                pool.nop(nofuse=True)

            @block.tensor
            def _(pe):
                def transpose_rows(b):
                    pe.wait_ge(x_loaded, b * 16 + 16)
                    for t in range(ROW_TILES):
                        for c in range(KC):
                            ins = pe.transpose(pX[t][:, c], xg[:, t, c * P:(c + 1) * P], ident[:])
                        ins.then_inc(x_transposed, 1)

                def layer1(b, j):
                    pe.wait_ge(split, b * CHUNKS + (j + 1))
                    pe.wait_ge(gelu_done, b * CHUNKS + (j + 1))
                    for u in range(CHUNK):
                        cols = slice(u * P, (u + 1) * P)
                        steps = [(w, v, c) for c in range(KC)
                                 for w, v in ((w1_hi, x_hi), (w1_hi, x_lo), (w1_lo, x_hi))]
                        for i, (w, v, c) in enumerate(steps):
                            ins = pe.matmul(pH[u][:], w[:, j, c, cols], v[:, c],
                                            start=i == 0, stop=i == len(steps) - 1)
                        ins.then_inc(hidden, 1)

                def layer2(b, j):
                    pe.wait_ge(h_ready, b * CHUNKS + (j + 1))
                    for u in range(CHUNK):
                        for t in range(ROW_TILES):
                            rows_t = slice(t * P, (t + 1) * P)
                            for i, (v, w) in enumerate(((h_hi, w2_hi), (h_hi, w2_lo), (h_lo, w2_hi))):
                                ins = pe.matmul(pY[t][:], v[:, j % 2, u, rows_t], w[:, j, u],
                                                start=j == 0 and u == 0 and i == 0,
                                                stop=j == CHUNKS - 1 and u == CHUNK - 1 and i == 2)
                    ins.then_inc(l2_done, 1)

                def compute(b):
                    pe.wait_ge(x_ready, b * ROW_TILES + ROW_TILES)
                    layer1(b, 0)
                    for j in range(1, CHUNKS):
                        layer1(b, j)
                        if j == 1:
                            pe.wait_ge(y_copied, b + 1)
                        if j == CHUNKS - 1:
                            transpose_rows(b + 1)
                        layer2(b, j - 1)
                    layer2(b, CHUNKS - 1)

                transpose_rows(0)
                over_blocks(pe, compute)

            @block.scalar
            def _(act):
                act.sem_inc(gelu_done, 1)

                def upper_rows(b):
                    for t in range(ROW_TILES):
                        act.wait_ge(x_transposed, b * ROW_TILES + (t + 1))
                        act.activation(x_hi[:, :, t * P:(t + 1) * P], pX[t][:], ACT.Copy
                                       ).then_inc(x_upper, 1)

                def gelu(b, j):
                    for u in range(CHUNK):
                        hc = CHUNK * j + u
                        act.wait_ge(hidden, b * HC + (hc + 1))
                        ins = act.activation(h_full[:, j % 2, u], pH[u][:], ACT.Gelu_apprx_tanh,
                                             bias=b1[:, hc:hc + 1])
                    ins.then_inc(gelu_done, 1)

                def next_upper(b, j):
                    act.wait_ge(l2_done, b * CHUNKS + (j + 1))
                    make_upper(b + 1, j)

                def activations(b):
                    act.wait_ge(b1_loaded, b * 16 + 16)
                    for j in range(CHUNKS):
                        gelu(b, j)
                        if j == CHUNKS - 1:
                            upper_rows(b + 1)
                        if j >= 2:
                            next_upper(b, j - 2)
                    next_upper(b, CHUNKS - 2)
                    next_upper(b, CHUNKS - 1)

                upper_rows(0)
                over_blocks(act, activations)

            @block.vector
            def _(dve):
                dve.sem_inc(y_copied, 1)

                def lower_rows(b):
                    for t in range(ROW_TILES):
                        part = slice(t * P, (t + 1) * P)
                        dve.wait_ge(x_upper, b * ROW_TILES + (t + 1))
                        dve.tensor_tensor(x_lo[:, :, part], pX[t][:], x_hi[:, :, part].bitcast(fp32),
                                          ALU.subtract).then_inc(x_ready, 1)

                def parts_and_result(b):
                    for j in range(CHUNKS):
                        dve.wait_ge(gelu_done, b * CHUNKS + (j + 2))
                        dve.tensor_copy(h_hi[:, j % 2], h_full[:, j % 2]).then_inc(h_upper, 1)
                        dve.wait_ge(h_upper, b * CHUNKS + (j + 1))
                        dve.tensor_tensor(h_lo[:, j % 2], h_full[:, j % 2], h_hi[:, j % 2].bitcast(fp32),
                                          ALU.subtract).then_inc(h_ready, 1)
                    lower_rows(b + 1)
                    dve.wait_ge(l2_done, b * CHUNKS + CHUNKS)
                    dve.wait_ge(y_saved, b * 16 + 16)
                    for t in range(ROW_TILES):
                        ins = dve.tensor_copy(yb[:, t], pY[t][:])
                    ins.then_inc(y_copied, 1)

                lower_rows(0)
                over_blocks(dve, parts_and_result)

        expert_stack.close()

        with ExitStack() as s:
            Y_RING = NODE_TILES
            Y = sb(s, "Y", [P, Y_RING, 2, DIM])
            gT = sb(s, "gT", [EXPERTS, NODE_TILES, P])
            pG = [ps(s, f"pG{k}", [EXPERTS, P]) for k in range(2)]
            pB = [ps(s, f"pB{k}", [P, DIM]) for k in range(4)]
            (g_transposed, g_copied, b_ready, chain6, combined, saved) = sems(
                s, "g_transposed", "g_copied", "b_ready", "chain6", "combined", "saved")
            fetched = sems(s, *[f"fetched{k}" for k in range(Y_RING)])
            block = s.enter_context(nc.Block())

            @block.gpsimd
            def _(pool):
                for t in range(NODE_TILES):
                    if t >= Y_RING:
                        pool.wait_ge(combined, t - Y_RING + 1)
                    for q in range(2):
                        pool.indirect_dma_start(
                            Y[0:rows(t), t % Y_RING, q, :], None, slots,
                            bass.IndirectOffsetOnAxis(ap=slot_i[0:rows(t), t, q:q + 1], axis=0)
                        ).then_inc(fetched[t % Y_RING], 16)

            @block.tensor
            def _(pe):
                for t in range(NODE_TILES):
                    if t >= 2:
                        pe.wait_ge(g_copied, t - 1)
                    pe.transpose(pG[t % 2][:], gates[:, t], ident[:]).then_inc(g_transposed, 1)
                    pe.wait_ge(g_copied, t + 1)
                    if t >= 4:
                        pe.wait_ge(combined, t - 3)
                    pe.matmul(pB[t % 4][:], gT[:, t], b2[:], start=True, stop=True).then_inc(b_ready, 1)

            @block.scalar
            def _(act):
                for t in range(NODE_TILES):
                    act.wait_ge(g_transposed, t + 1)
                    act.activation(gT[:, t], pG[t % 2][:], ACT.Copy).then_inc(g_copied, 1)

            @block.vector
            def _(dve):
                chain = Chain(dve, chain6)

                def add_bias(t):
                    r = rows(t)
                    dve.wait_ge(b_ready, t + 1)
                    dve.tensor_tensor(X[0:r, t, :], X[0:r, t, :], pB[t % 4][0:r], ALU.add
                                      ).then_inc(chain6, 1)
                    chain.n += 1
                    return chain.n

                added = add_bias(0)
                for t in range(NODE_TILES):
                    r = rows(t)
                    dve.wait_ge(chain6, added)
                    if t + 1 < NODE_TILES:
                        added = add_bias(t + 1)
                    y = Y[0:r, t % Y_RING]
                    dve.wait_ge(fetched[t % Y_RING], 32 * (t // Y_RING + 1))
                    chain.link(dve.scalar_tensor_tensor(X[0:r, t, :], y[:, 0], prob[0:r, t, 0:1],
                                                        X[0:r, t, :], ALU.mult, ALU.add))
                    dve.scalar_tensor_tensor(X[0:r, t, :], y[:, 1], prob[0:r, t, 1:2],
                                             X[0:r, t, :], ALU.mult, ALU.add).then_inc(combined, 1)

            @block.sync
            def _(sp):
                for t in range(NODE_TILES):
                    sp.wait_ge(combined, t + 1)
                    sp.dma_start(out[t * P:t * P + rows(t), :], X[0:rows(t), t, :]).then_inc(saved, 16)
                sp.wait_ge(saved, 16 * NODE_TILES)


def kernel(x, src, dst, edge_attr_4, edge_attr_8, L0_gnn_W_up0, L0_gnn_W_up1, L0_gnn_W_mlp1,
           L0_gnn_W_mlp2, L0_gnn_W_mlp3, L0_gnn_W_mlp4, L0_gnn_W_out0, L0_gnn_W_out1, L0_ffn_Wg,
           L0_ffn_W1, L0_ffn_b1, L0_ffn_W2, L0_ffn_b2):
    import numpy as np
    import concourse.bacc as bacc
    from concourse.bass_utils import run_bass_kernel_spmd

    pad = TILES * P - EDGES

    def tiles(a, mode="constant"):
        a = np.asarray(a)
        a = np.pad(a, [(0, pad)] + [(0, 0)] * (a.ndim - 1), mode=mode)
        return np.ascontiguousarray(a.reshape((TILES, P) + a.shape[1:]).swapaxes(0, 1))

    src_t = tiles(src)
    src_t = np.ascontiguousarray(np.concatenate([src_t, src_t[:, :ITER_TILES]], axis=1))
    basis = np.pad(np.asarray(edge_attr_8), [(0, pad), (0, 0)])
    basis = basis.reshape(ITERS, 2, HALF, BASIS).swapaxes(2, 3).reshape(ITERS, 2 * BASIS, HALF)
    basis = np.ascontiguousarray(np.concatenate([basis, basis[:3]], axis=0))
    b1 = np.ascontiguousarray(np.asarray(L0_ffn_b1).reshape(EXPERTS, HC, P).swapaxes(1, 2))

    arrays = {
        "x": np.ascontiguousarray(x), "src": src_t, "dst": tiles(dst, "edge"),
        "edge_y": tiles(edge_attr_4).reshape(P, TILES * 4), "edge_f": basis,
        "w_up0": np.ascontiguousarray(L0_gnn_W_up0), "w_up1": np.ascontiguousarray(L0_gnn_W_up1),
        "w_mlp1": np.ascontiguousarray(L0_gnn_W_mlp1), "w_mlp2": np.ascontiguousarray(L0_gnn_W_mlp2),
        "w_mlp3": np.ascontiguousarray(L0_gnn_W_mlp3), "w_mlp4": np.ascontiguousarray(L0_gnn_W_mlp4),
        "w_out0": np.ascontiguousarray(L0_gnn_W_out0), "w_out1": np.ascontiguousarray(L0_gnn_W_out1),
        "w_g": np.ascontiguousarray(L0_ffn_Wg), "w_1": np.ascontiguousarray(L0_ffn_W1), "b_1": b1,
        "w_2": np.ascontiguousarray(L0_ffn_W2), "b_2": np.ascontiguousarray(L0_ffn_b2),
    }
    nc = bacc.Bacc("TRN2", target_bir_lowering=False, num_devices=1)
    args = [nc.dram_tensor(n, a.shape, mybir.dt.from_np(a.dtype), kind="ExternalInput").ap()
            for n, a in arrays.items()]
    result = nc.dram_tensor("result", (NODES, DIM), mybir.dt.float32, kind="ExternalOutput").ap()
    program(nc, *args, result)
    r = run_bass_kernel_spmd(nc, [arrays], core_ids=[0])
    return r.results[0]["result"]
```

```python
import concourse.bass as bass
from concourse import mybir
from contextlib import ExitStack

NODES, DIM, EDGES = 1250, 512, 40000
MUL, BASIS, HIDDEN = 128, 8, 64
EXPERTS, FFN = 8, 1024
P = 128
NODE_TILES = -(-NODES // P)
LAST_ROWS = NODES - (NODE_TILES - 1) * P

WINDOW = 32
BLOCK_TILES = 3
ITER_TILES = 2 * BLOCK_TILES
ITERS = -(-EDGES // (ITER_TILES * P))
TILES = ITERS * ITER_TILES
BLOCKS = TILES // BLOCK_TILES
HALF = BLOCK_TILES * P
PASSES = -(-NODES // WINDOW)
ACC_ROWS = NODES + WINDOW + 2
ACC_COLS = 2 * MUL + MUL // 2
CLEAR_MAX = 1284
ACC_PIECES = -(-4 * ACC_ROWS * ACC_COLS // P // CLEAR_MAX)
EARLY_PIECES, LATE_PIECES = 5, 2

BLOCK_ROWS = 352
ROW_TILES = -(-BLOCK_ROWS // P)
MAX_BLOCKS = -(-NODES // BLOCK_ROWS)
SLOT_BLOCKS = 2 * NODES // BLOCK_ROWS + EXPERTS
SLOT_TILES = SLOT_BLOCKS * ROW_TILES
BLOCK_SLOTS = ROW_TILES * P
SURE_BLOCKS = -(-2 * NODES // BLOCK_ROWS)
CLEAR_ROWS = -(-(SLOT_BLOCKS - SURE_BLOCKS) * BLOCK_SLOTS // ITERS)
CLEAR_COLS = CLEAR_ROWS * DIM // P
SLOT_ROWS = SURE_BLOCKS * BLOCK_SLOTS + CLEAR_ROWS * ITERS
KC, HC = DIM // P, FFN // P
CHUNKS = 4
CHUNK = HC // CHUNKS

EPS = 1e-5
SILU_2MOM = 1.679177
SQRT3 = 3.0 ** 0.5
NEIGHBORS = 10.0


def program(nc, x, src, dst, edge_y, edge_f, w_up0, w_up1, w_mlp1, w_mlp2, w_mlp3, w_mlp4,
            w_out0, w_out1, w_g, w_1, b_1, w_2, b_2, out):
    fp32, f32r, i32 = mybir.dt.float32, mybir.dt.float32r, mybir.dt.int32
    bf16 = mybir.dt.bfloat16
    ACT, ALU, AX = mybir.ActivationFunctionType, mybir.AluOpType, mybir.AxisListType

    table = nc.dram_tensor("sender_table", (NODES, DIM), fp32).ap()
    acc = nc.dram_tensor("window_sums", (4 * ACC_ROWS, ACC_COLS), fp32).ap()
    x_rows = nc.dram_tensor("normalised_rows", (NODES, DIM), fp32).ap()
    slots = nc.dram_tensor("expert_results", (SLOT_ROWS, DIM), fp32).ap()

    ctx = ExitStack()
    with ctx:
        def sb(stack, name, shape, dt=fp32):
            return stack.enter_context(nc.sbuf_tensor(name, shape, dt))

        def ps(stack, name, shape):
            return stack.enter_context(nc.psum_tensor(name, shape, fp32))

        def sems(stack, *names):
            return [stack.enter_context(nc.semaphore(n)) for n in names]

        class Chain:

            def __init__(self, eng, sem):
                self.eng, self.sem, self.base, self.n = eng, sem, 0, 0

            def link(self, ins):
                self.n += 1
                ins.then_inc(self.sem, 1)
                self.eng.wait_ge(self.sem, self.base + self.n)

        def rows(t):
            return LAST_ROWS if t == NODE_TILES - 1 else P

        ident = sb(ctx, "ident", [P, P])
        ones = sb(ctx, "ones", [P, P])
        X = sb(ctx, "X", [P, NODE_TILES, DIM])
        wout0 = sb(ctx, "wout0", [P, 2, MUL])
        wout1 = sb(ctx, "wout1", [P, 2, MUL])
        wg = sb(ctx, "wg", [P, KC, EXPERTS])
        eps = sb(ctx, "eps", [P, 1])

        edge_stack = ExitStack()
        with edge_stack:
            E = edge_stack
            src_sb = sb(E, "src_sb", [P, TILES + 2 * ITER_TILES], i32)
            dst_i = sb(E, "dst_i", [P, TILES], i32)
            dst_f = sb(E, "dst_f", [P, TILES])
            y_sb = sb(E, "y_sb", [P, TILES, 4])
            wm1 = sb(E, "wm1", [2 * BASIS, 2 * HIDDEN])
            wm2 = sb(E, "wm2", [2 * HIDDEN, 2 * HIDDEN])
            wm3 = sb(E, "wm3", [2 * HIDDEN, 2 * HIDDEN])
            wm4_hi = sb(E, "wm4_hi", [2 * HIDDEN, 4 * MUL], f32r)
            wm4_lo = sb(E, "wm4_lo", [2 * HIDDEN, 4 * MUL], f32r)
            window_iota = sb(E, "window_iota", [P, WINDOW])
            window_step = sb(E, "window_step", [P, 1])
            sum_row = sb(E, "sum_row", [P, BLOCKS])
            npass_i = sb(E, "npass_i", [P, 1], i32)
            zeros = sb(E, "zeros", [P, CLEAR_MAX])
            (acc_cleared,) = sems(E, "acc_cleared")
            acc_flat = acc.rearrange("r c -> (r c)").rearrange("(p n) -> p n", p=P)

            def clear(piece):
                a, b = piece * CLEAR_MAX, min((piece + 1) * CLEAR_MAX, acc_flat.shape[1])
                nc.sync.dma_start(acc_flat[:, a:b], zeros[:, 0:b - a]).then_inc(acc_cleared, 16)

            with ExitStack() as s:
                GROUP = NODE_TILES // 2
                UP_RING = 4
                wm4 = sb(s, "wm4", [2 * HIDDEN, 4 * MUL])
                wup0 = sb(s, "wup0", [P, MUL])
                wup1 = sb(s, "wup1", [P, MUL])
                stats = sb(s, "stats", [P, NODE_TILES, 6])
                mv = sb(s, "mv", [P, NODE_TILES, 2])
                rstd = sb(s, "rstd", [P, NODE_TILES])
                xn = sb(s, "xn", [P, 2, DIM])
                xT = sb(s, "xT", [P, 2, 4, P])
                up = sb(s, "up", [P, UP_RING, 4, MUL])
                first = sb(s, "first", [P, BLOCKS])
                rel = sb(s, "rel", [P, TILES])
                hilo = sb(s, "hilo", [P, 4])
                row0 = sb(s, "row0", [P, 1], i32)
                row0f = sb(s, "row0f", [P, 1])
                iota_i = sb(s, "iota_i", [P, WINDOW], i32)
                pT = [ps(s, f"pT{k}", [P, 4, P]) for k in range(2)]
                pU = [ps(s, f"pU{k}", [P, 4, MUL]) for k in range(2)]
                pF = ps(s, "pF", [P, BLOCKS])
                pC = ps(s, "pC", [P, 1])
                (x_cleared, up_loaded, wout_loaded, small_loaded, dst_loaded, y_loaded,
                 blocks_cleared, mlp_loaded, ident_step, ident_made, ones_made,
                 iota_made, stats_made, stats_done, sqrt_done, chain1, xn_made, transposed, xT_made, up_done,
                 up_copied, first_ready, ok_made, ok_summed, row0_made, scaled, zeroed) = sems(
                    s, "x_cleared", "up_loaded", "wout_loaded", "small_loaded",
                    "dst_loaded", "y_loaded", "blocks_cleared", "mlp_loaded",
                    "ident_step", "ident_made", "ones_made", "iota_made", "stats_made", "stats_done",
                    "sqrt_done", "chain1", "xn_made", "transposed", "xT_made", "up_done",
                    "up_copied", "first_ready", "ok_made", "ok_summed", "row0_made",
                    "scaled", "zeroed")
                x_loaded = sems(s, "x_loaded0", "x_loaded1")
                table_saved = sems(s, *[f"table_saved{k}" for k in range(UP_RING)])
                block = s.enter_context(nc.Block())

                @block.sync
                def _(sp):
                    sp.dma_start(dst_i[:], dst).then_inc(dst_loaded, 16)
                    x_tiles = x[0:(NODE_TILES - 1) * P, :].rearrange("(t p) d -> p t d", p=P)
                    sp.dma_start(X[:, 0:GROUP], x_tiles[:, 0:GROUP]).then_inc(x_loaded[0], 16)
                    sp.dma_start(wup0[:], w_up0).then_inc(up_loaded, 16)
                    sp.dma_start(wup1[:], w_up1).then_inc(up_loaded, 16)
                    sp.dma_start(X[:, GROUP:NODE_TILES - 1], x_tiles[:, GROUP:]).then_inc(x_loaded[1], 16)
                    sp.wait_ge(x_cleared, 1)
                    sp.dma_start(X[0:LAST_ROWS, NODE_TILES - 1, :], x[(NODE_TILES - 1) * P:NODES, :]
                                 ).then_inc(x_loaded[1], 16)
                    sp.dma_start(wout0[:], w_out0.rearrange("(k p) v -> p k v", p=P)
                                 ).then_inc(wout_loaded, 16)
                    sp.dma_start(wout1[:], w_out1.rearrange("(k p) v -> p k v", p=P)
                                 ).then_inc(small_loaded, 16)
                    sp.dma_start(wg[:], w_g.rearrange("(k p) e -> p k e", p=P)
                                 ).then_inc(small_loaded, 16)
                    sp.dma_start(src_sb[:], src).then_inc(small_loaded, 16)
                    sp.wait_ge(blocks_cleared, 2)
                    for h in range(2):
                        r, c = h * BASIS, h * HIDDEN
                        sp.dma_start(wm1[r:r + BASIS, c:c + HIDDEN], w_mlp1).then_inc(mlp_loaded, 16)
                        sp.dma_start(wm2[c:c + HIDDEN, c:c + HIDDEN], w_mlp2).then_inc(mlp_loaded, 16)
                        for d in range(2):
                            sp.dma_start(wm3[c:c + HIDDEN, d * HIDDEN:(d + 1) * HIDDEN], w_mlp3
                                         ).then_inc(mlp_loaded, 16)
                        sp.dma_start(wm4[c:c + HIDDEN, :], w_mlp4).then_inc(mlp_loaded, 16)
                    sp.wait_ge(zeroed, 1)
                    for piece in range(EARLY_PIECES):
                        clear(piece)
                    for t in range(NODE_TILES):
                        sp.wait_ge(up_copied, t + 1)
                        sp.dma_start(table[t * P:t * P + rows(t), :],
                                     up[0:rows(t), t % UP_RING].rearrange("p c v -> p (c v)")
                                     ).then_inc(table_saved[t % UP_RING], 16)
                        if 0 <= t - 1 < ACC_PIECES - EARLY_PIECES - LATE_PIECES:
                            clear(EARLY_PIECES + t - 1)
                    sp.wait_ge(small_loaded, 48)
                    sp.wait_ge(mlp_loaded, 160)
                    for k in range(UP_RING):
                        sp.wait_ge(table_saved[k], 16 * len(range(k, NODE_TILES, UP_RING)))

                @block.scalar
                def _(act):
                    act.wait_ge(x_loaded[0], 16)
                    act.dma_start(y_sb[:].rearrange("p t m -> p (t m)"), edge_y).then_inc(y_loaded, 16)
                    for k in range(2):
                        group = slice(GROUP * k, GROUP * (k + 1))
                        act.wait_ge(stats_done, k + 1)
                        act.activation(rstd[:, group], mv[:, group, 1], ACT.Sqrt, bias=eps[:, 0:1]
                                       ).then_inc(sqrt_done, 1)

                    def copy_rows(t):
                        act.wait_ge(transposed, t + 1)
                        if t >= 2:
                            act.wait_ge(up_done, t - 1)
                        act.activation(xT[:, t % 2], pT[t % 2][:], ACT.Copy).then_inc(xT_made, 1)

                    copy_rows(0)
                    for t in range(NODE_TILES):
                        if t + 1 < NODE_TILES:
                            copy_rows(t + 1)
                        act.wait_ge(up_done, t + 1)
                        if t >= UP_RING:
                            act.wait_ge(table_saved[t % UP_RING], 16 * (t // UP_RING))
                        act.activation(up[:, t % UP_RING], pU[t % 2][:], ACT.Copy,
                                       scale=SILU_2MOM / HIDDEN ** 0.5 / MUL ** 0.5
                                       ).then_inc(up_copied, 1)
                    act.wait_ge(y_loaded, 16)

                @block.gpsimd
                def _(pool):
                    pool.memset(ident[:], 0.0).then_inc(ident_step, 1)
                    pool.memset(wm1[:], 0.0).then_inc(blocks_cleared, 1)
                    pool.memset(wm2[:], 0.0).then_inc(blocks_cleared, 1)
                    pool.wait_ge(ident_step, 1)
                    pool.affine_select(out=ident[:], in_=ident[:], compare_op=ALU.not_equal, fill=1.0,
                                       base=0, pattern=[[-1, P]], channel_multiplier=1
                                       ).then_inc(ident_made, 1)
                    pool.iota(iota_i[:], pattern=[[1, WINDOW]], base=0, channel_multiplier=0
                              ).then_inc(iota_made, 1)
                    for g in range(4):
                        pool.wait_ge(iota_made, g + 1)
                        pool.iota(row0[32 * g:32 * g + 32, :], pattern=[[1, 1]], base=g * ACC_ROWS,
                                  channel_multiplier=1).then_inc(iota_made, 1)
                    pool.wait_ge(iota_made, 5)
                    pool.memset(zeros[:], 0.0).then_inc(zeroed, 1)

                @block.vector
                def _(dve):
                    chain = Chain(dve, chain1)
                    dve.memset(X[:, NODE_TILES - 1, :], 0.0).then_inc(x_cleared, 1)
                    dve.memset(ones[:], 1.0).then_inc(ones_made, 1)
                    chain.link(dve.memset(eps[:], EPS))
                    dve.wait_ge(dst_loaded, 16)
                    dve.tensor_copy(dst_f[:], dst_i[:]).then_inc(row0_made, 1)
                    dve.wait_ge(first_ready, 1)
                    chain.link(dve.tensor_copy(first[:], pF[:]))
                    blocks3 = lambda a: a.rearrange("p (b k) -> p b k", k=BLOCK_TILES)
                    wide = first[:, :, None].broadcast_to((P, BLOCKS, BLOCK_TILES))
                    chain.link(dve.tensor_tensor(blocks3(rel[:]), blocks3(dst_f[:]), wide, ALU.subtract))
                    chain.link(dve.tensor_reduce(hilo[:, 0:1], rel[:], AX.X, ALU.max))
                    chain.link(dve.tensor_reduce(hilo[:, 1:2], rel[:], AX.X, ALU.min))
                    chain.link(dve.tensor_scalar(hilo[:, 0:1], hilo[:, 0:1], float(WINDOW - 1), None,
                                                 ALU.is_le))
                    chain.link(dve.tensor_scalar(hilo[:, 1:2], hilo[:, 1:2], 0.0, None, ALU.is_ge))
                    dve.tensor_tensor(hilo[:, 2:3], hilo[:, 0:1], hilo[:, 1:2], ALU.mult
                                      ).then_inc(ok_made, 1)
                    def statistics(k):
                        dve.wait_ge(x_loaded[k], 16 * (k + 1))
                        tiles = range(GROUP * k, GROUP * (k + 1))
                        for t in tiles:
                            dve.bn_stats(stats[:, t, :], X[:, t, :]).then_inc(stats_made, 1)
                        for t in tiles:
                            dve.wait_ge(stats_made, t + 1)
                            ins = dve.bn_aggr(mv[:, t, :], stats[:, t, :])
                        ins.then_inc(stats_done, 1)

                    def place_windows():
                        dve.wait_ge(ok_summed, 1)
                        chain.link(dve.tensor_scalar(hilo[:, 3:4], pC[:], float(P), None, ALU.is_equal))
                        fits = hilo[:, 3:4]
                        chain.link(dve.tensor_scalar(first[:], first[:], fits, None, ALU.mult))
                        chain.link(dve.tensor_tensor(blocks3(dst_f[:]), blocks3(dst_f[:]), wide,
                                                     ALU.subtract))
                        dve.wait_ge(iota_made, 5)
                        chain.link(dve.tensor_copy(row0f[:], row0[:]))
                        chain.link(dve.tensor_scalar(sum_row[:], first[:], row0f[:, 0:1], None, ALU.add))
                        chain.link(dve.tensor_scalar(window_step[:], fits, -float(WINDOW), float(WINDOW),
                                                     ALU.mult, ALU.add))
                        chain.link(dve.tensor_scalar(npass_i[:], fits, 1.0 - PASSES, float(PASSES),
                                                     ALU.mult, ALU.add))
                        chain.link(dve.tensor_copy(window_iota[:], iota_i[:]))

                    statistics(0)
                    for k in range(2):
                        group = slice(GROUP * k, GROUP * (k + 1))
                        dve.wait_ge(sqrt_done, k + 1)
                        chain.link(dve.reciprocal(rstd[:, group], rstd[:, group]))
                        for t in range(GROUP * k, GROUP * (k + 1)):
                            if t >= 2:
                                dve.wait_ge(transposed, t - 1)
                            dve.tensor_scalar(xn[:, t % 2, :], X[:, t, :], mv[:, t, 0:1],
                                              rstd[:, t:t + 1], ALU.subtract, ALU.mult
                                              ).then_inc(xn_made, 1)
                            if t == 1:
                                place_windows()
                                statistics(1)
                    dve.wait_ge(wout_loaded, 16)
                    dve.tensor_scalar(wout0[:, 1, :], wout0[:, 1, :], 1.0 / SQRT3, None, ALU.mult
                                      ).then_inc(scaled, 1)
                    dve.wait_ge(mlp_loaded, 160)
                    chain.link(dve.tensor_copy(wm4_hi[:], wm4[:]))
                    chain.link(dve.tensor_tensor(wm4_lo[:], wm4[:], wm4_hi[:].bitcast(fp32), ALU.subtract))

                @block.tensor
                def _(pe):
                    pe.wait_ge(ones_made, 1)
                    pe.wait_ge(row0_made, 1)
                    pe.matmul(pF[:], ones[0:1, :], dst_f[0:1, 0:TILES:BLOCK_TILES], start=True, stop=True
                              ).then_inc(first_ready, 1)
                    pe.wait_ge(ok_made, 1)
                    pe.matmul(pC[:], ones[:], hilo[:, 2:3], start=True, stop=True).then_inc(ok_summed, 1)
                    pe.wait_ge(ident_made, 1)
                    pe.wait_ge(up_loaded, 32)

                    def transpose(t):
                        pe.wait_ge(xn_made, t + 1)
                        if t >= 2:
                            pe.wait_ge(xT_made, t - 1)
                        v = xn[:, t % 2, MUL:].rearrange("p (u m) -> p m u", m=3)
                        pe.transpose(pT[t % 2][:, 0], xn[:, t % 2, 0:MUL], ident[:])
                        for m in range(3):
                            ins = pe.transpose(pT[t % 2][:, 1 + m], v[:, m], ident[:])
                        ins.then_inc(transposed, 1)

                    def project(t):
                        pe.wait_ge(xT_made, t + 1)
                        if t >= 2:
                            pe.wait_ge(up_copied, t - 1)
                        for c in range(4):
                            ins = pe.matmul(pU[t % 2][:, c], xT[:, t % 2, c], (wup0 if c == 0 else wup1)[:],
                                            start=True, stop=True)
                        ins.then_inc(up_done, 1)

                    transpose(0)
                    for t in range(NODE_TILES):
                        if t + 1 < NODE_TILES:
                            transpose(t + 1)
                        project(t)

            with ExitStack() as s:
                ef = sb(s, "ef", [2 * BASIS, HALF])
                h = [sb(s, f"h{k}", [2 * HIDDEN, HALF]) for k in range(2)]
                h3 = [sb(s, f"h3_{k}", [2 * HIDDEN, HALF], f32r) for k in range(2)]
                h3_full = [sb(s, f"h3_full{k}", [2 * HIDDEN, HALF]) for k in range(2)]
                gidx = sb(s, "gidx", [P, ITER_TILES], i32)
                S = sb(s, "S", [P, ITER_TILES, 4, MUL])
                M = sb(s, "M", [P, 3, 8, MUL])
                eq = sb(s, "eq", [P, 2, BLOCK_TILES, WINDOW])
                hot = sb(s, "hot", [P, 2, BLOCK_TILES, 4, WINDOW])
                sums = sb(s, "sums", [P, 2, ACC_COLS])
                fidx_f = sb(s, "fidx_f", [P, 2])
                fidx = sb(s, "fidx", [P, 2], i32)
                pass_row = sb(s, "pass_row", [P, 1])
                pW = [ps(s, f"pW{k}", [P, 4, MUL]) for k in range(3)]
                pZ = [ps(s, f"pZ{k}", [P, HALF]) for k in range(3)]
                pA = [ps(s, f"pA{k}", [P, ACC_COLS]) for k in range(2)]
                (ef_loaded, z_ready, h_ready, w_ready, product, scattered, hot_step, hot_ready,
                 sums_copied, parts_ready, slot_cleared, idx_made, fidx_step, fidx_made,
                 pass_step, window_moved) = sems(
                    s, "ef_loaded", "z_ready", "h_ready", "w_ready", "product", "scattered",
                    "hot_step", "hot_ready", "sums_copied", "parts_ready", "slot_cleared", "idx_made",
                    "fidx_step", "fidx_made", "pass_step", "window_moved")
                gathered = sems(s, *[f"gathered{j}" for j in range(ITER_TILES)])
                flushed = sems(s, "flushed0", "flushed1")
                block = s.enter_context(nc.Block())
                RING = 3

                def passes(eng):
                    return eng.value_load(npass_i[0:1, 0:1], min_val=1, max_val=PASSES)

                slots_flat = slots[SURE_BLOCKS * BLOCK_SLOTS:].rearrange("r c -> (r c)").rearrange(
                    "(p n) -> p n", p=P)

                @block.sync
                def _(sp):
                    n = passes(sp)
                    sp.dma_start(ef[:], edge_f[0]).then_inc(ef_loaded, 16)
                    sp.wait_ge(z_ready, 1)
                    for piece in range(ACC_PIECES - LATE_PIECES, ACC_PIECES):
                        clear(piece)
                    sp.dma_start(ef[:], edge_f[1]).then_inc(ef_loaded, 16)
                    sp.wait_ge(z_ready, 5)
                    sp.dma_start(ef[:], edge_f[2]).then_inc(ef_loaded, 16)
                    with sp.Fori(0, n) as p:
                        with sp.Fori(0, ITERS) as i:
                            g = p * ITERS + i
                            sp.wait_ge(z_ready, g * 4 + 8)
                            sp.dma_start(ef[:], edge_f[bass.ds(i + 3, 1)].rearrange("o r n -> (o r) n")
                                         ).then_inc(ef_loaded, 16)
                            sp.dma_start(slots_flat[:, bass.ds(i * CLEAR_COLS, CLEAR_COLS)],
                                         zeros[:, 0:CLEAR_COLS]).then_inc(slot_cleared, 16)
                    sp.wait_ge(ef_loaded, n * (16 * ITERS) + 48)
                    sp.nop(nofuse=True)
                    sp.wait_ge(slot_cleared, n * (16 * ITERS))
                    sp.nop(nofuse=True)

                @block.scalar
                def _(act):
                    n = passes(act)
                    act.sem_inc(sums_copied, 2)

                    def silu(layer, z):
                        act.wait_ge(z_ready, z)
                        scale = (1.0 / BASIS ** 0.5, SILU_2MOM / HIDDEN ** 0.5, SILU_2MOM / HIDDEN ** 0.5)
                        act.activation(h[layer][:], pZ[1 - layer][:], ACT.Silu, scale=scale[layer]
                                       ).then_inc(h_ready, 1)

                    def copy_sums(g, k):
                        act.wait_ge(scattered, g * ITER_TILES + (ITER_TILES + BLOCK_TILES * (k + 1)))
                        act.wait_ge(flushed[k], g * 16 + 16)
                        act.activation(sums[:, k], pA[k][:], ACT.Copy).then_inc(sums_copied, 1)

                    def silu_parts(q, z):
                        act.wait_ge(z_ready, z)
                        scale = SILU_2MOM / HIDDEN ** 0.5
                        act.activation(h3[q][:], pZ[2 * (1 - q)][:], ACT.Silu, scale=scale)
                        act.activation(h3_full[q][HIDDEN:], pZ[2 * (1 - q)][HIDDEN:], ACT.Silu, scale=scale
                                       ).then_inc(h_ready, 1)

                    silu(0, 1)
                    silu(1, 2)
                    silu_parts(0, 3)
                    silu_parts(1, 4)
                    silu(0, 5)
                    silu(1, 6)
                    with act.Fori(0, n) as p:
                        with act.Fori(0, ITERS) as i:
                            g = p * ITERS + i
                            act.wait_ge(w_ready, g * ITER_TILES + BLOCK_TILES)
                            silu_parts(0, g * 4 + 7)
                            silu(0, g * 4 + 8)
                            copy_sums(g, 0)
                            act.wait_ge(w_ready, g * ITER_TILES + 2 * BLOCK_TILES)
                            silu_parts(1, g * 4 + 9)
                            silu(1, g * 4 + 10)
                            copy_sums(g, 1)

                @block.gpsimd
                def _(pool):
                    n = passes(pool)
                    pool.memset(pass_row[:], 0.0).then_inc(pass_step, 1)

                    def gather(j):
                        pool.indirect_dma_start(
                            S[:, j].rearrange("p c u -> p (c u)"), None, table,
                            bass.IndirectOffsetOnAxis(ap=gidx[:, j:j + 1], axis=0)
                        ).then_inc(gathered[j], 16)

                    for k in range(2):
                        half = slice(BLOCK_TILES * k, BLOCK_TILES * (k + 1))
                        pool.tensor_copy(gidx[:, half], src_sb[:, half]).then_inc(idx_made, 1)
                    pool.wait_ge(idx_made, 2)
                    for j in range(ITER_TILES):
                        gather(j)
                    for k in range(2):
                        pool.dma_start(sums[:, k], zeros[:, 0:ACC_COLS]).then_inc(flushed[k], 16)
                    for j in range(BLOCK_TILES):
                        pool.wait_ge(gathered[j], 16)
                    pool.tensor_copy(gidx[:, 0:BLOCK_TILES],
                                     src_sb[:, ITER_TILES:ITER_TILES + BLOCK_TILES]).then_inc(idx_made, 1)
                    with pool.Fori(0, n) as p:
                        with pool.Fori(0, ITERS) as i:
                            g = p * ITERS + i
                            g6 = g * ITER_TILES
                            for k in range(2):
                                pool.wait_ge(pass_step, p + 1)
                                pool.nop(nofuse=True)
                                pool.tensor_tensor(fidx_f[:, k:k + 1],
                                                   sum_row[:, bass.ds(i * 2 + k, 1)],
                                                   pass_row[:], ALU.add).then_inc(fidx_step, 1)
                                pool.wait_ge(idx_made, g * 2 + (k + 3))
                                for j in range(BLOCK_TILES * k, BLOCK_TILES * (k + 1)):
                                    pool.wait_ge(product, g6 + (RING + j + 1))
                                    pool.nop(nofuse=True)
                                    gather(j)
                                    if j == BLOCK_TILES * k:
                                        pool.wait_ge(fidx_step, g * 2 + (k + 1))
                                        pool.nop(nofuse=True)
                                        pool.tensor_copy(fidx[:, k:k + 1], fidx_f[:, k:k + 1]
                                                         ).then_inc(fidx_made, 1)
                                q = 1 - k
                                for j in range(BLOCK_TILES * q, BLOCK_TILES * (q + 1)):
                                    pool.wait_ge(gathered[j], g * 16 + 16 * (k + 1))
                                pool.nop(nofuse=True)
                                ahead = ITER_TILES + BLOCK_TILES * (k + 1)
                                pool.tensor_copy(gidx[:, BLOCK_TILES * q:BLOCK_TILES * (q + 1)],
                                                 src_sb[:, bass.ds(i * ITER_TILES + ahead, BLOCK_TILES)]
                                                 ).then_inc(idx_made, 1)
                                pool.wait_ge(fidx_made, g * 2 + (k + 1))
                                if k == 0:
                                    pool.wait_ge(acc_cleared, 16 * ACC_PIECES)
                                    pool.wait_ge(flushed[1], g * 16 + 16)
                                else:
                                    pool.wait_ge(flushed[0], g * 16 + 32)
                                pool.wait_ge(sums_copied, g * 2 + (k + 3))
                                pool.nop(nofuse=True)
                                pool.indirect_dma_start(
                                    acc, bass.IndirectOffsetOnAxis(ap=fidx[:, k:k + 1], axis=0),
                                    sums[:, k], None, compute_op=ALU.add).then_inc(flushed[k], 16)
                        pool.tensor_tensor(pass_row[:], pass_row[:], window_step[:], ALU.add
                                           ).then_inc(pass_step, 1)
                    for j in range(ITER_TILES):
                        pool.wait_ge(gathered[j], n * (16 * ITERS) + 16)
                    for k in range(2):
                        pool.wait_ge(flushed[k], n * (16 * ITERS) + 16)

                @block.vector
                def _(dve):
                    n = passes(dve)
                    dve.sem_inc(product, RING)

                    def receivers(g, i, k):
                        tiles = bass.ds(i * ITER_TILES + BLOCK_TILES * k, BLOCK_TILES)
                        dve.wait_ge(scattered, g * ITER_TILES + BLOCK_TILES * (k + 1))
                        dve.tensor_tensor(
                            eq[:, k], dst_f[:, tiles, None].broadcast_to((P, BLOCK_TILES, WINDOW)),
                            window_iota[:, None, :].broadcast_to((P, BLOCK_TILES, WINDOW)),
                            ALU.is_equal).then_inc(hot_step, 1)

                    def one_hots(g, i, k):
                        tiles = bass.ds(i * ITER_TILES + BLOCK_TILES * k, BLOCK_TILES)
                        dve.wait_ge(hot_step, g * 2 + (k + 1))
                        dve.tensor_tensor(
                            hot[:, k],
                            eq[:, k, :, None, :].broadcast_to((P, BLOCK_TILES, 4, WINDOW)),
                            y_sb[:, tiles, :, None].broadcast_to((P, BLOCK_TILES, 4, WINDOW)),
                            ALU.mult).then_inc(hot_ready, 1)

                    def products(g, g6, j):
                        W, m = pW[j % 3], M[:, j % 3]
                        dve.wait_ge(w_ready, g6 + (j + 1))
                        dve.wait_ge(gathered[j], g * 16 + 16)
                        dve.wait_ge(scattered, g6 + (j + 1 + ITER_TILES - RING))
                        dve.tensor_tensor(m[:, 0:2], W[:, 0:2],
                                          S[:, j, 0:1].broadcast_to((P, 2, MUL)), ALU.mult)
                        dve.tensor_tensor(
                            m[:, 2:8].rearrange("p (a b) u -> p a b u", a=2),
                            W[:, 2:4, None, :].broadcast_to((P, 2, 3, MUL)),
                            S[:, j, None, 1:4].broadcast_to((P, 2, 3, MUL)), ALU.mult
                        ).then_inc(product, 1)

                    def parts(q, count):
                        dve.wait_ge(h_ready, count)
                        dve.tensor_tensor(h3[q][HIDDEN:], h3_full[q][HIDDEN:],
                                          h3[q][HIDDEN:].bitcast(fp32), ALU.subtract
                                          ).then_inc(parts_ready, 1)

                    parts(0, 3)
                    parts(1, 4)
                    with dve.Fori(0, n) as p:
                        with dve.Fori(0, ITERS) as i:
                            g = p * ITERS + i
                            g6 = g * ITER_TILES
                            receivers(g, i, 0)
                            products(g, g6, 0)
                            one_hots(g, i, 0)
                            products(g, g6, 1)
                            receivers(g, i, 1)
                            products(g, g6, 2)
                            one_hots(g, i, 1)
                            parts(0, g * 4 + 7)
                            products(g, g6, 3)
                            products(g, g6, 4)
                            products(g, g6, 5)
                            parts(1, g * 4 + 9)
                        dve.tensor_scalar(window_iota[:], window_iota[:], window_step[:, 0:1], None,
                                          ALU.add).then_inc(window_moved, 1)
                        dve.wait_ge(window_moved, p + 1)

                @block.tensor
                def _(pe):
                    n = passes(pe)
                    pe.sem_inc(scattered, ITER_TILES)

                    def mlp(layer, done, chunk=None, half=None):
                        if layer == 0:
                            pe.wait_ge(ef_loaded, chunk)
                        if done is not None:
                            pe.wait_ge(h_ready, done)
                        if layer < 2:
                            pe.matmul(pZ[1 - layer][:], (wm1, wm2)[layer][:], (ef, h[0])[layer][:],
                                      start=True, stop=True).then_inc(z_ready, 1)
                            return
                        for q in (0, 1) if half is None else (half,):
                            r = HIDDEN * q
                            pe.matmul(pZ[2 * (1 - q)][:], wm3[r:r + HIDDEN, :], h[1][r:r + HIDDEN, :],
                                      start=True, stop=True).then_inc(z_ready, 1)

                    def edge_weights(j, free):
                        pe.wait_ge(product, free)
                        q, c = j // BLOCK_TILES, P * (j % BLOCK_TILES)
                        for n, w in enumerate((wm4_hi, wm4_lo)):
                            ins = pe.matmul(pW[j % 3][:].rearrange("p c u -> p (c u)"),
                                            h3[q][:, c:c + P], w[:], start=n == 0, stop=n == 1)
                        ins.then_inc(w_ready, 1)

                    def scatter(g, g6, j):
                        k, t = j // BLOCK_TILES, j % BLOCK_TILES
                        if t == 0:
                            pe.wait_ge(hot_ready, g * 2 + (k + 1))
                            pe.wait_ge(sums_copied, g * 2 + (k + 1))
                        pe.wait_ge(product, g6 + (j + 1 + RING))
                        A, m, first, last = pA[k], M[:, j % 3], t == 0, t == BLOCK_TILES - 1
                        for grp, y, a, b in ((0, 0, 0, 2), (1, 0, 3, 4), (2, 1, 1, 5), (3, 2, 1, 6)):
                            pe.matmul(A[32 * grp:32 * grp + 32, 0:2 * MUL], hot[:, k, t, y],
                                      m[:, a:b + 1:b - a], start=first, stop=last,
                                      skip_group_check=True)
                        for grp, unit, part in ((0, 1, 0), (1, 7, 0), (2, 1, 1), (3, 7, 1)):
                            ins = pe.matmul(A[32 * grp:32 * grp + 32, 2 * MUL:], hot[:, k, t, 3],
                                            m[:, unit, part * MUL // 2:(part + 1) * MUL // 2],
                                            start=False, stop=last, skip_group_check=True)
                        ins.then_inc(scattered, 1)

                    for layer in range(3):
                        mlp(layer, layer or None, 16)
                    mlp(0, 4, 32)
                    pe.wait_ge(parts_ready, 1)
                    edge_weights(0, 1)
                    edge_weights(1, 2)
                    mlp(1, 5)
                    with pe.Fori(0, n) as p:
                        with pe.Fori(0, ITERS) as i:
                            g = p * ITERS + i
                            g6 = g * ITER_TILES
                            for j in range(ITER_TILES):
                                nxt = j + 2
                                if nxt % BLOCK_TILES == 0:
                                    pe.wait_ge(parts_ready, g * 2 + (nxt // BLOCK_TILES + 1))
                                edge_weights(nxt % ITER_TILES, g6 + (nxt + 1))
                                scatter(g, g6, j)
                                if j == 0:
                                    mlp(2, g * 4 + 6, half=0)
                                elif j == 1:
                                    mlp(0, None, g * 16 + 48)
                                elif j == 2:
                                    mlp(2, None, half=1)
                                elif j == 4:
                                    mlp(1, g * 4 + 9)

        prob = sb(ctx, "prob", [P, NODE_TILES, 2])
        slot_i = sb(ctx, "slot_i", [P, 2, NODE_TILES], i32)
        slot_node = sb(ctx, "slot_node", [P, SLOT_TILES], i32)
        expert_i = sb(ctx, "expert_i", [P, SLOT_BLOCKS], i32)
        last_block_i = sb(ctx, "last_block_i", [P, 1], i32)

        expert_stack = ctx.enter_context(ExitStack())
        raw1 = sb(expert_stack, "raw1", [P, CHUNKS, KC, CHUNK * P])
        raw2 = sb(expert_stack, "raw2", [P, CHUNKS, CHUNK, DIM])
        w1_hi = sb(expert_stack, "w1_hi", [P, CHUNKS, KC, CHUNK * P], f32r)
        w1_lo = sb(expert_stack, "w1_lo", [P, CHUNKS, KC, CHUNK * P], f32r)
        w2_hi = sb(expert_stack, "w2_hi", [P, CHUNKS, CHUNK, DIM], f32r)
        w2_lo = sb(expert_stack, "w2_lo", [P, CHUNKS, CHUNK, DIM], f32r)
        b1 = sb(expert_stack, "b1", [P, HC])
        b2 = sb(expert_stack, "b2", [P, DIM])
        raw_loaded = sems(expert_stack, *[f"raw_loaded{j}" for j in range(CHUNKS)])
        b1_loaded, b2_loaded, upper_made, split = sems(expert_stack, "b1_loaded", "b2_loaded",
                                                       "upper_made", "split")

        def load_chunk(e, j):
            sp = nc.sync
            sp.dma_start(raw1[:, j],
                         w_1[bass.ds(e, 1)].rearrange("o (c p) h -> p (o c) h", p=P)
                         [:, :, j * CHUNK * P:(j + 1) * CHUNK * P]).then_inc(raw_loaded[j], 16)
            sp.dma_start(raw2[:, j],
                         w_2[bass.ds(e, 1)].rearrange("o (c p) h -> p (o c) h", p=P)
                         [:, j * CHUNK:(j + 1) * CHUNK]).then_inc(raw_loaded[j], 16)

        def load_bias1(e):
            nc.sync.dma_start(b1[:], b_1[bass.ds(e, 1)].rearrange("o p c -> (o p) c")
                              ).then_inc(b1_loaded, 16)

        def load_bias2(e):
            nc.sync.dma_start(b2[:], b_2[bass.ds(e, 1)].broadcast_to((P, DIM))
                              ).then_inc(b2_loaded, 16)

        def make_upper(b, j):
            act = nc.scalar
            act.wait_ge(raw_loaded[j], b * 32 + 32)
            act.activation(w1_hi[:, j], raw1[:, j], ACT.Copy)
            act.activation(w2_hi[:, j], raw2[:, j], ACT.Copy).then_inc(upper_made, 1)

        def make_lower(b, j):
            pool = nc.gpsimd
            pool.wait_ge(upper_made, b * CHUNKS + (j + 1))
            pool.nop(nofuse=True)
            pool.tensor_tensor(w1_lo[:, j], raw1[:, j], w1_hi[:, j].bitcast(fp32), ALU.subtract)
            pool.tensor_tensor(w2_lo[:, j], raw2[:, j], w2_hi[:, j].bitcast(fp32), ALU.subtract
                               ).then_inc(split, 1)

        with ExitStack() as s:
            A_RING = 3
            PAD = 8
            NODE_LOW = 32
            xn2 = sb(s, "xn2", [P, NODE_TILES, DIM])
            A = sb(s, "A", [P, A_RING, 4, ACC_COLS])
            joined = sb(s, "joined", [P, A_RING, 2, P])
            msgT = sb(s, "msgT", [P, 2, 8, P])
            x2T = sb(s, "x2T", [P, 2, KC, P])
            stats = sb(s, "stats2", [P, 2, 6])
            mv = sb(s, "mv2", [P, 2, 2])
            rstd = sb(s, "rstd2", [P, 2])
            top = sb(s, "top", [P, NODE_TILES])
            esum = sb(s, "esum", [P, NODE_TILES])
            ex = sb(s, "ex", [P, NODE_TILES, EXPERTS])
            left = sb(s, "left", [P, NODE_TILES, EXPERTS])
            place = sb(s, "place", [P, NODE_TILES])
            found = sb(s, "found", [P, NODE_TILES, EXPERTS])
            mask = sb(s, "mask", [P, 2, NODE_TILES, EXPERTS])
            mask12 = sb(s, "mask12", [P, NODE_TILES, EXPERTS])
            order_i = sb(s, "order_i", [P, EXPERTS], i32)
            order = sb(s, "order", [P, EXPERTS])
            node_i = sb(s, "node_i", [P, NODE_TILES], i32)
            valid = sb(s, "valid", [P, NODE_TILES])
            before = sb(s, "before", [P, P])
            run = [sb(s, f"run{k}", [P, PAD + NODE_TILES, EXPERTS]) for k in range(2)]
            end = [sb(s, f"end{k}", [P, PAD + EXPERTS]) for k in range(2)]
            rank = sb(s, "rank", [P, NODE_TILES, EXPERTS])
            thr_i = sb(s, "thr_i", [P, MAX_BLOCKS], i32)
            thr = sb(s, "thr", [P, MAX_BLOCKS])
            over = sb(s, "over", [P, EXPERTS, MAX_BLOCKS])
            blk_i = sb(s, "blk_i", [P, SLOT_BLOCKS], i32)
            blk = sb(s, "blk", [P, SLOT_BLOCKS])
            passed = sb(s, "passed", [P, SLOT_BLOCKS, EXPERTS - 1])
            expert_f = sb(s, "expert_f", [P, SLOT_BLOCKS])
            base = sb(s, "base", [P, EXPERTS])
            place_in = sb(s, "place_in", [P, 2, NODE_TILES])
            slot_f = sb(s, "slot_f", [P, 2, NODE_TILES])
            full = sb(s, "full", [P, 2, NODE_TILES, MAX_BLOCKS - 1])
            passed_blocks = sb(s, "passed_blocks", [P, 2, NODE_TILES])
            tile_i = sb(s, "tile_i", [P, 2, NODE_TILES], i32)
            row_f = sb(s, "row_f", [P, 2, NODE_TILES])
            tile_f = sb(s, "tile_f", [P, 2, NODE_TILES])
            row_iota_i = sb(s, "row_iota_i", [P, P], i32)
            row_iota = sb(s, "row_iota", [P, P])
            tile_iota_i = sb(s, "tile_iota_i", [P, SLOT_TILES], i32)
            tile_iota = sb(s, "tile_iota", [P, SLOT_TILES])
            node = sb(s, "node", [P, NODE_TILES])
            row_hot = sb(s, "row_hot", [P, 2, NODE_TILES, P], bf16)
            tile_hot = sb(s, "tile_hot", [P, 2, NODE_TILES, SLOT_TILES])
            tile_node = sb(s, "tile_node", [P, 2, NODE_TILES, 2, SLOT_TILES], bf16)
            node_part_i = sb(s, "node_part_i", [P, NODE_TILES], i32)
            node_part = sb(s, "node_part", [P, 2, NODE_TILES])
            lower = sb(s, "lower", [P, SLOT_TILES])
            picked = sb(s, "picked", [P, 2, NODE_TILES, EXPERTS])
            pM = [ps(s, f"pM{k}", [P, 4, P]) for k in range(2)]
            pO = [ps(s, f"pO{k}", [P, 4, MUL]) for k in range(2)]
            pX = [ps(s, f"pX{k}", [P, KC, P]) for k in range(2)]
            pL = ps(s, "pL", [P, 2 * NODE_TILES, EXPERTS])
            pR = ps(s, "pR", [P, 2, NODE_TILES, EXPERTS])
            (iota_made, sums_added, msg_transposed, msg_copied, out_done, chain3, stats_made,
             sqrt_ready, sqrt_done, xn_made, x_transposed, x_copied, logits, shifted, exp_done,
             masks_made, ranked, tiles_made, rows_made, inverted, x_saved) = sems(
                s, "iota3_made", "sums_added", "msg_transposed", "msg_copied", "out_done", "chain3",
                "stats_made", "sqrt_ready3", "sqrt_done3", "xn_made3", "x_transposed", "x_copied",
                "logits", "shifted", "exp_done", "masks_made", "ranked", "tiles_made", "rows_made",
                "inverted", "x_saved")
            acc_loaded = sems(s, *[f"acc_loaded{k}" for k in range(A_RING)])
            block = s.enter_context(nc.Block())
            pN = pL[:].rearrange("p t e -> p (t e)")[:, 0:2 * SLOT_TILES].rearrange(
                "p (k t) -> p k t", k=2)
            STEPS = NODE_TILES + 3
            UPPER_STEPS = (4, 5, 7, 8)

            def stage(step, lag):
                t = step - lag
                return t if 0 <= t < NODE_TILES else None

            @block.sync
            def _(sp):
                for t in range(NODE_TILES):
                    if t >= A_RING:
                        sp.wait_ge(msg_transposed, 2 * (t - A_RING + 1))
                    sp.dma_start(A[:, t % A_RING],
                                 acc.rearrange("(g n) c -> n g c", g=4)[t * P:(t + 1) * P]
                                 ).then_inc(acc_loaded[t % A_RING], 16)
                    if t == A_RING:
                        load_chunk(0, 0)
                        load_chunk(0, 1)
                    elif t == 2 * A_RING:
                        load_chunk(0, 2)
                        load_chunk(0, 3)
                load_bias1(0)
                load_bias2(0)
                for t in range(NODE_TILES):
                    sp.wait_ge(xn_made, t + 1)
                    sp.dma_start(x_rows[t * P:t * P + rows(t), :], xn2[0:rows(t), t]
                                 ).then_inc(x_saved, 16)
                sp.wait_ge(x_saved, 16 * NODE_TILES)

            @block.gpsimd
            def _(pool):
                pool.affine_select(out=before[:], in_=ones[:], compare_op=ALU.is_gt, fill=0.0, base=0,
                                   pattern=[[1, P]], channel_multiplier=-1).then_inc(iota_made, 1)
                pool.iota(order_i[:], pattern=[[-1, EXPERTS]], base=EXPERTS, channel_multiplier=0
                          ).then_inc(iota_made, 1)
                pool.iota(node_i[:], pattern=[[P, NODE_TILES]], base=0, channel_multiplier=1
                          ).then_inc(iota_made, 1)
                pool.iota(thr_i[:], pattern=[[BLOCK_ROWS, MAX_BLOCKS]], base=0, channel_multiplier=0
                          ).then_inc(iota_made, 1)
                pool.iota(blk_i[:], pattern=[[1, SLOT_BLOCKS]], base=0, channel_multiplier=0
                          ).then_inc(iota_made, 1)
                pool.iota(row_iota_i[:], pattern=[[1, P]], base=0, channel_multiplier=0
                          ).then_inc(iota_made, 1)
                pool.iota(tile_iota_i[:], pattern=[[1, SLOT_TILES]], base=0, channel_multiplier=0
                          ).then_inc(iota_made, 1)
                for j in range(CHUNKS):
                    make_lower(0, j)

            @block.tensor
            def _(pe):
                for step in range(STEPS):
                    t = stage(step, 0)
                    if t is not None:
                        a = A[:, t % A_RING]
                        pe.wait_ge(sums_added, t + 1)
                        parts = [a[:, 0, 0:P], joined[:, t % A_RING, 0],
                                 a[:, 2, 0:P], a[:, 0, P:2 * P], a[:, 3, 0:P], a[:, 1, 0:P],
                                 joined[:, t % A_RING, 1], a[:, 1, P:2 * P]]
                        for q in range(2):
                            if t >= 1:
                                pe.wait_ge(msg_copied, 2 * (t - 1) + q + 1)
                            for u in range(4):
                                ins = pe.transpose(pM[q][:, u], parts[4 * q + u], ident[:])
                            ins.then_inc(msg_transposed, 1)
                    t = stage(step, 1)
                    if t is not None:
                        pe.wait_ge(msg_copied, 2 * t + 2)
                        if t >= 2:
                            pe.wait_ge(sqrt_ready, t - 1)
                        for c in range(4):
                            w = wout0 if c == 0 else wout1
                            for q in range(2):
                                ins = pe.matmul(pO[t % 2][:, c], msgT[:, t % 2, 2 * c + q], w[:, q],
                                                start=q == 0, stop=q == 1)
                        ins.then_inc(out_done, 1)
                    t = stage(step, 2)
                    if t is not None:
                        pe.wait_ge(xn_made, t + 1)
                        if t >= 2:
                            pe.wait_ge(x_copied, t - 1)
                        for k in range(KC):
                            ins = pe.transpose(pX[t % 2][:, k], xn2[:, t, k * P:(k + 1) * P], ident[:])
                        ins.then_inc(x_transposed, 1)
                    t = stage(step, 3)
                    if t is not None:
                        pe.wait_ge(x_copied, t + 1)
                        for k in range(KC):
                            ins = pe.matmul(pL[:, t], x2T[:, t % 2, k], wg[:, k],
                                            start=k == 0, stop=k == KC - 1)
                        ins.then_inc(logits, 1)
                pe.wait_ge(iota_made, 1)
                pe.wait_ge(masks_made, 1)
                flat = mask12[:].rearrange("p t e -> p (t e)")
                pe.matmul(pR[:, 0].rearrange("p t e -> p (t e)"), before[:], flat, start=True, stop=True)
                pe.matmul(pR[:, 1].rearrange("p t e -> p (t e)"), ones[:], flat, start=True, stop=True
                          ).then_inc(ranked, 1)
                pe.wait_ge(tiles_made, 2)
                for q in range(2):
                    pe.wait_ge(rows_made, q + 1)
                    for t in range(NODE_TILES):
                        ins = pe.matmul(pN.rearrange("p k t -> p (k t)"), row_hot[:, q, t],
                                        tile_node[:, q, t].rearrange("p k t -> p (k t)"),
                                        start=q == 0 and t == 0, stop=q == 1 and t == NODE_TILES - 1)
                ins.then_inc(inverted, 1)

            @block.scalar
            def _(act):
                for step in range(STEPS):
                    t = stage(step, 0)
                    if t is not None:
                        for q in range(2):
                            act.wait_ge(msg_transposed, 2 * t + q + 1)
                            if t >= 2 and q == 0:
                                act.wait_ge(out_done, t - 1)
                            act.activation(msgT[:, t % 2, 4 * q:4 * q + 4], pM[q][:], ACT.Copy
                                           ).then_inc(msg_copied, 1)
                    t = stage(step, 2)
                    if t is not None:
                        act.wait_ge(x_transposed, t + 1)
                        if t >= 2:
                            act.wait_ge(logits, t - 1)
                        act.activation(x2T[:, t % 2], pX[t % 2][:], ACT.Copy).then_inc(x_copied, 1)
                    t = stage(step, 1)
                    if t is not None:
                        act.wait_ge(sqrt_ready, t + 1)
                        if t >= 2:
                            act.wait_ge(xn_made, t - 1)
                        act.activation(rstd[:, t % 2:t % 2 + 1], mv[:, t % 2, 1:2], ACT.Sqrt,
                                       bias=eps[:, 0:1]).then_inc(sqrt_done, 1)
                    if step in UPPER_STEPS:
                        make_upper(0, UPPER_STEPS.index(step))
                act.wait_ge(shifted, 1)
                act.activation(ex[:], ex[:], ACT.Exp).then_inc(exp_done, 1)

            @block.vector
            def _(dve):
                chain = Chain(dve, chain3)
                scale = 1.0 / (2 * MUL) ** 0.5 / NEIGHBORS

                def add_parts(t):
                    a = A[:, t % A_RING]
                    halves = lambda part: part.rearrange("p (h u) -> p h u", h=2)
                    total, last = joined[:, t % A_RING, 0], joined[:, t % A_RING, 1]
                    dve.wait_ge(acc_loaded[t % A_RING], 16 * (t // A_RING + 1))
                    chain.link(dve.tensor_tensor(halves(total), a[:, 1:4:2, 2 * P:],
                                                 halves(a[:, 2, P:2 * P]), ALU.add))
                    dve.tensor_copy(halves(last), a[:, 0:3:2, 2 * P:])
                    dve.tensor_tensor(total, total, a[:, 3, P:2 * P], ALU.add).then_inc(sums_added, 1)

                add_parts(0)
                for step in range(STEPS):
                    t = stage(step, 2)
                    if t is not None:
                        dve.wait_ge(sqrt_done, t + 1)
                        r = rstd[:, t % 2:t % 2 + 1]
                        chain.link(dve.reciprocal(r, r))
                        dve.tensor_scalar(xn2[:, t, :], X[:, t, :], mv[:, t % 2, 0:1], r,
                                          ALU.subtract, ALU.mult).then_inc(xn_made, 1)
                    t = stage(step, -1)
                    if t is not None:
                        add_parts(t)
                    t = stage(step, 1)
                    if t is not None:
                        dve.wait_ge(out_done, t + 1)
                        o = pO[t % 2]
                        xv = X[:, t, MUL:].rearrange("p (u m) -> p m u", m=3)
                        dve.scalar_tensor_tensor(X[:, t, 0:MUL], o[:, 0], scale, X[:, t, 0:MUL],
                                                 ALU.mult, ALU.add)
                        chain.link(dve.scalar_tensor_tensor(xv, o[:, 1:4], scale, xv, ALU.mult, ALU.add))
                        dve.bn_stats(stats[:, t % 2], X[:, t, :]).then_inc(stats_made, 1)
                        if t >= 2:
                            dve.wait_ge(xn_made, t - 1)
                        dve.wait_ge(stats_made, t + 1)
                        dve.bn_aggr(mv[:, t % 2], stats[:, t % 2]).then_inc(sqrt_ready, 1)

                wide = lambda a: a[:, :, None].broadcast_to((P, NODE_TILES, EXPERTS))
                dve.wait_ge(iota_made, 7)
                chain.link(dve.tensor_copy(row_iota[:], row_iota_i[:]))
                chain.link(dve.tensor_copy(tile_iota[:], tile_iota_i[:]))
                chain.link(dve.tensor_copy(node[:], node_i[:]))
                chain.link(dve.tensor_copy(order[:], order_i[:]))
                chain.link(dve.tensor_copy(valid[:], node_i[:]))
                chain.link(dve.tensor_scalar(valid[:], valid[:], float(NODES), None, ALU.is_lt))
                chain.link(dve.tensor_scalar(node_part_i[:], node_i[:], NODE_LOW.bit_length() - 1, None,
                                             ALU.logical_shift_right))
                chain.link(dve.tensor_copy(node_part[:, 0], node_part_i[:]))
                chain.link(dve.scalar_tensor_tensor(node_part[:, 1], node_part[:, 0], -float(NODE_LOW),
                                                    node[:], ALU.mult, ALU.add))
                chain.link(dve.tensor_tensor(
                    node_part[:], node_part[:],
                    valid[:, None, :].broadcast_to((P, 2, NODE_TILES)), ALU.mult))
                chain.link(dve.tensor_copy(thr[:], thr_i[:]))
                chain.link(dve.tensor_copy(blk[:], blk_i[:]))
                for k in range(2):
                    chain.link(dve.memset(run[k][:, 0:PAD], 0.0))
                    chain.link(dve.memset(end[k][:, 0:PAD], 0.0))

                def running_sums(buffers, n):
                    a, b = buffers
                    distance = 1
                    while distance < n:
                        chain.link(dve.tensor_tensor(b[:, PAD:], a[:, PAD:],
                                                     a[:, PAD - distance:PAD + n - distance], ALU.add))
                        a, b, distance = b, a, 2 * distance
                    return a
                dve.wait_ge(logits, NODE_TILES)
                chain.link(dve.tensor_reduce(top[:], pL[:, 0:NODE_TILES], AX.X, ALU.max))
                dve.tensor_tensor(ex[:], pL[:, 0:NODE_TILES], wide(top), ALU.subtract).then_inc(shifted, 1)
                dve.wait_ge(exp_done, 1)
                chain.link(dve.tensor_reduce(esum[:], ex[:], AX.X, ALU.add))
                chain.link(dve.reciprocal(esum[:], esum[:]))
                chain.link(dve.tensor_tensor(ex[:], ex[:], wide(esum), ALU.mult))
                orders = order[:, None, :].broadcast_to((P, NODE_TILES, EXPERTS))
                for q, values in enumerate((ex, left)):
                    chain.link(dve.tensor_reduce(prob[:, :, q], values[:], AX.X, ALU.max))
                    chain.link(dve.tensor_tensor(found[:], values[:],
                                                 prob[:, :, q:q + 1].broadcast_to((P, NODE_TILES, EXPERTS)),
                                                 ALU.is_equal))
                    chain.link(dve.tensor_tensor(found[:], found[:], orders, ALU.mult))
                    chain.link(dve.tensor_reduce(place[:], found[:], AX.X, ALU.max))
                    chain.link(dve.tensor_tensor(mask[:, q], orders, wide(place), ALU.is_equal))
                    if q == 0:
                        chain.link(dve.scalar_tensor_tensor(left[:], mask[:, 0], -2.0, ex[:],
                                                            ALU.mult, ALU.add))
                chain.link(dve.tensor_tensor(mask12[:], mask[:, 0], mask[:, 1], ALU.add))
                dve.tensor_tensor(mask12[:], mask12[:], wide(valid), ALU.mult).then_inc(masks_made, 1)
                dve.wait_ge(ranked, 1)
                chain.link(dve.tensor_copy(run[0][:, PAD:], pR[:, 1]))
                upto = running_sums(run, NODE_TILES)
                chain.link(dve.tensor_tensor(rank[:], pR[:, 0], upto[:, PAD - 1:PAD + NODE_TILES - 1],
                                             ALU.add))
                chain.link(dve.tensor_tensor(
                    over[:], upto[:, PAD + NODE_TILES - 1, :, None].broadcast_to((P, EXPERTS, MAX_BLOCKS)),
                    thr[:, None, :].broadcast_to((P, EXPERTS, MAX_BLOCKS)), ALU.is_gt))
                chain.link(dve.tensor_reduce(end[0][:, PAD:], over[:], AX.X, ALU.add))
                chain.link(dve.tensor_scalar(end[0][:, PAD:PAD + 1], end[0][:, PAD:PAD + 1], 1.0, None,
                                             ALU.max))
                ends = running_sums(end, EXPERTS)
                chain.link(dve.tensor_scalar(base[:], ends[:, PAD - 1:PAD + EXPERTS - 1],
                                             float(BLOCK_SLOTS), None, ALU.mult))
                picks = mask[:]
                both = (P, 2, NODE_TILES, EXPERTS)
                chain.link(dve.tensor_tensor(picked[:], rank[:, None].broadcast_to(both), picks, ALU.mult))
                chain.link(dve.tensor_reduce(place_in[:], picked[:], AX.X, ALU.add))
                chain.link(dve.tensor_tensor(picked[:], base[:, None, None, :].broadcast_to(both), picks,
                                             ALU.mult))
                chain.link(dve.tensor_reduce(slot_f[:], picked[:], AX.X, ALU.add))
                chain.link(dve.tensor_tensor(slot_f[:], slot_f[:], place_in[:], ALU.add))
                many = (P, 2, NODE_TILES, MAX_BLOCKS - 1)
                chain.link(dve.tensor_tensor(full[:], place_in[:, :, :, None].broadcast_to(many),
                                             thr[:, None, None, 1:].broadcast_to(many), ALU.is_ge))
                chain.link(dve.tensor_reduce(passed_blocks[:], full[:], AX.X, ALU.add))
                chain.link(dve.scalar_tensor_tensor(slot_f[:], passed_blocks[:],
                                                    float(BLOCK_SLOTS - BLOCK_ROWS), slot_f[:],
                                                    ALU.mult, ALU.add))
                chain.link(dve.tensor_copy(slot_i[:], slot_f[:]))
                chain.link(dve.tensor_scalar(tile_i[:], slot_i[:], P.bit_length() - 1, None,
                                             ALU.logical_shift_right))
                chain.link(dve.tensor_copy(tile_f[:], tile_i[:]))
                chain.link(dve.scalar_tensor_tensor(row_f[:], tile_f[:], -float(P), slot_f[:],
                                                    ALU.mult, ALU.add))
                wide_tiles = (P, 2, NODE_TILES, SLOT_TILES)
                chain.link(dve.tensor_tensor(tile_hot[:], tile_f[:, :, :, None].broadcast_to(wide_tiles),
                                             tile_iota[:, None, None, :].broadcast_to(wide_tiles),
                                             ALU.is_equal))
                for part in range(2):
                    dve.tensor_tensor(tile_node[:, :, :, part], tile_hot[:],
                                      node_part[:, part, None, :, None].broadcast_to(wide_tiles), ALU.mult
                                      ).then_inc(tiles_made, 1)
                for q in range(2):
                    dve.tensor_tensor(row_hot[:, q],
                                      row_f[:, q, :, None].broadcast_to((P, NODE_TILES, P)),
                                      row_iota[:, None, :].broadcast_to((P, NODE_TILES, P)),
                                      ALU.is_equal).then_inc(rows_made, 1)
                chain.link(dve.tensor_tensor(
                    passed[:], blk[:, :, None].broadcast_to((P, SLOT_BLOCKS, EXPERTS - 1)),
                    ends[:, None, PAD:PAD + EXPERTS - 1].broadcast_to((P, SLOT_BLOCKS, EXPERTS - 1)),
                    ALU.is_ge))
                chain.link(dve.tensor_reduce(expert_f[:], passed[:], AX.X, ALU.add))
                chain.link(dve.tensor_copy(expert_i[:], expert_f[:]))
                chain.link(dve.tensor_scalar(last_block_i[:], ends[:, PAD + EXPERTS - 1:], -1.0, None,
                                             ALU.add))
                dve.wait_ge(inverted, 1)
                chain.link(dve.tensor_copy(lower[:], pN[:, 1]))
                chain.link(dve.scalar_tensor_tensor(lower[:], pN[:, 0], float(NODE_LOW), lower[:],
                                                    ALU.mult, ALU.add))
                chain.link(dve.tensor_copy(slot_node[:], lower[:]))

        with ExitStack() as s:
            xg = sb(s, "xg", [P, ROW_TILES, DIM])
            row_index = sb(s, "row_index", [P, ROW_TILES], i32)
            x_hi = sb(s, "x_hi", [P, KC, BLOCK_ROWS], f32r)
            x_lo = sb(s, "x_lo", [P, KC, BLOCK_ROWS], f32r)
            h_full = sb(s, "h_full", [P, 2, CHUNK, BLOCK_ROWS])
            h_hi = sb(s, "h_hi", [P, 2, CHUNK, ROW_TILES * P], f32r)
            h_lo = sb(s, "h_lo", [P, 2, CHUNK, ROW_TILES * P], f32r)
            none = sb(s, "none", [P, 2, CHUNK, ROW_TILES * P - BLOCK_ROWS])
            yb = sb(s, "yb", [P, ROW_TILES, DIM])
            pX = [ps(s, f"pX4_{t}", [P, KC, P]) for t in range(ROW_TILES)]
            pH = [ps(s, f"pH{u}", [P, BLOCK_ROWS]) for u in range(CHUNK)]
            pY = [ps(s, f"pY{t}", [P, DIM]) for t in range(ROW_TILES)]
            (x_loaded, x_transposed, x_upper, x_ready, hidden, gelu_done, h_upper, h_ready, l2_done,
             y_copied, y_saved, cleared, index_made) = sems(
                s, "xg_loaded", "x_transposed4", "x_upper", "x_ready", "hidden", "gelu_done",
                "h_upper", "h_ready", "l2_done", "y_copied", "y_saved",
                "cleared4", "index_made")
            block = s.enter_context(nc.Block())

            def tile_rows(t):
                return min(P, BLOCK_ROWS - t * P)

            def over_blocks(eng, body):
                last = eng.value_load(last_block_i[0:1, 0:1], min_val=2 * NODES // BLOCK_ROWS,
                                      max_val=SLOT_BLOCKS - 1)
                with eng.Fori(0, last) as b:
                    body(b, True)
                body(last, False)
                return last

            @block.sync
            def _(sp):
                def weights_and_result(b, more):
                    if more:
                        e = sp.value_load(expert_i[0:1, bass.ds(b + 1, 1)], min_val=0,
                                          max_val=EXPERTS - 1)
                        for j in range(CHUNKS):
                            sp.wait_ge(split, b * CHUNKS + (j + 1))
                            sp.nop(nofuse=True)
                            load_chunk(e, j)
                        sp.wait_ge(gelu_done, b * CHUNKS + (CHUNKS + 1))
                        sp.nop(nofuse=True)
                        load_bias1(e)
                    sp.wait_ge(y_copied, b + 2)
                    sp.nop(nofuse=True)
                    sp.dma_start(slots[bass.ds(b * BLOCK_SLOTS, BLOCK_SLOTS), :]
                                 .rearrange("(t p) d -> p t d", p=P), yb[:]).then_inc(y_saved, 16)
                    if more:
                        load_bias2(e)

                sp.wait_ge(x_transposed, 1)
                sp.dma_start(yb[0:1, 0], x_rows[0:1]).then_inc(y_saved, 16)
                last = over_blocks(sp, weights_and_result)
                sp.wait_ge(y_saved, last * 16 + 32)
                sp.nop(nofuse=True)

            @block.gpsimd
            def _(pool):
                def load_rows(b):
                    pool.tensor_copy(row_index[:], slot_node[:, bass.ds(b * ROW_TILES, ROW_TILES)]
                                     ).then_inc(index_made, 1)
                    pool.wait_ge(index_made, b + 1)
                    pool.nop(nofuse=True)
                    for t in range(ROW_TILES):
                        r = tile_rows(t)
                        pool.indirect_dma_start(
                            xg[0:r, t], None, x_rows,
                            bass.IndirectOffsetOnAxis(ap=row_index[0:r, t:t + 1], axis=0)
                        ).then_inc(x_loaded, 16)

                def rows_and_lower_parts(b, more):
                    if not more:
                        return
                    pool.wait_ge(x_transposed, b * ROW_TILES + ROW_TILES)
                    pool.nop(nofuse=True)
                    load_rows(b + 1)
                    for j in range(CHUNKS):
                        make_lower(b + 1, j)

                load_rows(0)
                over_blocks(pool, rows_and_lower_parts)

            @block.tensor
            def _(pe):
                def transpose_rows(b):
                    pe.wait_ge(x_loaded, b * (16 * ROW_TILES) + 16 * ROW_TILES)
                    for t in range(ROW_TILES):
                        for c in range(KC):
                            r = tile_rows(t)
                            ins = pe.transpose(pX[t][:, c, 0:r], xg[0:r, t, c * P:(c + 1) * P],
                                               ident[0:r, 0:r])
                        ins.then_inc(x_transposed, 1)

                def layer1(b, j):
                    pe.wait_ge(split, b * CHUNKS + (j + 1))
                    pe.wait_ge(gelu_done, b * CHUNKS + (j + 1))
                    for u in range(CHUNK):
                        cols = slice(u * P, (u + 1) * P)
                        steps = [(w, v, c) for c in range(KC)
                                 for w, v in ((w1_hi, x_hi), (w1_hi, x_lo), (w1_lo, x_hi))]
                        for i, (w, v, c) in enumerate(steps):
                            ins = pe.matmul(pH[u][:], w[:, j, c, cols], v[:, c],
                                            start=i == 0, stop=i == len(steps) - 1)
                        ins.then_inc(hidden, 1)

                def layer2(b, j):
                    pe.wait_ge(h_ready, b * CHUNKS + (j + 1))
                    for u in range(CHUNK):
                        for t in range(ROW_TILES):
                            rows_t = slice(t * P, (t + 1) * P)
                            for i, (v, w) in enumerate(((h_hi, w2_hi), (h_hi, w2_lo), (h_lo, w2_hi))):
                                ins = pe.matmul(pY[t][:], v[:, j % 2, u, rows_t], w[:, j, u],
                                                start=j == 0 and u == 0 and i == 0,
                                                stop=j == CHUNKS - 1 and u == CHUNK - 1 and i == 2)
                    ins.then_inc(l2_done, 1)

                def compute(b, more):
                    pe.wait_ge(x_ready, b * ROW_TILES + ROW_TILES)
                    layer1(b, 0)
                    for j in range(1, CHUNKS):
                        layer1(b, j)
                        if j == 1:
                            pe.wait_ge(y_copied, b + 1)
                        if j == CHUNKS - 1 and more:
                            transpose_rows(b + 1)
                        layer2(b, j - 1)
                    layer2(b, CHUNKS - 1)

                transpose_rows(0)
                over_blocks(pe, compute)

            @block.scalar
            def _(act):
                act.sem_inc(gelu_done, 1)

                def upper_rows(b):
                    for t in range(ROW_TILES):
                        act.wait_ge(x_transposed, b * ROW_TILES + (t + 1))
                        r = tile_rows(t)
                        act.activation(x_hi[:, :, t * P:t * P + r], pX[t][:, :, 0:r], ACT.Copy
                                       ).then_inc(x_upper, 1)

                def gelu(b, j):
                    for u in range(CHUNK):
                        hc = CHUNK * j + u
                        act.wait_ge(hidden, b * HC + (hc + 1))
                        ins = act.activation(h_full[:, j % 2, u], pH[u][:], ACT.Gelu_apprx_tanh,
                                             bias=b1[:, hc:hc + 1])
                    ins.then_inc(gelu_done, 1)

                def next_upper(b, j):
                    act.wait_ge(l2_done, b * CHUNKS + (j + 1))
                    make_upper(b + 1, j)

                def activations(b, more):
                    act.wait_ge(b1_loaded, b * 16 + 16)
                    for j in range(CHUNKS):
                        gelu(b, j)
                        if j == CHUNKS - 1 and more:
                            upper_rows(b + 1)
                        if j >= 2 and more:
                            next_upper(b, j - 2)
                    if more:
                        next_upper(b, CHUNKS - 2)
                        next_upper(b, CHUNKS - 1)

                upper_rows(0)
                over_blocks(act, activations)

            @block.vector
            def _(dve):
                dve.sem_inc(y_copied, 1)
                dve.memset(none[:], 0.0).then_inc(cleared, 1)
                dve.wait_ge(cleared, 1)
                for part in (h_hi, h_lo):
                    dve.tensor_copy(part[:, :, :, BLOCK_ROWS:], none[:]).then_inc(cleared, 1)

                def lower_rows(b):
                    for t in range(ROW_TILES):
                        r = tile_rows(t)
                        part = slice(t * P, t * P + r)
                        dve.wait_ge(x_upper, b * ROW_TILES + (t + 1))
                        dve.tensor_tensor(x_lo[:, :, part], pX[t][:, :, 0:r], x_hi[:, :, part].bitcast(fp32),
                                          ALU.subtract).then_inc(x_ready, 1)

                def parts_and_result(b, more):
                    for j in range(CHUNKS):
                        dve.wait_ge(gelu_done, b * CHUNKS + (j + 2))
                        hi = h_hi[:, j % 2, :, 0:BLOCK_ROWS]
                        lo = h_lo[:, j % 2, :, 0:BLOCK_ROWS]
                        dve.tensor_copy(hi, h_full[:, j % 2]).then_inc(h_upper, 1)
                        dve.wait_ge(h_upper, b * CHUNKS + (j + 1))
                        dve.tensor_tensor(lo, h_full[:, j % 2], hi.bitcast(fp32), ALU.subtract
                                          ).then_inc(h_ready, 1)
                    if more:
                        lower_rows(b + 1)
                    dve.wait_ge(l2_done, b * CHUNKS + CHUNKS)
                    dve.wait_ge(y_saved, b * 16 + 16)
                    dve.wait_ge(b2_loaded, b * 16 + 16)
                    for t in range(ROW_TILES):
                        ins = dve.tensor_tensor(yb[:, t], pY[t][:], b2[:], ALU.add)
                    ins.then_inc(y_copied, 1)

                lower_rows(0)
                over_blocks(dve, parts_and_result)

        expert_stack.close()

        with ExitStack() as s:
            Y = sb(s, "Y", [P, NODE_TILES, 2, DIM])
            (chain5, combined, saved) = sems(s, "chain5", "combined", "saved")
            fetched = sems(s, *[f"fetched{k}" for k in range(NODE_TILES)])
            block = s.enter_context(nc.Block())

            @block.gpsimd
            def _(pool):
                for t in range(NODE_TILES):
                    for q in range(2):
                        pool.indirect_dma_start(
                            Y[0:rows(t), t, q, :], None, slots,
                            bass.IndirectOffsetOnAxis(ap=slot_i[0:rows(t), q, t:t + 1], axis=0)
                        ).then_inc(fetched[t], 16)

            @block.vector
            def _(dve):
                chain = Chain(dve, chain5)
                for t in range(NODE_TILES):
                    r = rows(t)
                    y = Y[0:r, t]
                    dve.wait_ge(fetched[t], 32)
                    chain.link(dve.scalar_tensor_tensor(X[0:r, t, :], y[:, 0], prob[0:r, t, 0:1],
                                                        X[0:r, t, :], ALU.mult, ALU.add))
                    dve.scalar_tensor_tensor(X[0:r, t, :], y[:, 1], prob[0:r, t, 1:2],
                                             X[0:r, t, :], ALU.mult, ALU.add).then_inc(combined, 1)

            @block.sync
            def _(sp):
                for t in range(NODE_TILES):
                    sp.wait_ge(combined, t + 1)
                    sp.dma_start(out[t * P:t * P + rows(t), :], X[0:rows(t), t, :]).then_inc(saved, 16)
                sp.wait_ge(saved, 16 * NODE_TILES)


def kernel(x, src, dst, edge_attr_4, edge_attr_8, L0_gnn_W_up0, L0_gnn_W_up1, L0_gnn_W_mlp1,
           L0_gnn_W_mlp2, L0_gnn_W_mlp3, L0_gnn_W_mlp4, L0_gnn_W_out0, L0_gnn_W_out1, L0_ffn_Wg,
           L0_ffn_W1, L0_ffn_b1, L0_ffn_W2, L0_ffn_b2):
    import numpy as np
    import concourse.bacc as bacc
    from concourse.bass_utils import run_bass_kernel_spmd

    pad = TILES * P - EDGES

    def tiles(a, mode="constant"):
        a = np.asarray(a)
        a = np.pad(a, [(0, pad)] + [(0, 0)] * (a.ndim - 1), mode=mode)
        return np.ascontiguousarray(a.reshape((TILES, P) + a.shape[1:]).swapaxes(0, 1))

    src_t = tiles(src)
    src_t = np.ascontiguousarray(np.concatenate([src_t, src_t[:, :2 * ITER_TILES]], axis=1))
    basis = np.pad(np.asarray(edge_attr_8), [(0, pad), (0, 0)])
    basis = basis.reshape(ITERS, 2, HALF, BASIS).swapaxes(2, 3).reshape(ITERS, 2 * BASIS, HALF)
    basis = np.ascontiguousarray(np.concatenate([basis, basis[:3]], axis=0))
    b1 = np.ascontiguousarray(np.asarray(L0_ffn_b1).reshape(EXPERTS, HC, P).swapaxes(1, 2))

    arrays = {
        "x": np.ascontiguousarray(x), "src": src_t, "dst": tiles(dst, "edge"),
        "edge_y": tiles(edge_attr_4).reshape(P, TILES * 4), "edge_f": basis,
        "w_up0": np.ascontiguousarray(L0_gnn_W_up0), "w_up1": np.ascontiguousarray(L0_gnn_W_up1),
        "w_mlp1": np.ascontiguousarray(L0_gnn_W_mlp1), "w_mlp2": np.ascontiguousarray(L0_gnn_W_mlp2),
        "w_mlp3": np.ascontiguousarray(L0_gnn_W_mlp3), "w_mlp4": np.ascontiguousarray(L0_gnn_W_mlp4),
        "w_out0": np.ascontiguousarray(L0_gnn_W_out0), "w_out1": np.ascontiguousarray(L0_gnn_W_out1),
        "w_g": np.ascontiguousarray(L0_ffn_Wg), "w_1": np.ascontiguousarray(L0_ffn_W1), "b_1": b1,
        "w_2": np.ascontiguousarray(L0_ffn_W2), "b_2": np.ascontiguousarray(L0_ffn_b2),
    }
    nc = bacc.Bacc("TRN2", target_bir_lowering=False, num_devices=1)
    args = [nc.dram_tensor(n, a.shape, mybir.dt.from_np(a.dtype), kind="ExternalInput").ap()
            for n, a in arrays.items()]
    result = nc.dram_tensor("result", (NODES, DIM), mybir.dt.float32, kind="ExternalOutput").ap()
    program(nc, *args, result)
    r = run_bass_kernel_spmd(nc, [arrays], core_ids=[0])
    return r.results[0]["result"]
```
